# Optimizing a Trainium2 kernel written in Bass

```python
import numpy as np
import jax
import jax.numpy as jnp

def _softmax(x, axis=-1):
    return jax.nn.softmax(x, axis=axis)

def _gelu(x):
    return jax.nn.gelu(x, approximate=True)

def _silu(x):
    return jax.nn.silu(x)

def _sigmoid(x):
    return jax.nn.sigmoid(x)

def _layernorm(x, axis=-1, eps=1e-05):
    m = jnp.mean(x, axis=axis, keepdims=True)
    v = jnp.var(x, axis=axis, keepdims=True)
    return (x - m) / jnp.sqrt(v + eps)

def _scatter_add(tgt, idx, src, axis=0):
    return tgt.at[idx].add(src)

def _segment_sum(src, seg, n):
    return jax.ops.segment_sum(src, seg, n)
kernel_name = 'mk_gnn_resnorm_d2_gnn_r8_96c75d'

def setup_inputs(seed: int=0):
    np.random.seed(seed)
    _w = jnp.asarray

    def _rec_inputs():
        import jax
        import jax.numpy as jnp
        _gk = jax.random.key(seed)
        x = -0.0005121 + 1.001 * jax.random.normal(jax.random.fold_in(_gk, 1), (12500, 64), jnp.float32)
        _s = jax.random.randint(jax.random.fold_in(_gk, 2), (200000,), 0, 12500, jnp.int32)
        _d = jax.random.randint(jax.random.fold_in(_gk, 3), (200000,), 0, 12500, jnp.int32)
        _loop = jnp.arange(12500, dtype=jnp.int32)
        src = jnp.concatenate([_s, _d, _loop])
        dst = jnp.concatenate([_d, _s, _loop])
        _o = jnp.argsort(dst, stable=True)
        src = src[_o]
        dst = dst[_o]
        edge_attr_2 = 0.000452788 + 0.999756 * jax.random.normal(jax.random.fold_in(_gk, 11), (412500, 2), jnp.float32)
        edge_attr_64 = -9.77346e-05 + 0.999888 * jax.random.normal(jax.random.fold_in(_gk, 12), (412500, 64), jnp.float32)
        return (x, src, dst, edge_attr_2, edge_attr_64)
    x, src, dst, edge_attr_2, edge_attr_64 = _rec_inputs()

    def _L0_gnn_setup():
        import jax, jax.numpy as jnp
        import numpy as np
        NUM_LAYERS = 3

        def _lightgcn_layer(x, src, dst, num_nodes):
            msgs = x[src]
            summed = jax.ops.segment_sum(msgs, dst, num_segments=num_nodes)
            counts = jax.ops.segment_sum(jnp.ones((src.shape[0],), x.dtype), dst, num_segments=num_nodes)
            denom = jnp.maximum(counts, 1.0)
            return summed / denom[:, None]
        key = jax.random.key(seed)
        k1, k2, k3 = jax.random.split(key, 3)
        N, D, E = (6250, 64, 100000)
        x = jax.random.normal(k1, (N, D), dtype=jnp.float32)
        src = jax.random.randint(k2, (E,), 0, N)
        dst = jax.random.randint(k3, (E,), 0, N)
        edge_index = jnp.stack([src, dst], axis=0).astype(jnp.int64)
        return {'x': x, 'edge_index': edge_index}
    _L0_gnn_all = _L0_gnn_setup()
    _L0_gnn_in = {k: v for k, v in _L0_gnn_all.items() if k in ()}
    del _L0_gnn_all

    def _L1_gnn_setup():
        import jax, jax.numpy as jnp
        import numpy as np
        N = 6250
        E = 100000
        C = 64
        SPACEDIM = 2
        LN_EPS = 1e-05

        def _mlp(x, Wh, bh, Wo, bo, ln_w, ln_b):
            for i in range(Wh.shape[0]):
                x = jax.nn.relu(x @ Wh[i] + bh[i])
            x = x @ Wo + bo
            mu = jnp.mean(x, axis=-1, keepdims=True)
            var = jnp.var(x, axis=-1, keepdims=True)
            return (x - mu) * jax.lax.rsqrt(var + LN_EPS) * ln_w + ln_b
        key = jax.random.key(seed)
        ks = jax.random.split(key, 16)
        s = 1.0 / np.sqrt(C)
        inp = {'x': jax.random.normal(ks[0], (N, C), jnp.float32), 'e': jax.random.normal(ks[1], (E, C), jnp.float32), 'nvec': jax.random.normal(ks[2], (E, SPACEDIM), jnp.float32), 'edge_index': jax.random.randint(ks[3], (2, E), 0, N, jnp.int64), 'flux_Wh': jax.random.normal(ks[4], (3, C, C), jnp.float32) * s, 'flux_bh': jax.random.normal(ks[5], (3, C), jnp.float32) * s, 'flux_Wo': jax.random.normal(ks[6], (C, C * SPACEDIM), jnp.float32) * s, 'flux_bo': jax.random.normal(ks[7], (C * SPACEDIM,), jnp.float32) * s, 'flux_ln_w': jnp.ones((C * SPACEDIM,), jnp.float32), 'flux_ln_b': jnp.zeros((C * SPACEDIM,), jnp.float32), 'a_Wh': jax.random.normal(ks[8], (3, C, C), jnp.float32) * s, 'a_bh': jax.random.normal(ks[9], (3, C), jnp.float32) * s, 'a_Wo': jax.random.normal(ks[10], (C, C), jnp.float32) * s, 'a_bo': jax.random.normal(ks[11], (C,), jnp.float32) * s, 'a_ln_w': jnp.ones((C,), jnp.float32), 'a_ln_b': jnp.zeros((C,), jnp.float32)}
        return inp
    _L1_gnn_all = _L1_gnn_setup()
    _L1_gnn_in = {k: v for k, v in _L1_gnn_all.items() if k in ('flux_Wh', 'flux_bh', 'flux_Wo', 'flux_bo', 'flux_ln_w', 'flux_ln_b', 'a_Wh', 'a_bh', 'a_Wo', 'a_bo', 'a_ln_w', 'a_ln_b')}
    del _L1_gnn_all
    return {'x': x, 'src': src, 'dst': dst, 'edge_attr_2': edge_attr_2, 'edge_attr_64': edge_attr_64, 'L1_gnn_flux_Wh': _L1_gnn_in['flux_Wh'], 'L1_gnn_flux_bh': _L1_gnn_in['flux_bh'], 'L1_gnn_flux_Wo': _L1_gnn_in['flux_Wo'], 'L1_gnn_flux_bo': _L1_gnn_in['flux_bo'], 'L1_gnn_flux_ln_w': _L1_gnn_in['flux_ln_w'], 'L1_gnn_flux_ln_b': _L1_gnn_in['flux_ln_b'], 'L1_gnn_a_Wh': _L1_gnn_in['a_Wh'], 'L1_gnn_a_bh': _L1_gnn_in['a_bh'], 'L1_gnn_a_Wo': _L1_gnn_in['a_Wo'], 'L1_gnn_a_bo': _L1_gnn_in['a_bo'], 'L1_gnn_a_ln_w': _L1_gnn_in['a_ln_w'], 'L1_gnn_a_ln_b': _L1_gnn_in['a_ln_b']}

def reference(x, src, dst, edge_attr_2, edge_attr_64, L1_gnn_flux_Wh, L1_gnn_flux_bh, L1_gnn_flux_Wo, L1_gnn_flux_bo, L1_gnn_flux_ln_w, L1_gnn_flux_ln_b, L1_gnn_a_Wh, L1_gnn_a_bh, L1_gnn_a_Wo, L1_gnn_a_bo, L1_gnn_a_ln_w, L1_gnn_a_ln_b):
    import jax
    import jax.numpy as jnp

    def _L0_gnn_ref(x, edge_index):
        import jax, jax.numpy as jnp
        import numpy as np
        NUM_LAYERS = 3

        def _lightgcn_layer(x, src, dst, num_nodes):
            msgs = x[src]
            summed = jax.ops.segment_sum(msgs, dst, num_segments=num_nodes)
            counts = jax.ops.segment_sum(jnp.ones((src.shape[0],), x.dtype), dst, num_segments=num_nodes)
            denom = jnp.maximum(counts, 1.0)
            return summed / denom[:, None]
        src = edge_index[0]
        dst = edge_index[1]
        n = x.shape[0]
        for _ in range(NUM_LAYERS):
            x = _lightgcn_layer(x, src, dst, n)
        return x

    def _L1_gnn_ref(x, e, nvec, edge_index, flux_Wh, flux_bh, flux_Wo, flux_bo, flux_ln_w, flux_ln_b, a_Wh, a_bh, a_Wo, a_bo, a_ln_w, a_ln_b):
        import jax, jax.numpy as jnp
        import numpy as np
        N = 6250
        E = 100000
        C = 64
        SPACEDIM = 2
        LN_EPS = 1e-05

        def _mlp(x, Wh, bh, Wo, bo, ln_w, ln_b):
            for i in range(Wh.shape[0]):
                x = jax.nn.relu(x @ Wh[i] + bh[i])
            x = x @ Wo + bo
            mu = jnp.mean(x, axis=-1, keepdims=True)
            var = jnp.var(x, axis=-1, keepdims=True)
            return (x - mu) * jax.lax.rsqrt(var + LN_EPS) * ln_w + ln_b
        src = edge_index[0]
        dst = edge_index[1]
        x_send = x[src]
        x_recv = x[dst]
        n_e = x_send.shape[0]
        c = x.shape[1]
        fs = _mlp(x_send, flux_Wh, flux_bh, flux_Wo, flux_bo, flux_ln_w, flux_ln_b)
        fr = _mlp(x_recv, flux_Wh, flux_bh, flux_Wo, flux_bo, flux_ln_w, flux_ln_b)
        flux_send = jnp.einsum('ecd,ed->ec', fs.reshape(n_e, c, SPACEDIM), nvec)
        flux_recv = jnp.einsum('ecd,ed->ec', fr.reshape(n_e, c, SPACEDIM), nvec)
        a_ws = _mlp((x_send + x_recv) * 0.5, a_Wh, a_bh, a_Wo, a_bo, a_ln_w, a_ln_b)
        flux = 0.5 * (flux_send + flux_recv) - 0.5 * a_ws * (x_send - x_recv)
        agg = jax.ops.segment_sum(flux, dst, num_segments=x.shape[0])
        return x + agg
    edge_index = jnp.stack([src, dst])
    x = _layernorm(x + _L0_gnn_ref(x, edge_index), axis=-1)
    x = _layernorm(x + _L1_gnn_ref(x, edge_attr_64, edge_attr_2, edge_index, L1_gnn_flux_Wh, L1_gnn_flux_bh, L1_gnn_flux_Wo, L1_gnn_flux_bo, L1_gnn_flux_ln_w, L1_gnn_flux_ln_b, L1_gnn_a_Wh, L1_gnn_a_bh, L1_gnn_a_Wo, L1_gnn_a_bo, L1_gnn_a_ln_w, L1_gnn_a_ln_b), axis=-1)
    return x

_drawn_inputs = setup_inputs


def setup_inputs(seed=0):
    import zlib

    import numpy as np

    out = dict(_drawn_inputs(seed))
    spreads = {'L1_gnn_flux_ln_w': (1.0, 0.2),
     'L1_gnn_flux_ln_b': (0.0, 0.1),
     'L1_gnn_a_ln_w': (1.0, 0.2),
     'L1_gnn_a_ln_b': (0.0, 0.1)}
    factors = {}
    for name, (base, spread) in spreads.items():
        noise = np.random.default_rng([zlib.crc32(name.encode()), seed]).standard_normal(out[name].shape)
        drawn = base * np.exp(spread * noise) if base else spread * noise
        out[name] = jnp.asarray(drawn.astype(out[name].dtype))
    for name, factor in factors.items():
        out[name] = (out[name] * factor).astype(out[name].dtype)
    return out
```

```python
from contextlib import ExitStack, contextmanager

import concourse.bass as bass
import concourse.mybir as mybir

F32 = mybir.dt.float32
BF16 = mybir.dt.bfloat16
I32 = mybir.dt.int32
ALU = mybir.AluOpType
ACT = mybir.ActivationFunctionType
AX = mybir.AxisListType.X

P = 128
N = 12500
E = 412500
C = 64
K = 16
NB = 4
CH = -(-E // (P * K))
T = CH * K
EP = P * T
J = -(-N // P)
NP = P * J
PEEL = NB + (CH - NB) % NB
E_LAST = E - (P - 1) * T
N_LAST = N - (P - 1) * J
W4 = 2 * C + 2
ROW = 5 * C
JG = 14
NG = J // JG
GP = 8
PADP = max(p for p in range(1, P + 1) if 2 * (EP - E) % p == 0)
EPS = 1e-5
PAD_DST = 128 * P - 1
assert J % JG == 0 and CH > NB and PEEL % NB == CH % NB


class Chunk:

    def __init__(self, r, place):
        self.c = r * NB + place
        self.b4, self.b2 = place % NB, place % 2
        self.turn4 = r + place // NB
        self.turn2 = r * (NB // 2) + place // 2
        self.r, self.place = r, place

    def before(self):
        return Chunk(self.r, self.place - 1)


def chunks(eng, body):
    for c in range(PEEL):
        body(Chunk(0, c))
    with eng.Fori(0, (CH - PEEL) // NB) as r:
        for j in range(NB):
            body(Chunk(r, PEEL + j))


def early(h, n):
    return isinstance(h.c, int) and h.c < n


@contextmanager
def semaphores(nc):
    held = []

    def sem(name):
        held.append(nc.alloc_semaphore(name))
        return held[-1]
    yield sem
    nc.clear_and_free_semaphores(held)
    nc.all_engine_barrier()


class Chain:

    def __init__(self, eng, sem):
        self.eng, self.sem, self.base, self.n = eng, sem, 0, 0

    def link(self, ins):
        self.n += 1
        ins.then_inc(self.sem, 1)
        self.eng.wait_ge(self.sem, self.base + self.n)

    def at(self, base):
        self.base, self.n = base, 0


def build_program(nc, x, src, dst, nvec, fWh, fbh, fWo, fbo, flw, flb, aWh, abh, aWo, abo, alw, alb, out):
    scratch = lambda name, shape: nc.dram_tensor(name, shape, F32).ap()
    X = scratch("x_layer", (NP, C))
    X1 = scratch("x_mid", (NP, C))
    S = scratch("running", (EP, C))
    S4 = scratch("running_flux", (EP, W4))
    B = scratch("first_rows", (EP + NP, C))
    T4 = scratch("table", (NP, ROW))
    NV = scratch("nvec_padded", (EP, 2))
    CNT = scratch("counts_dram", (P * P,))
    END = scratch("ends_dram", (P * P,))
    per_part = lambda t: t.rearrange("(p t) c -> p (t c)", p=P)

    top = ExitStack()
    with top:
        sb = lambda name, shape, dt=F32: top.enter_context(nc.sbuf_tensor(name, shape, dt))
        src_sb = sb("src_sb", [P, T], I32)
        keep = sb("keep", [P, T])
        ident = sb("ident", [P, P])
        eps_col = sb("eps_col", [P, 1])
        end_idx = sb("end_idx", [P, J], I32)
        start_idx = sb("start_idx", [P, J], I32)
        has = sb("has", [P, J])
        cnt = sb("cnt", [P, J])
        rcnt = sb("rcnt", [P, J])
        first_dst = sb("first_dst", [P, 1], I32)
        lead_idx = sb("lead_idx", [P, 1], I32)
        goes_on = sb("goes_on", [P, P])
        passes = sb("passes", [P, P])
        ends_here = sb("ends_here", [P, P])
        run_end = sb("run_end", [P, W4])
        carried = sb("carried", [P, W4])

        with ExitStack() as ctx:
            sb = lambda name, shape, dt=F32: ctx.enter_context(nc.sbuf_tensor(name, shape, dt))
            dst_sb = sb("dst_sb", [P, T], I32)
            dst_f = sb("dst_f", [P, T])
            a_f = sb("a_f", [P, T])
            b_f = sb("b_f", [P, T])
            a_i = sb("a_i", [P, T], I32)
            b_i = sb("b_i", [P, T], I32)
            iota_row = sb("iota_row", [P, P])
            row_id = sb("row_id", [P, 1])
            node_id = sb("node_id", [P, J])
            part_row = sb("part_row", [P, 1])
            lead = sb("lead", [P, 1])
            ends = sb("ends", [P, 2 * P])
            ones = sb("ones", [P, P])
            first_row = sb("first_row", [P, 2 * P])
            one_part = sb("one_part", [P, P])
            same = sb("same", [P, T])
            zeros = sb("zeros", [P, K * C])
            oh_a = sb("oh_a", [P, 2, K, P], BF16)
            oh_b = sb("oh_b", [P, 2, K, P], BF16)
            zero_bf = sb("zero_bf", [P, P], BF16)
            rows = sb("rows", [P, NB, K, C])
            idx = sb("idx", [P, NB, K], I32)
            kc = sb("kc", [P, 2, K])
            carry = sb("carry", [P, C])
            cnt_ab = sb("cnt_ab", [P, P])
            end_ab = sb("end_ab", [P, P])
            before = sb("before", [P, P])
            hist = ctx.enter_context(nc.psum_tensor("hist", [P, P], F32))
            rows_ps = ctx.enter_context(nc.psum_tensor("rows_ps", [P, 2 * P], F32))
            pre_ps = ctx.enter_context(nc.psum_tensor("pre_ps", [P, 1], F32))
            with semaphores(nc) as sem:
                cleared = sem("cleared")
                loaded = sem("loaded")
                src_loaded = sem("src_loaded")
                consts = sem("consts")
                order = sem("order")
                pool_order = sem("pool_order")
                diag_ready = sem("diag_ready")
                rows_seen = sem("rows_seen")
                nv_zero = sem("nv_zero")
                with nc.Block() as block:
                    @block.sync
                    def _(sp):
                        sp.wait_ge(cleared, 3)
                        sp.dma_start(dst_sb[0:P - 1, :], dst[0:(P - 1) * T].rearrange("(p t) -> p t", p=P - 1)).then_inc(loaded, 16)
                        sp.dma_start(dst_sb[P - 1:P, 0:E_LAST], dst[(P - 1) * T:E].rearrange("(p t) -> p t", p=1)).then_inc(loaded, 16)
                        sp.dma_start(src_sb[0:P - 1, :], src[0:(P - 1) * T].rearrange("(p t) -> p t", p=P - 1)).then_inc(src_loaded, 16)
                        sp.dma_start(src_sb[P - 1:P, 0:E_LAST], src[(P - 1) * T:E].rearrange("(p t) -> p t", p=1)).then_inc(src_loaded, 16)
                        sp.dma_start(NV[0:E, :], nvec[:, :]).then_inc(nv_zero, 16)
                        sp.dma_start(NV[E:EP, :].rearrange("t c -> (t c)").rearrange("(p t) -> p t", p=PADP),
                                     zeros[0:PADP, 0:2 * (EP - E) // PADP]).then_inc(nv_zero, 16)
                        sp.wait_ge(loaded, 32)
                        sp.wait_ge(src_loaded, 32)
                        sp.wait_ge(nv_zero, 32)

                    @block.gpsimd
                    def _(pool):
                        order_ = Chain(pool, pool_order)
                        order_.link(pool.memset(ident[:, :], 0.0))
                        order_.link(pool.memset(before[:, :], 1.0))
                        pool.memset(ones[:, :], 1.0).then_inc(consts, 1)
                        pool.affine_select(out=ident[:, :], in_=ident[:, :], compare_op=ALU.not_equal, fill=1.0,
                                           base=0, pattern=[[-1, P]], channel_multiplier=1).then_inc(consts, 1)
                        pool.affine_select(out=before[:, :], in_=before[:, :], compare_op=ALU.is_ge, fill=0.0,
                                           base=-1, pattern=[[1, P]], channel_multiplier=-1).then_inc(consts, 1)
                        pool.iota(iota_row[:, :], pattern=[[1, P]], base=0, channel_multiplier=0,
                                  allow_small_or_imprecise_dtypes=True).then_inc(consts, 1)
                        pool.iota(part_row[:, :], pattern=[[1, 1]], base=0, channel_multiplier=T,
                                  allow_small_or_imprecise_dtypes=True).then_inc(consts, 1)
                        pool.iota(node_id[:, :], pattern=[[1, J]], base=0, channel_multiplier=J,
                                  allow_small_or_imprecise_dtypes=True).then_inc(consts, 1)

                    @block.tensor
                    def _(pe):
                        pe.wait_ge(consts, 6)
                        pe.wait_ge(diag_ready, 2)
                        pe.matmul(rows_ps[:, :], ones[:, :], ends[:, :], start=True, stop=True).then_inc(rows_seen, 1)

                    @block.vector
                    def _(dve):
                        o = Chain(dve, order)
                        dve.memset(src_sb[96:P, E_LAST:T], 0).then_inc(cleared, 1)
                        dve.memset(dst_sb[96:P, E_LAST:T], PAD_DST).then_inc(cleared, 1)
                        dve.memset(zeros[:, :], 0.0).then_inc(cleared, 1)
                        dve.memset(zero_bf[:, :], 0.0)
                        dve.memset(eps_col[:, :], EPS)
                        dve.memset(keep[:, 0:1], 0.0)
                        dve.memset(carry[:, :], 0.0)
                        dve.memset(goes_on[:, 0:1], 0.0)
                        dve.memset(passes[:, 0:1], 0.0)
                        dve.memset(ends_here[:, P - 1:P], 1.0)
                        dve.wait_ge(loaded, 32)
                        o.link(dve.tensor_copy(dst_f[:, :], dst_sb[:, :]))
                        dve.tensor_tensor(keep[:, 1:T], dst_f[:, 1:T], dst_f[:, 0:T - 1], ALU.is_equal)
                        o.link(dve.tensor_single_scalar(a_i[:, :], dst_sb[:, :], 7, ALU.logical_shift_right))
                        o.link(dve.tensor_single_scalar(b_i[:, :], dst_sb[:, :], P - 1, ALU.bitwise_and))
                        dve.tensor_copy(a_f[:, :], a_i[:, :])
                        dve.tensor_copy(b_f[:, :], b_i[:, :])
                        dve.tensor_copy(first_dst[:, :], dst_sb[:, 0:1])
                        o.link(dve.tensor_scalar(same[:, :], dst_f[:, :], dst_f[:, 0:1], None, ALU.is_equal))
                        o.link(dve.tensor_reduce(lead[:, :], same[:, :], AX, ALU.add))
                        dve.wait_ge(consts, 6)
                        o.link(dve.tensor_scalar(lead[:, :], lead[:, :], part_row[:, 0:1], -1.0, ALU.add, ALU.add))
                        dve.tensor_copy(lead_idx[:, :], lead[:, :])
                        dve.tensor_scalar(ends[:, 0:P], ident[:, :], dst_f[:, 0:1], None, ALU.mult).then_inc(diag_ready, 1)
                        dve.tensor_scalar(ends[:, P:2 * P], ident[:, :], dst_f[:, T - 1:T], None, ALU.mult).then_inc(diag_ready, 1)
                        dve.wait_ge(rows_seen, 1)
                        o.link(dve.tensor_copy(first_row[:, :], rows_ps[:, :]))
                        fr, lr = first_row[:, 0:P], first_row[:, P:2 * P]
                        o.link(dve.tensor_tensor(one_part[:, :], fr, lr, ALU.is_equal))
                        o.link(dve.tensor_tensor(goes_on[:, 1:P], fr[:, 1:P], lr[:, 0:P - 1], ALU.is_equal))
                        o.link(dve.tensor_tensor(passes[:, 1:P], goes_on[:, 1:P], one_part[:, 0:P - 1], ALU.mult))
                        o.link(dve.tensor_scalar(ends_here[:, 0:P - 1], passes[:, 1:P], -1.0, 1.0, ALU.mult, ALU.add))

            with semaphores(nc) as sem:
                gcn_pass(nc, sem, "l1", x, src_sb, keep, rows, idx, kc, carry, S, run_end,
                         hist_parts=(a_f, b_f, iota_row, oh_a, oh_b, zero_bf, hist, zeros, B))
            counts(nc, hist, before, pre_ps, cnt_ab, end_ab, CNT, END, cnt, has, rcnt, node_id,
                   end_idx, start_idx)
            node_sums(nc, "n1", S, X, run_end, carried, ident, goes_on, passes, ends_here, lead_idx,
                      end_idx, rcnt)
        for layer in (2, 3):
            with ExitStack() as ctx:
                sb = lambda name, shape, dt=F32: ctx.enter_context(nc.sbuf_tensor(f"{name}{layer}", shape, dt))
                rows = sb("rows", [P, NB, K, C])
                idx = sb("idx", [P, NB, K], I32)
                kc = sb("kc", [P, 2, K])
                carry = sb("carry", [P, C])
                with semaphores(nc) as sem:
                    gcn_pass(nc, sem, f"l{layer}", X, src_sb, keep, rows, idx, kc, carry, S, run_end)
                node_sums(nc, f"n{layer}", S, X, run_end, carried, ident, goes_on, passes, ends_here,
                          lead_idx, end_idx, rcnt)
        node_mlps(nc, x, X, X1, T4, B, start_idx, eps_col, ident, fWh, fbh, fWo, fbo, flw, flb,
                  aWh, alw, alb)
        flux_pass(nc, T4, B, NV, S4, src_sb, keep, first_dst, run_end, ident, eps_col,
                  aWh, abh, aWo, abo)
        final(nc, S4, T4, X1, out, run_end, carried, ident, goes_on, passes, ends_here, lead_idx,
              end_idx, has, cnt, eps_col, alw, alb)


def gcn_pass(nc, sem_, tag, table, src_sb, keep, rows, idx, kc, carry, S, run_end, hist_parts=None):
    sem = lambda name: sem_(f"{tag}_{name}")
    idx_ready = [sem(f"idx_ready{b}") for b in range(NB)]
    gathered = [sem(f"gathered{b}") for b in range(NB)]
    stored = [sem(f"stored{b}") for b in range(NB)]
    issued = sem("issued")
    order = sem("order")
    summed = sem("summed")
    carry_zero = sem("carry_zero")
    oh_ready, oh_used, zeroed, counted = sem("oh_ready"), sem("oh_used"), sem("zeroed"), sem("counted")
    Sv = S.rearrange("(p t) c -> p (t c)", p=P)

    with nc.Block() as block:
        @block.sync
        def _(sp):
            def store(c, b):
                sp.wait_ge(summed, c + 1)
                sp.dma_start(Sv[:, bass.ds(c * (K * C), K * C)],
                             rows[:, b, :, :].rearrange("p k c -> p (k c)")).then_inc(stored[b], 16)

            def step(h):
                if not (early(h, NB)):
                    sp.wait_ge(summed, h.c - (NB - 1))
                sp.dma_start(idx[:, h.b4, :], src_sb[:, bass.ds(h.c * K, K)]).then_inc(idx_ready[h.b4], 16)
                if not (early(h, 3)):
                    store(h.c - 3, (h.b4 + 1) % NB)
            chunks(sp, step)
            for c in range(CH - 3, CH):
                store(c, c % NB)
            for b in range(NB):
                sp.wait_ge(stored[b], 16 * len(range(b, CH, NB)))

        @block.gpsimd
        def _(pool):
            def step(h):
                pool.wait_ge(idx_ready[h.b4], 16 * (h.turn4 + 1))
                if not (early(h, NB)):
                    pool.wait_ge(stored[h.b4], 16 * h.turn4)
                pool.sem_inc(issued, 1)
                for k in range(K):
                    pool.indirect_dma_start(rows[:, h.b4, k, :], None, table,
                                            bass.IndirectOffsetOnAxis(ap=idx[:, h.b4, k:k + 1], axis=0))\
                        .then_inc(gathered[h.b4], 16)
            chunks(pool, step)

        @block.vector
        def _(dve):
            o = Chain(dve, order)
            dve.memset(carry[:, :], 0.0).then_inc(carry_zero, 1)

            def step(h):
                o.at(h.c * (K + 1))
                o.link(dve.tensor_copy(kc[:, h.b2, :], keep[:, bass.ds(h.c * K, K)]))
                if hist_parts:
                    a_f, b_f, iota_row, oh_a, oh_b, *_ = hist_parts
                    if not (early(h, 2)):
                        dve.wait_ge(oh_used, h.c - 1)
                    for parts, oh in ((a_f, oh_a), (b_f, oh_b)):
                        dve.tensor_tensor(oh[:, h.b2, :, :],
                                          iota_row[:, :].unsqueeze(1).broadcast_to([P, K, P]),
                                          parts[:, bass.ds(h.c * K, K)].unsqueeze(2).broadcast_to([P, K, P]),
                                          ALU.is_equal).then_inc(oh_ready, 1)
                dve.wait_ge(gathered[h.b4], 16 * K * (h.turn4 + 1))
                if early(h, 1):
                    dve.wait_ge(carry_zero, 1)
                else:
                    dve.wait_ge(summed, h.c)
                for k in range(K):
                    prev = carry[:, :] if k == 0 else rows[:, h.b4, k - 1, :]
                    o.link(dve.scalar_tensor_tensor(rows[:, h.b4, k, :], prev, kc[:, h.b2, k:k + 1],
                                                    rows[:, h.b4, k, :], ALU.mult, ALU.add))
                dve.tensor_copy(carry[:, :], rows[:, h.b4, K - 1, :]).then_inc(summed, 1)
            chunks(dve, step)
            dve.wait_ge(summed, CH)
            o.at(CH * (K + 1))
            o.link(dve.tensor_copy(run_end[:, 0:C], carry[:, :]))

        if hist_parts:
            a_f, b_f, iota_row, oh_a, oh_b, zero_bf, hist, zeros, B = hist_parts

            @block.tensor
            def _(pe):
                def step(h):
                    pe.wait_ge(oh_ready, 2 * h.c + 2)
                    for k in range(K):
                        mm = pe.matmul(hist[:, :], oh_a[:, h.b2, k, :], oh_b[:, h.b2, k, :],
                                       start=(early(h, 1) and k == 0), stop=False)
                    mm.then_inc(oh_used, 1)
                chunks(pe, step)
                pe.matmul(hist[:, :], zero_bf[:, :], zero_bf[:, :], start=False, stop=True).then_inc(counted, 1)
                pe.wait_ge(counted, 1)

            @block.scalar
            def _(act):
                Bv = B[0:EP, :].rearrange("(p t) c -> p (t c)", p=P)

                def step(h):
                    act.wait_ge(summed, h.c + 1)
                    act.dma_start(Bv[:, bass.ds(h.c * (K * C), K * C)], zeros[:, :]).then_inc(zeroed, 16)
                chunks(act, step)
                act.wait_ge(zeroed, 16 * CH)


def counts(nc, hist, before, pre_ps, cnt_ab, end_ab, CNT, END, cnt, has, rcnt, node_id, end_idx, start_idx):
    with semaphores(nc) as sem_, ExitStack() as ctx:
        sem = lambda name: sem_(f"cnt_{name}")
        sb = lambda name, shape, dt=F32: ctx.enter_context(nc.sbuf_tensor(f"cnt_{name}", shape, dt))
        one = sb("one", [P, P])
        tot = sb("tot", [P, 1])
        end = sb("end", [P, J])
        t = sb("t", [P, J])
        u = sb("u", [P, J])
        order, scanned, prefixed, ready, back = sem("order"), sem("scanned"), sem("prefixed"), sem("ready"), sem("back")
        to_dram = sem("to_dram")
        with nc.Block() as block:
            @block.vector
            def _(dve):
                o = Chain(dve, order)
                o.link(dve.memset(one[:, :], 1.0))
                o.link(dve.tensor_copy(cnt_ab[:, :], hist[:, :]))
                o.link(dve.tensor_tensor_scan(end_ab[:, :], one[:, :], cnt_ab[:, :], 0.0, ALU.mult, ALU.add))
                dve.tensor_copy(tot[:, :], end_ab[:, P - 1:P]).then_inc(scanned, 1)
                dve.wait_ge(prefixed, 1)
                dve.tensor_scalar(end_ab[:, :], end_ab[:, :], pre_ps[:, 0:1], None, ALU.add).then_inc(ready, 1)
                dve.wait_ge(back, 32)
                o.link(dve.tensor_scalar(has[:, :], cnt[:, :], 0.0, None, ALU.is_gt))
                o.link(dve.tensor_scalar(t[:, :], cnt[:, :], 1.0, None, ALU.max))
                o.link(dve.reciprocal(t[:, :], t[:, :]))
                o.link(dve.tensor_tensor(rcnt[:, :], t[:, :], has[:, :], ALU.mult))
                o.link(dve.tensor_scalar(t[:, :], end[:, :], -1.0, 0.0, ALU.add, ALU.max))
                o.link(dve.tensor_copy(end_idx[:, :], t[:, :]))
                o.link(dve.tensor_tensor(t[:, :], end[:, :], cnt[:, :], ALU.subtract))
                o.link(dve.tensor_scalar(u[:, :], node_id[:, :], float(EP), None, ALU.add))
                o.link(dve.tensor_tensor(t[:, :], t[:, :], u[:, :], ALU.subtract))
                o.link(dve.tensor_tensor(t[:, :], t[:, :], has[:, :], ALU.mult))
                o.link(dve.tensor_tensor(t[:, :], t[:, :], u[:, :], ALU.add))
                o.link(dve.tensor_copy(start_idx[:, :], t[:, :]))

            @block.tensor
            def _(pe):
                pe.wait_ge(scanned, 1)
                pe.matmul(pre_ps[:, :], before[:, :], tot[:, :], start=True, stop=True).then_inc(prefixed, 1)

            @block.sync
            def _(sp):
                sp.wait_ge(ready, 1)
                sp.dma_start(CNT.rearrange("(a b) -> a b", a=P), cnt_ab[:, :]).then_inc(to_dram, 16)
                sp.dma_start(END.rearrange("(a b) -> a b", a=P), end_ab[:, :]).then_inc(to_dram, 16)
                sp.wait_ge(to_dram, 32)
                sp.dma_start(cnt[:, :], CNT[0:NP].rearrange("(p j) -> p j", p=P)).then_inc(back, 16)
                sp.dma_start(end[:, :], END[0:NP].rearrange("(p j) -> p j", p=P)).then_inc(back, 16)
                sp.wait_ge(back, 32)


def mend(nc, sem_, ctx, tag, S, width, run_end, carried, ident, goes_on, passes, ends_here, lead_idx, mended):
    sem = lambda name: sem_(f"{tag}_m_{name}")
    sb = lambda name, shape, dt=F32: ctx.enter_context(nc.sbuf_tensor(f"{tag}_m_{name}", shape, dt))
    parts = [(lo, min(lo + P, width)) for lo in range(0, width, P)]
    n = len(parts)
    turned_ps = [ctx.enter_context(nc.psum_tensor(f"{tag}_m_turned{i}", [P, P], F32)) for i in range(n)]
    back_ps = [ctx.enter_context(nc.psum_tensor(f"{tag}_m_back{i}", [P, P], F32)) for i in range(n)]
    arriving = sb("arriving", [P, n, P])
    coming = sb("coming", [P, n, P])
    turned, swept, turned_back, order, set_ = (sem(s) for s in ("turned", "swept", "turned_back", "order", "set"))

    def pe_part(pe):
        for i, (lo, hi) in enumerate(parts):
            pe.transpose(turned_ps[i][0:hi - lo, :], run_end[:, lo:hi], ident[:, :]).then_inc(turned, 1)
        for i, (lo, hi) in enumerate(parts):
            w = hi - lo
            pe.wait_ge(swept, i + 1)
            pe.transpose(back_ps[i][:, 0:w], coming[0:w, i, :], ident[0:w, 0:w]).then_inc(turned_back, 1)

    def dve_part(dve):
        o = Chain(dve, order)
        for i, (lo, hi) in enumerate(parts):
            w = hi - lo
            dve.wait_ge(turned, i + 1)
            o.link(dve.memset(arriving[0:w, i, 0:1], 0.0))
            o.link(dve.tensor_tensor(arriving[0:w, i, 1:P], turned_ps[i][0:w, 0:P - 1], goes_on[0:w, 1:P], ALU.mult))
            o.link(dve.tensor_tensor_scan(coming[0:w, i, :], passes[0:w, :], arriving[0:w, i, :], 0.0, ALU.mult, ALU.add))
            dve.tensor_tensor(coming[0:w, i, :], coming[0:w, i, :], ends_here[0:w, :], ALU.mult).then_inc(swept, 1)
        for i, (lo, hi) in enumerate(parts):
            dve.wait_ge(turned_back, i + 1)
            dve.tensor_copy(carried[:, lo:hi], back_ps[i][:, 0:hi - lo]).then_inc(set_, 1)

    def pool_part(pool):
        pool.wait_ge(set_, n)
        pool.indirect_dma_start(S, bass.IndirectOffsetOnAxis(ap=lead_idx[:, 0:1], axis=0), carried[:, 0:width], None,
                                compute_op=ALU.add).then_inc(mended, 16)
        pool.wait_ge(mended, 16)

    return pe_part, dve_part, pool_part


def node_sums(nc, tag, S, X, run_end, carried, ident, goes_on, passes, ends_here, lead_idx, end_idx, rcnt):
    with semaphores(nc) as sem_, ExitStack() as ctx:
        sem = lambda name: sem_(f"{tag}_{name}")
        sb = lambda name, shape, dt=F32: ctx.enter_context(nc.sbuf_tensor(f"{tag}_{name}", shape, dt))
        sums = sb("sums", [P, J, C])
        mended, scaled, stored = sem("mended"), sem("scaled"), sem("stored")
        fetched = [sem(f"fetched{g}") for g in range(NG)]
        block = ctx.enter_context(nc.Block())
        pe_part, dve_part, pool_part = mend(nc, sem_, ctx, tag, S, C, run_end, carried, ident, goes_on,
                                            passes, ends_here, lead_idx, mended)

        @block.tensor
        def _(pe):
            pe_part(pe)

        @block.vector
        def _(dve):
            dve_part(dve)
            for g in range(NG):
                js = slice(g * JG, (g + 1) * JG)
                dve.wait_ge(fetched[g], 16 * JG)
                dve.tensor_tensor(sums[:, js, :], sums[:, js, :],
                                  rcnt[:, js].unsqueeze(2).broadcast_to([P, JG, C]), ALU.mult).then_inc(scaled, 1)

        @block.gpsimd
        def _(pool):
            pool_part(pool)
            for j in range(J):
                pool.indirect_dma_start(sums[:, j, :], None, S,
                                        bass.IndirectOffsetOnAxis(ap=end_idx[:, j:j + 1], axis=0))\
                    .then_inc(fetched[j // JG], 16)

        @block.sync
        def _(sp):
            for g in range(NG):
                sp.wait_ge(scaled, g + 1)
                sp.dma_start(X.rearrange("(p j) c -> p (j c)", p=P)[:, g * JG * C:(g + 1) * JG * C],
                             sums[:, g * JG:(g + 1) * JG, :].rearrange("p j c -> p (j c)")).then_inc(stored, 16)
            sp.wait_ge(stored, 16 * NG)


def layer_norm(o, dve, h, sq, stat, mean, eps_col, root, n):
    G = h.shape[1]
    wide = lambda col: col.unsqueeze(2).broadcast_to([P, G, n])
    o.link(dve.tensor_reduce(mean, h, AX, ALU.add))
    o.link(dve.tensor_scalar(mean, mean, 1.0 / n, None, ALU.mult))
    o.link(dve.tensor_tensor(h, h, wide(mean), ALU.subtract))
    o.link(dve.tensor_tensor(sq, h, h, ALU.mult))
    o.link(dve.tensor_reduce(stat, sq, AX, ALU.add))
    root()
    o.link(dve.reciprocal(stat, stat))
    o.link(dve.tensor_tensor(h, h, wide(stat), ALU.mult))


def both_halves(ap):
    return ap[0:C], ap[C:2 * C]


def node_mlps(nc, x, X, X1, T4, B, start_idx, eps_col, ident, fWh, fbh, fWo, fbo, flw, flb, aWh, alw, alb):
    PAD_J = -(-J // GP) * GP
    NGP = PAD_J // GP
    with semaphores(nc) as sem_, ExitStack() as ctx:
        sem = lambda name: sem_(f"mlp_{name}")
        sb = lambda name, shape, dt=F32: ctx.enter_context(nc.sbuf_tensor(f"mlp_{name}", shape, dt))
        ps = lambda name, shape: ctx.enter_context(nc.psum_tensor(f"mlp_{name}", shape, F32))
        x1 = sb("x1", [P, PAD_J, C])
        x3 = sb("x3", [P, J, C])
        mean, stat = sb("mean", [P, J]), sb("stat", [P, J])
        W = sb("W", [P, 3, P])
        WY = sb("WY", [P, P])
        WO = sb("WO", [P, 2, 2 * C])
        wo = sb("wo", [P, 2 * C])
        wmean = sb("wmean", [P, 1])
        bh = sb("bh", [P, 3])
        bo = sb("bo", [P, 2 * C])
        bo4 = sb("bo4", [1, 4, 2 * C])
        ones = sb("ones", [1, P])
        flw_b, flb_b = sb("flw", [P, 2 * C]), sb("flb", [P, 2 * C])
        alw_b, alb_b = sb("alw", [P, C]), sb("alb", [P, C])
        xT = sb("xT", [P, 4 * P])
        hT = [sb(f"h{i}", [P, 4 * P]) for i in range(3)]
        sq = sb("sq", [P, GP, 2 * C])
        ssq = sb("ssq", [P, GP])
        row = sb("row", [P, 2, GP, ROW])
        tp = ps("tp", [P, 4 * P])
        yp = ps("yp", [P, 4 * P])
        hp = [ps(f"hp{i}", [P, 4 * P]) for i in range(3)]
        op = ps("op", [P, 2 * 4 * P])
        names = "cleared loaded order order2 rooted squares normed w_ready turned x_ready h_ready m_ready y_ready o_ready sq_ready std_ready y_done row_done scattered y_stored x_stored row_stored act_order var2"
        S_ = {k: sem(k) for k in names.split()}
        row_stored = [sem(f"row_stored{b}") for b in range(2)]
        scattered = [sem(f"scattered{b}") for b in range(2)]
        block = ctx.enter_context(nc.Block())
        real = [min(GP, J - g * GP) for g in range(NGP)]

        @block.sync
        def _(sp):
            L = S_["loaded"]
            sp.wait_ge(S_["cleared"], 5)
            sp.dma_start(x1[0:P - 1, 0:J, :], x[0:(P - 1) * J, :].rearrange("(p j) c -> p j c", p=P - 1)).then_inc(L, 16)
            sp.dma_start(x1[P - 1:P, 0:N_LAST, :], x[(P - 1) * J:N, :].rearrange("(p j) c -> p j c", p=1)).then_inc(L, 16)
            sp.dma_start(x3[:, :, :], X.rearrange("(p j) c -> p j c", p=P)).then_inc(L, 16)
            for half in range(2):
                r = slice(C * half, C * half + C)
                for i in range(3):
                    sp.dma_start(W[r, i, r], fWh[i, :, :]).then_inc(L, 16)
                    sp.dma_start(bh[r, i:i + 1], fbh[i, :].rearrange("(c o) -> c o", o=1)).then_inc(L, 16)
                sp.dma_start(WY[r, r], aWh[0, :, :]).then_inc(L, 16)
                sp.dma_start(wo[r, :], fWo).then_inc(L, 16)
            for t, a in ((bo, fbo), (flw_b, flw), (flb_b, flb), (alw_b, alw), (alb_b, alb)):
                sp.dma_start(t[:, :], a.partition_broadcast(P)).then_inc(L, 16)
            sp.wait_ge(S_["normed"], 1)
            sp.dma_start(X1.rearrange("(p j) c -> p j c", p=P), x1[:, 0:J, :]).then_inc(S_["x_stored"], 16)
            for g in range(NGP):
                sp.wait_ge(S_["row_done"], g + 1)
                sp.dma_start(T4.rearrange("(p j) c -> p j c", p=P)[:, g * GP:g * GP + real[g], :],
                             row[:, g % 2, 0:real[g], :]).then_inc(row_stored[g % 2], 16)
            sp.wait_ge(S_["x_stored"], 16)
            for b in range(2):
                sp.wait_ge(row_stored[b], 16 * len(range(b, NGP, 2)))

        n_loaded = 16 * (3 + 2 * 8 + 5)

        @block.vector
        def _(dve):
            o = Chain(dve, S_["order"])
            cl = S_["cleared"]
            dve.memset(x1[96:P, 0:J, :], 0.0).then_inc(cl, 1)
            dve.memset(W[:, :, :], 0.0).then_inc(cl, 1)
            dve.memset(WY[:, :], 0.0).then_inc(cl, 1)
            dve.memset(x1[:, J:PAD_J, :], 0.0).then_inc(cl, 1)
            dve.memset(WO[:, :, :], 0.0).then_inc(cl, 1)
            o.link(dve.memset(ones[:, :], 1.0))
            dve.wait_ge(S_["loaded"], n_loaded)
            for t in (wo, bo):
                o.link(dve.tensor_reduce(wmean[:, :], t[:, :], AX, ALU.add))
                o.link(dve.tensor_scalar(wmean[:, :], wmean[:, :], 1.0 / (2 * C), None, ALU.mult))
                o.link(dve.tensor_scalar(t[:, :], t[:, :], wmean[:, 0:1], None, ALU.subtract))
            for half in range(2):
                r = slice(C * half, C * half + C)
                o.link(dve.tensor_copy(WO[r, half, :], wo[r, :]))
            o.link(dve.tensor_copy(bo4[0:1, :, :], bo[0:1, :].unsqueeze(1).broadcast_to([1, 4, 2 * C])))
            o.link(dve.tensor_scalar(WY[:, :], WY[:, :], 0.5, None, ALU.mult))
            xr = x1[:, 0:J, :]
            o.link(dve.tensor_tensor(xr, xr, x3[:, :, :], ALU.add))

            def root():
                dve.sem_inc(S_["squares"], 1)
                dve.wait_ge(S_["rooted"], 1)
            layer_norm(o, dve, xr, x3[:, :, :], stat[:, :], mean[:, :], eps_col, root, C)
            dve.sem_inc(S_["normed"], 1)
            o2 = Chain(dve, S_["order2"])
            for g in range(NGP):
                rw = row[:, g % 2, :, :]
                xg = x1[:, g * GP:(g + 1) * GP, :]
                n = real[g]
                if g >= 2:
                    dve.wait_ge(row_stored[g % 2], 16 * (g // 2))
                    dve.wait_ge(scattered[g % 2], 16 * sum(real[g % 2:g - 1:2]))
                for i, t in enumerate((alw_b, alb_b)):
                    dve.tensor_tensor(rw[:, :, i * C:(i + 1) * C], xg, t[:, :].unsqueeze(1).broadcast_to([P, GP, C]), ALU.mult)
                dve.wait_ge(S_["y_ready"], g + 1)
                dve.tensor_copy(rw[:, :, 2 * C:3 * C], yp[:, :].rearrange("p (j c) -> p j c", c=C)).then_inc(S_["y_done"], 1)
                dve.wait_ge(S_["sq_ready"], g + 1)
                o2.link(dve.tensor_reduce(ssq[:, :], sq[:, :, :], AX, ALU.add))
                dve.sem_inc(S_["var2"], 1)
                dve.wait_ge(S_["std_ready"], g + 1)
                o2.link(dve.reciprocal(ssq[:, :], ssq[:, :]))
                fx = rw[:, :, 3 * C:5 * C]
                o2.link(dve.tensor_tensor(fx, op[:, :].rearrange("p (j c) -> p j c", c=2 * C),
                                          ssq[:, :].unsqueeze(2).broadcast_to([P, GP, 2 * C]), ALU.mult))
                o2.link(dve.tensor_tensor(fx, fx, flw_b[:, :].unsqueeze(1).broadcast_to([P, GP, 2 * C]), ALU.mult))
                dve.tensor_tensor(fx, fx, flb_b[:, :].unsqueeze(1).broadcast_to([P, GP, 2 * C]), ALU.add)\
                    .then_inc(S_["row_done"], 1)

        @block.scalar
        def _(act):
            act.wait_ge(S_["squares"], 1)
            act.activation(stat[:, :], stat[:, :], ACT.Sqrt, bias=eps_col[:, 0:1], scale=1.0 / C).then_inc(S_["rooted"], 1)
            for g in range(NGP):
                act.wait_ge(S_["turned"], g + 1)
                if g:
                    act.wait_ge(S_["y_ready"], g)
                act.activation(xT[:, :], tp[:, :], ACT.Copy).then_inc(S_["x_ready"], 1)
                for i in range(3):
                    act.wait_ge(S_["m_ready"], 3 * g + i + 1)
                    act.activation(hT[i][:, :], hp[i][:, :], ACT.Relu, bias=bh[:, i:i + 1]).then_inc(S_["h_ready"], 1)
                act.wait_ge(S_["o_ready"], g + 1)
                if g:
                    act.wait_ge(S_["var2"], g)
                act.activation(sq[:, :, :].rearrange("p j c -> p (j c)"), op[:, :], ACT.Square).then_inc(S_["sq_ready"], 1)
                act.wait_ge(S_["var2"], g + 1)
                act.activation(ssq[:, :], ssq[:, :], ACT.Sqrt, bias=eps_col[:, 0:1], scale=1.0 / (2 * C)).then_inc(S_["std_ready"], 1)

        @block.tensor
        def _(pe):
            pe.wait_ge(S_["normed"], 1)
            for g in range(NGP):
                if g:
                    pe.wait_ge(S_["x_ready"], g)
                for q in range(4):
                    j = g * GP + 2 * q
                    mm = pe.transpose(tp[:, q * P:(q + 1) * P], x1[:, j:j + 2, :].rearrange("p j c -> p (j c)"), ident[:, :])
                mm.then_inc(S_["turned"], 1)
                pe.wait_ge(S_["x_ready"], g + 1)
                pe.matmul(hp[0][:, :], W[:, 0, :], xT[:, :], start=True, stop=True).then_inc(S_["m_ready"], 1)
                if g:
                    pe.wait_ge(S_["y_done"], g)
                for q in range(4):
                    mm = pe.matmul(yp[:, q * P:(q + 1) * P], xT[:, q * P:(q + 1) * P], WY[:, :], start=True, stop=True)
                mm.then_inc(S_["y_ready"], 1)
                for i in (1, 2):
                    pe.wait_ge(S_["h_ready"], 3 * g + i)
                    pe.matmul(hp[i][:, :], W[:, i, :], hT[i - 1][:, :], start=True, stop=True).then_inc(S_["m_ready"], 1)
                pe.wait_ge(S_["h_ready"], 3 * g + 3)
                if g:
                    pe.wait_ge(S_["row_done"], g)
                for bank in range(2):
                    pe.matmul(op[:, bank * 512:(bank + 1) * 512], ones[0:1, :], bo4[0:1, :, :].rearrange("p j c -> p (j c)"),
                              start=True, stop=False)
                    for q in range(2):
                        at = bank * 512 + q * 256
                        mm = pe.matmul(op[:, at:at + 256], hT[2][:, (2 * bank + q) * P:(2 * bank + q + 1) * P],
                                       WO[:, :, :].rearrange("p h c -> p (h c)"), start=False, stop=(q == 1))
                mm.then_inc(S_["o_ready"], 1)

        @block.gpsimd
        def _(pool):
            for g in range(NGP):
                pool.wait_ge(S_["y_done"], g + 1)
                for jj in range(real[g]):
                    pool.indirect_dma_start(B, bass.IndirectOffsetOnAxis(ap=start_idx[:, g * GP + jj:g * GP + jj + 1], axis=0),
                                            row[:, g % 2, jj, 2 * C:3 * C], None).then_inc(scattered[g % 2], 16)
            for b in range(2):
                pool.wait_ge(scattered[b], 16 * sum(real[b::2]))


def flux_pass(nc, T4, B, NV, S4, src_sb, keep, first_dst, run_end, ident, eps_col, aWh, abh, aWo, abo):
    Q = K // 2
    H = K * C // 512
    with semaphores(nc) as sem_, ExitStack() as ctx:
        sem = lambda name: sem_(f"flux_{name}")
        sb = lambda name, shape, dt=F32: ctx.enter_context(nc.sbuf_tensor(f"flux_{name}", shape, dt))
        ps = lambda name, shape: ctx.enter_context(nc.psum_tensor(f"flux_{name}", shape, F32))
        rows = sb("rows", [P, NB, K, ROW])
        idx = sb("idx", [P, NB, K], I32)
        nv = sb("nv", [P, NB, K, 2])
        yr = sb("yr", [P, 2, K, C])
        h0 = sb("h0", [P, 2, K, C])
        kc = sb("kc", [P, 4, K])
        row_first = sb("row_first", [P, ROW])
        y_carry = sb("y_carry", [P, C])
        carry = sb("carry", [P, W4])
        hT = [sb(f"h{i + 1}", [P, Q * P]) for i in range(3)]
        sq = sb("sq", [P, K, C])
        ssq = sb("ssq", [P, K])
        fn = sb("fn", [P, 2, K, C])
        ax = sb("ax", [P, K, C])
        run = sb("run", [P, 2, K, W4])
        W = sb("W", [P, 2, P])
        WO = sb("WO", [P, P])
        wo = sb("wo", [P, C])
        wmean = sb("wmean", [P, 1])
        bo = sb("bo", [P, C])
        bo8 = sb("bo8", [1, 8, C])
        ones = sb("ones", [1, P])
        bh = sb("bh", [P, 3])
        tp, mp = ps("tp", [P, Q * P]), ps("mp", [P, Q * P])
        mp2, zp = ps("mp2", [P, Q * P]), ps("zp", [P, Q * P])
        names = ("cleared loaded setup first fetched_first summed issued order_a order_b h0_ready turned h_ready "
                 "m_ready z_ready sq_ready ssq_ready std_ready fn_ready v_done z_used carry_set y_carried nrow_ready")
        S_ = {k: sem(k) for k in names.split()}
        ring = lambda name, n: [sem(f"{name}{b}") for b in range(n)]
        idx_ready, nv_ready, gathered = ring("idx_ready", NB), ring("nv_ready", NB), ring("gathered", NB)
        yr_ready, stored = ring("yr_ready", 2), ring("stored", 2)
        Bv = B[0:EP, :].rearrange("(p t) c -> p (t c)", p=P)
        S4v = S4.rearrange("(p t) c -> p (t c)", p=P)
        NVv = NV.rearrange("(p t) c -> p (t c)", p=P)
    
        n_loaded = 16 * (2 * (2 + 3 + 1) + 1)
        block = ctx.enter_context(nc.Block())

        @block.sync
        def _(sp):
            L = S_["loaded"]
            sp.wait_ge(S_["cleared"], 2)
            for half in range(2):
                r = slice(C * half, C * half + C)
                for i in range(2):
                    sp.dma_start(W[r, i, r], aWh[i + 1, :, :]).then_inc(L, 16)
                for i in range(3):
                    sp.dma_start(bh[r, i:i + 1], abh[i, :].rearrange("(c o) -> c o", o=1)).then_inc(L, 16)
                sp.dma_start(wo[r, :], aWo).then_inc(L, 16)
            sp.dma_start(bo[:, :], abo.partition_broadcast(P)).then_inc(L, 16)

            def store(c, b):
                sp.wait_ge(S_["summed"], c + 1)
                sp.dma_start(S4v[:, bass.ds(c * (K * W4), K * W4)],
                             run[:, b, :, :].rearrange("p k c -> p (k c)")).then_inc(stored[b], 16)

            def step(h):
                if not early(h, NB):
                    sp.wait_ge(S_["summed"], h.c - (NB - 1))
                sp.dma_start(idx[:, h.b4, :], src_sb[:, bass.ds(h.c * K, K)]).then_inc(idx_ready[h.b4], 16)
                sp.dma_start(nv[:, h.b4, :, :].rearrange("p k c -> p (k c)"),
                             NVv[:, bass.ds(h.c * (2 * K), 2 * K)]).then_inc(nv_ready[h.b4], 16)
                if not early(h, 2):
                    sp.wait_ge(S_["h0_ready"], h.c - 1)
                    sp.wait_ge(S_["y_carried"], h.c - 1)
                sp.dma_start(yr[:, h.b2, :, :].rearrange("p k c -> p (k c)"),
                             Bv[:, bass.ds(h.c * (K * C), K * C)]).then_inc(yr_ready[h.b2], 16)
                if not early(h, 3):
                    store(h.c - 3, (h.b2 + 1) % 2)
            chunks(sp, step)
            for c in range(CH - 3, CH):
                store(c, c % 2)
            for b in range(2):
                sp.wait_ge(stored[b], 16 * len(range(b, CH, 2)))

        @block.gpsimd
        def _(pool):
            pool.indirect_dma_start(row_first[:, :], None, T4, bass.IndirectOffsetOnAxis(ap=first_dst[:, 0:1], axis=0))\
                .then_inc(S_["fetched_first"], 16)

            def step(h):
                pool.wait_ge(idx_ready[h.b4], 16 * (h.turn4 + 1))
                if not early(h, NB):
                    pool.wait_ge(S_["v_done"], h.c - (NB - 1))
                pool.sem_inc(S_["issued"], 1)
                for k in range(K):
                    pool.indirect_dma_start(rows[:, h.b4, k, :], None, T4,
                                            bass.IndirectOffsetOnAxis(ap=idx[:, h.b4, k:k + 1], axis=0))\
                        .then_inc(gathered[h.b4], 16)
            chunks(pool, step)

        @block.tensor
        def _(pe):
            pe.wait_ge(S_["setup"], 1)

            def step(h):
                pe.wait_ge(S_["h0_ready"], h.c + 1)
                if not early(h, 1):
                    pe.wait_ge(S_["h_ready"], h.c * 6 - 4)
                for q in range(Q):
                    mm = pe.transpose(tp[:, q * P:(q + 1) * P], h0[:, h.b2, 2 * q:2 * q + 2, :].rearrange("p k c -> p (k c)"),
                                      ident[:, :])
                    if q % 4 == 3:
                        mm.then_inc(S_["turned"], 1)
                for i, m in ((0, mp), (1, mp2)):
                    for half in range(H):
                        pe.wait_ge(S_["h_ready"], h.c * 6 + i * H + half + 1)
                        cols = slice(512 * half, 512 * half + 512)
                        pe.matmul(m[:, cols], W[:, i, :], hT[i][:, cols], start=True, stop=True).then_inc(S_["m_ready"], 1)
                if not early(h, 1):
                    pe.wait_ge(S_["z_used"], h.c)
                for half in range(H):
                    pe.wait_ge(S_["h_ready"], h.c * 6 + 2 * H + half + 1)
                    pe.matmul(zp[:, 512 * half:512 * half + 512], ones[0:1, :], bo8[0:1, :, :].rearrange("p j c -> p (j c)"),
                              start=True, stop=False)
                    for q in range(4):
                        cols = slice((4 * half + q) * P, (4 * half + q + 1) * P)
                        mm = pe.matmul(zp[:, cols], hT[2][:, cols], WO[:, :], start=False, stop=(q == 3))
                    mm.then_inc(S_["z_ready"], 1)
            chunks(pe, step)

        @block.scalar
        def _(act):
            act.wait_ge(S_["setup"], 1)

            def step(h):
                for i, p in enumerate((tp, mp, mp2)):
                    for half in range(H):
                        cols = slice(512 * half, 512 * half + 512)
                        if i == 0:
                            act.wait_ge(S_["turned"], h.c * H + half + 1)
                            if not early(h, 1):
                                act.wait_ge(S_["m_ready"], (h.c - 1) * 2 * H + half + 1)
                        else:
                            act.wait_ge(S_["m_ready"], h.c * 2 * H + (i - 1) * H + half + 1)
                            if i == 2 and not early(h, 1):
                                act.wait_ge(S_["z_ready"], (h.c - 1) * H + half + 1)
                        act.activation(hT[i][:, cols], p[:, cols], ACT.Relu, bias=bh[:, i:i + 1]).then_inc(S_["h_ready"], 1)
                act.wait_ge(gathered[h.b4], 16 * K * (h.turn4 + 1))
                act.wait_ge(nv_ready[h.b4], 16 * (h.turn4 + 1))
                if not early(h, 1):
                    act.wait_ge(S_["v_done"], h.c)
                fx = rows[:, h.b4, :, 3 * C:5 * C].rearrange("p k (c d) -> p k c d", d=2)
                for d in range(2):
                    for k in range(K):
                        a = act.activation(fn[:, d, k, :], fx[:, k, :, d], ACT.Copy, scale=nv[:, h.b4, k, d:d + 1])
                a.then_inc(S_["fn_ready"], 1)
                act.wait_ge(S_["z_ready"], (h.c + 1) * H)
                if not early(h, 1):
                    act.wait_ge(S_["ssq_ready"], h.c)
                act.activation(sq[:, :, :].rearrange("p k c -> p (k c)"), zp[:, :], ACT.Square).then_inc(S_["sq_ready"], 1)
                act.wait_ge(S_["ssq_ready"], h.c + 1)
                act.activation(ssq[:, :], ssq[:, :], ACT.Sqrt, bias=eps_col[:, 0:1], scale=1.0 / C).then_inc(S_["std_ready"], 1)
                if not early(h, 2):
                    act.wait_ge(stored[h.b2], 16 * h.turn2)
                act.activation(run[:, h.b2, :, 2 * C:W4], nv[:, h.b4, :, :], ACT.Copy).then_inc(S_["nrow_ready"], 1)
            chunks(act, step)

        A_STEPS = 1 + K
        B_STEPS = 4 + K

        @block.vector
        def _(dve):
            o = Chain(dve, S_["order_a"])
            dve.memset(W[:, :, :], 0.0).then_inc(S_["cleared"], 1)
            dve.memset(WO[:, :], 0.0).then_inc(S_["cleared"], 1)
            o.link(dve.memset(ones[:, :], 1.0))
            o.link(dve.memset(carry[:, :], 0.0))
            dve.wait_ge(S_["loaded"], n_loaded)
            for t in (wo, bo):
                o.link(dve.tensor_reduce(wmean[:, :], t[:, :], AX, ALU.add))
                o.link(dve.tensor_scalar(wmean[:, :], wmean[:, :], 1.0 / C, None, ALU.mult))
                o.link(dve.tensor_scalar(t[:, :], t[:, :], wmean[:, 0:1], None, ALU.subtract))
            for half in range(2):
                r = slice(C * half, C * half + C)
                o.link(dve.tensor_copy(WO[r, r], wo[r, :]))
            o.link(dve.tensor_copy(bo8[0:1, :, :], bo[0:1, :].unsqueeze(1).broadcast_to([1, 8, C])))
            dve.sem_inc(S_["setup"], 1)
            base = o.n

            def spread(h):
                o.at(h.c * A_STEPS + base)
                o.link(dve.tensor_copy(kc[:, h.b4, :], keep[:, bass.ds(h.c * K, K)]))
                dve.wait_ge(yr_ready[h.b2], 16 * (h.turn2 + 1))
                if early(h, 1):
                    dve.wait_ge(S_["fetched_first"], 16)
                    o.link(dve.tensor_copy(yr[:, h.b2, 0, :], row_first[:, 2 * C:3 * C]))
                else:
                    dve.wait_ge(S_["y_carried"], h.c)
                    o.link(dve.scalar_tensor_tensor(yr[:, h.b2, 0, :], y_carry[:, :], kc[:, h.b4, 0:1],
                                                    yr[:, h.b2, 0, :], ALU.mult, ALU.add))
                for k in range(1, K):
                    o.link(dve.scalar_tensor_tensor(yr[:, h.b2, k, :], yr[:, h.b2, k - 1, :], kc[:, h.b4, k:k + 1],
                                                    yr[:, h.b2, k, :], ALU.mult, ALU.add))
                dve.tensor_copy(y_carry[:, :], yr[:, h.b2, K - 1, :]).then_inc(S_["y_carried"], 1)
                dve.wait_ge(gathered[h.b4], 16 * K * (h.turn4 + 1))
                if not early(h, 2):
                    dve.wait_ge(S_["turned"], (h.c - 1) * H)
                dve.tensor_tensor(h0[:, h.b2, :, :], rows[:, h.b4, :, 2 * C:3 * C], yr[:, h.b2, :, :], ALU.add)\
                    .then_inc(S_["h0_ready"], 1)

            ob = Chain(dve, S_["order_b"])

            def combine(h):
                ob.at(h.c * B_STEPS)
                a, v, f = run[:, h.b2, :, C:2 * C], run[:, h.b2, :, 0:C], fn[:, 0, :, :]
                dve.wait_ge(S_["sq_ready"], h.c + 1)
                dve.tensor_reduce(ssq[:, :], sq[:, :, :], AX, ALU.add).then_inc(S_["ssq_ready"], 1)
                dve.wait_ge(S_["fn_ready"], h.c + 1)
                ob.link(dve.tensor_tensor(f, f, fn[:, 1, :, :], ALU.add))
                ob.link(dve.tensor_tensor(f, f, rows[:, h.b4, :, C:2 * C], ALU.subtract))
                dve.wait_ge(S_["std_ready"], h.c + 1)
                ob.link(dve.reciprocal(ssq[:, :], ssq[:, :]))
                if not early(h, 2):
                    dve.wait_ge(stored[h.b2], 16 * h.turn2)
                dve.tensor_tensor(a, zp[:, :].rearrange("p (k c) -> p k c", c=C),
                                  ssq[:, :].unsqueeze(2).broadcast_to([P, K, C]), ALU.mult).then_inc(S_["z_used"], 1)
                dve.wait_ge(S_["z_used"], h.c + 1)
                ob.link(dve.tensor_tensor(ax[:, :, :], a, rows[:, h.b4, :, 0:C], ALU.mult))
                dve.tensor_tensor(v, f, ax[:, :, :], ALU.subtract).then_inc(S_["v_done"], 1)
                dve.wait_ge(S_["v_done"], h.c + 1)
                dve.wait_ge(S_["nrow_ready"], h.c + 1)
                if not early(h, 1):
                    dve.wait_ge(S_["summed"], h.c)
                for k in range(K):
                    prev = carry[:, :] if k == 0 else run[:, h.b2, k - 1, :]
                    ob.link(dve.scalar_tensor_tensor(run[:, h.b2, k, :], prev, kc[:, h.b4, k:k + 1],
                                                     run[:, h.b2, k, :], ALU.mult, ALU.add))
                dve.tensor_copy(carry[:, :], run[:, h.b2, K - 1, :]).then_inc(S_["summed"], 1)

            def step(h):
                spread(h)
                if not early(h, 1):
                    combine(h.before())
            chunks(dve, step)
            combine(Chunk(0, CH - 1))
            dve.wait_ge(S_["summed"], CH)
            ob.at(CH * B_STEPS)
            ob.link(dve.tensor_copy(run_end[:, :], carry[:, :]))


def final(nc, S4, T4, X1, out, run_end, carried, ident, goes_on, passes, ends_here, lead_idx, end_idx,
          has, cnt, eps_col, alw, alb):
    with semaphores(nc) as sem_, ExitStack() as ctx:
        sem = lambda name: sem_(f"fin_{name}")
        sb = lambda name, shape, dt=F32: ctx.enter_context(nc.sbuf_tensor(f"fin_{name}", shape, dt))
        sums = sb("sums", [P, 2, JG, W4])
        own = sb("own", [P, 2, JG, 2 * C])
        x1 = sb("x1", [P, 2, JG, C])
        sq, am = sb("sq", [P, JG, C]), sb("am", [P, JG, C])
        stat, mean = sb("stat", [P, JG]), sb("mean", [P, JG])
        res = sb("res", [P, J, C])
        alw_b, alb_b = sb("alw", [P, C]), sb("alb", [P, C])
        mended, order, loaded, squares, rooted, used, done, stored = (
            sem(n) for n in ("mended", "order", "loaded", "squares", "rooted", "used", "done", "stored"))
        fetched = [sem(f"fetched{b}") for b in range(2)]
        brought = [sem(f"brought{b}") for b in range(2)]
        block = ctx.enter_context(nc.Block())
        pe_part, dve_part, pool_part = mend(nc, sem_, ctx, "fin", S4, W4, run_end, carried, ident, goes_on,
                                            passes, ends_here, lead_idx, mended)

        @block.tensor
        def _(pe):
            pe_part(pe)

        @block.gpsimd
        def _(pool):
            pool_part(pool)
            for g in range(NG):
                if g >= 2:
                    pool.wait_ge(used, g - 1)
                for jj in range(JG):
                    pool.indirect_dma_start(sums[:, g % 2, jj, :], None, S4,
                                            bass.IndirectOffsetOnAxis(ap=end_idx[:, g * JG + jj:g * JG + jj + 1], axis=0))\
                        .then_inc(fetched[g % 2], 16)

        @block.sync
        def _(sp):
            sp.dma_start(alw_b[:, :], alw.partition_broadcast(P)).then_inc(loaded, 16)
            sp.dma_start(alb_b[:, :], alb.partition_broadcast(P)).then_inc(loaded, 16)
            for g in range(NG):
                if g >= 2:
                    sp.wait_ge(used, g - 1)
                js = slice(g * JG, (g + 1) * JG)
                sp.dma_start(own[:, g % 2, :, :], T4.rearrange("(p j) c -> p j c", p=P)[:, js, 3 * C:5 * C]).then_inc(brought[g % 2], 16)
                sp.dma_start(x1[:, g % 2, :, :], X1.rearrange("(p j) c -> p j c", p=P)[:, js, :]).then_inc(brought[g % 2], 16)
            sp.wait_ge(done, 1)
            sp.dma_start(out[0:(P - 1) * J, :].rearrange("(p j) c -> p j c", p=P - 1), res[0:P - 1, :, :]).then_inc(stored, 16)
            sp.dma_start(out[(P - 1) * J:N, :].rearrange("(p j) c -> p j c", p=1), res[P - 1:P, 0:N_LAST, :]).then_inc(stored, 16)
            sp.wait_ge(stored, 32)

        @block.scalar
        def _(act):
            for g in range(NG):
                act.wait_ge(squares, g + 1)
                act.activation(stat[:, :], stat[:, :], ACT.Sqrt, bias=eps_col[:, 0:1], scale=1.0 / C).then_inc(rooted, 1)

        @block.vector
        def _(dve):
            dve_part(dve)
            o = Chain(dve, order)
            dve.wait_ge(loaded, 32)
            for g in range(NG):
                b, js = g % 2, slice(g * JG, (g + 1) * JG)
                dve.wait_ge(fetched[b], 16 * JG * (g // 2 + 1))
                dve.wait_ge(brought[b], 32 * (g // 2 + 1))
                sm, ow, xg, h = sums[:, b, :, :], own[:, b, :, :], x1[:, b, :, :], res[:, js, :]
                wide = lambda col, n: col.unsqueeze(2).broadcast_to([P, JG, n])
                each = lambda rw: rw.unsqueeze(1).broadcast_to([P, JG, C])
                o.link(dve.tensor_tensor(sm, sm, wide(has[:, js], W4), ALU.mult))
                ow4 = ow.rearrange("p j (c d) -> p j c d", d=2)
                o.link(dve.tensor_tensor(ow4, ow4, sm[:, :, 2 * C:W4].unsqueeze(2).broadcast_to([P, JG, C, 2]), ALU.mult))
                o.link(dve.tensor_tensor(h, ow4[:, :, :, 0], ow4[:, :, :, 1], ALU.add))
                o.link(dve.tensor_tensor(h, h, sm[:, :, 0:C], ALU.add))
                o.link(dve.tensor_tensor(am[:, :, :], sm[:, :, C:2 * C], each(alw_b[:, :]), ALU.mult))
                o.link(dve.tensor_tensor(sq[:, :, :], wide(cnt[:, js], C), each(alb_b[:, :]), ALU.mult))
                o.link(dve.tensor_tensor(am[:, :, :], am[:, :, :], sq[:, :, :], ALU.add))
                o.link(dve.scalar_tensor_tensor(am[:, :, :], am[:, :, :], 4.0, xg, ALU.add, ALU.mult))
                o.link(dve.tensor_tensor(h, h, am[:, :, :], ALU.add))
                o.link(dve.tensor_scalar(h, h, 0.5, None, ALU.mult))
                dve.sem_inc(used, 1)

                def root():
                    dve.sem_inc(squares, 1)
                    dve.wait_ge(rooted, g + 1)
                layer_norm(o, dve, h, sq[:, :, :], stat[:, :], mean[:, :], eps_col, root, C)
            dve.sem_inc(done, 1)


_INS = ["x", "src", "dst", "edge_attr_2"] + [f"L1_gnn_{n}" for n in (
    "flux_Wh", "flux_bh", "flux_Wo", "flux_bo", "flux_ln_w", "flux_ln_b",
    "a_Wh", "a_bh", "a_Wo", "a_bo", "a_ln_w", "a_ln_b")]


def kernel(**inputs):
    import numpy as _np
    import concourse.bacc as _bacc
    from concourse import mybir as _mybir
    from concourse.bass_utils import run_bass_kernel_spmd as _run

    nc = _bacc.Bacc("TRN2", target_bir_lowering=False, num_devices=1)
    arrays, args = {}, []
    for name in _INS:
        a = _np.ascontiguousarray(inputs[name])
        arrays[f"in_{name}"] = a
        args.append(nc.dram_tensor(f"in_{name}", a.shape, _mybir.dt.from_np(a.dtype), kind="ExternalInput").ap())
    args.append(nc.dram_tensor("out_0", (N, C), F32, kind="ExternalOutput").ap())
    build_program(nc, *args)
    r = _run(nc, [arrays], core_ids=[0])
    return r.results[0]["out_0"]
```

```python
from contextlib import ExitStack, contextmanager

import concourse.bass as bass
import concourse.mybir as mybir

F32 = mybir.dt.float32
BF16 = mybir.dt.bfloat16
I32 = mybir.dt.int32
ALU = mybir.AluOpType
ACT = mybir.ActivationFunctionType
AX = mybir.AxisListType.X

P = 128
N = 12500
E = 412500
C = 64
K = 16
NB = 4
CH = -(-E // (P * K))
T = CH * K
EP = P * T
J = -(-N // P)
NP = P * J
U8 = mybir.dt.uint8
FP8 = mybir.dt.float8e4
SLOTS = 64
BLK = 32
NBLK = T // BLK
NEAR = 7
MANY = 4
PAIRS = J // 2
GN = 8
STEPS = P // GN
VALS = P + J
AROW = J * P
E_LAST = E - (P - 1) * T
N_LAST = N - (J - 1) * P
W4 = 2 * C + 2
ROW = 5 * C
JG = 14
NG = J // JG
GP = 8
PADP = max(p for p in range(1, P + 1) if 2 * (EP - E) % p == 0)
EPS = 1e-5
PAD_DST = 128 * P - 1
assert J % JG == 0 and CH > NB and P == 128 and J < P and T % BLK == 0 and 2 * SLOTS == P and JG % 2 == 0
CLEARS = 64
Z = T * C // CLEARS


class Chunk:

    def __init__(self, r, place, ring=NB):
        self.r, self.place, self.ring = r, place, ring
        self.c = r * ring + place
        self.b, self.b2 = place % ring, place % 2
        self.turn = r + place // ring
        self.turn2 = r * (ring // 2) + place // 2

    def before(self):
        return Chunk(self.r, self.place - 1, self.ring)


def chunks(eng, body, total=CH, ring=NB):
    peel = ring + (total - ring) % ring
    for c in range(peel):
        body(Chunk(0, c, ring))
    with eng.Fori(0, (total - peel) // ring) as r:
        for j in range(ring):
            body(Chunk(r, peel + j, ring))


def early(h, n):
    return isinstance(h.c, int) and h.c < n


@contextmanager
def semaphores(nc):
    held = []

    def sem(name):
        held.append(nc.alloc_semaphore(name))
        return held[-1]
    yield sem
    nc.clear_and_free_semaphores(held)
    nc.all_engine_barrier()


class Chain:

    def __init__(self, eng, sem):
        self.eng, self.sem, self.base, self.n = eng, sem, 0, 0

    def link(self, ins):
        self.n += 1
        ins.then_inc(self.sem, 1)
        self.eng.wait_ge(self.sem, self.base + self.n)

    def at(self, base):
        self.base, self.n = base, 0


def build_program(nc, x, src, dst, nvec, fWh, fbh, fWo, fbo, flw, flb, aWh, abh, aWo, abo, alw, alb, out):
    scratch = lambda name, shape, dt=F32: nc.dram_tensor(name, shape, dt).ap()
    X = scratch("x_layer", (NP, C))
    X1 = scratch("x_mid", (NP, C))
    S = scratch("running", (EP, C))
    S4 = scratch("running_flux", (EP, W4))
    B = scratch("first_rows", (EP + NP, C))
    T4 = scratch("table", (NP, ROW))
    NV = scratch("nvec_padded", (EP, 2))
    A = scratch("adjacency", (J * P, AROW), U8)
    FIRST = scratch("block_firsts", (P, NBLK))
    DST = scratch("dst_padded", (EP,))
    SRC2 = scratch("src_split", (EP, 2), BF16)
    SLOT = scratch("slots", (P, PAIRS * 2 * P), BF16)

    top = ExitStack()
    with top:
        sb = lambda name, shape, dt=F32: top.enter_context(nc.sbuf_tensor(name, shape, dt))
        src_sb = sb("src_sb", [P, T], I32)
        keep = sb("keep", [P, T])
        ident = sb("ident", [P, P])
        eps_col = sb("eps_col", [P, 1])
        end_idx = sb("end_idx", [P, J], I32)
        start_idx = sb("start_idx", [P, J], I32)
        has = sb("has", [P, J])
        cnt = sb("cnt", [P, J])
        rcnt = sb("rcnt", [P, J])
        beyond = sb("beyond", [P, 1], I32)
        first_dst = sb("first_dst", [P, 1], I32)
        lead_idx = sb("lead_idx", [P, 1], I32)
        goes_on = sb("goes_on", [P, P])
        passes = sb("passes", [P, P])
        ends_here = sb("ends_here", [P, P])
        run_end = sb("run_end", [P, W4])
        carried = sb("carried", [P, W4])
        ones = sb("ones", [P, P])

        b_zero = nc.alloc_semaphore("b_zero")
        front = ExitStack()
        zeros = front.enter_context(nc.sbuf_tensor("zeros", [P, Z], F32))
        with ExitStack() as ctx:
            sb = lambda name, shape, dt=F32: ctx.enter_context(nc.sbuf_tensor(name, shape, dt))
            src_f = sb("src_f", [P, NEAR + T])
            first_row = sb("first_row", [P, 2 * P])
            prepare(nc, src, dst, nvec, NV, FIRST, DST, SRC2, src_sb, src_f, keep, ident, eps_col, first_dst,
                    lead_idx, goes_on, passes, ends_here, ones, first_row, zeros)
            find_nodes(nc, B, b_zero, zeros, FIRST, DST, SRC2, SLOT, src_f, first_row, ident, ones, cnt, has, rcnt, end_idx,
                       start_idx, beyond)
        build_matrix(nc, SLOT, A, B, b_zero, zeros)
        nc.clear_and_free_semaphores([b_zero])
        nc.all_engine_barrier()
        front.close()

        general = nc.values_load(beyond[0:1, 0:1], min_val=0, max_val=2 * P)
        with nc.If(general == 0):
            nc.all_engine_barrier()
            dense_layers(nc, A, x, X, rcnt)
            nc.all_engine_barrier()
        with nc.Else():
            nc.all_engine_barrier()
            for layer, table in ((1, x), (2, X), (3, X)):
                gcn_pass(nc, f"l{layer}", table, src_sb, keep, S, run_end)
                node_sums(nc, f"n{layer}", S, X, run_end, carried, ident, goes_on, passes, ends_here,
                          lead_idx, end_idx, rcnt)
            nc.all_engine_barrier()
        node_mlps(nc, x, X, X1, T4, B, start_idx, eps_col, ident, fWh, fbh, fWo, fbo, flw, flb,
                  aWh, alw, alb)
        flux_pass(nc, T4, B, NV, S4, src_sb, keep, first_dst, run_end, ident, eps_col,
                  aWh, abh, aWo, abo)
        final(nc, S4, T4, X1, out, run_end, carried, ident, goes_on, passes, ends_here, lead_idx,
              end_idx, has, cnt, eps_col, alw, alb)


def prepare(nc, src, dst, nvec, NV, FIRST, DST, SRC2, src_sb, src_f, keep, ident, eps_col, first_dst,
            lead_idx, goes_on, passes, ends_here, ones, first_row, zeros):
    with semaphores(nc) as sem_, ExitStack() as ctx:
        sem = lambda name: sem_(f"prep_{name}")
        sb = lambda name, shape, dt=F32: ctx.enter_context(nc.sbuf_tensor(f"prep_{name}", shape, dt))
        wide_src = sb("wide_src", [P, NEAR + T], I32)
        dst_i = sb("dst_i", [P, T], I32)
        dst_f, col = sb("dst_f", [P, T]), sb("col", [P, T])
        low = sb("low", [P, T], I32)
        firsts = sb("firsts", [P, NBLK])
        split = sb("split", [P, T, 2], BF16)
        part_row = sb("part_row", [P, 1])
        lead = sb("lead", [P, 1])
        diag = sb("diag", [P, 2 * P])
        one_part = sb("one_part", [P, P])
        rows_ps = ctx.enter_context(nc.psum_tensor("rows_ps", [P, 2 * P], F32))
        cleared, zeroed, loaded, consts, order, pool_order = (
            sem(n) for n in ("cleared", "zeroed", "loaded", "consts", "order", "pool_order"))
        diag_ready, rows_seen, nv_done, tables, written = (
            sem(n) for n in ("diag_ready", "rows_seen", "nv_done", "tables", "written"))
        mid = slice(NEAR, NEAR + T)
        block = ctx.enter_context(nc.Block())

        @block.sync
        def _(sp):
            sp.wait_ge(cleared, 2)
            for own, e in ((dst_i[:, :], dst), (wide_src[:, mid], src)):
                sp.dma_start(own[0:P - 1, :], e[0:(P - 1) * T].rearrange("(p t) -> p t", p=P - 1)).then_inc(loaded, 16)
                sp.dma_start(own[P - 1:P, 0:E_LAST], e[(P - 1) * T:E].rearrange("(p t) -> p t", p=1)).then_inc(loaded, 16)
            sp.dma_start(wide_src[1:P, 0:NEAR], src[0:(P - 1) * T].rearrange("(p t) -> p t", p=P - 1)[:, T - NEAR:T]).then_inc(loaded, 16)
            sp.wait_ge(tables, 1)
            sp.dma_start(DST.rearrange("(p t) -> p t", p=P), dst_f[:, :]).then_inc(written, 16)
            sp.wait_ge(tables, 2)
            sp.dma_start(FIRST, firsts[:, :]).then_inc(written, 16)
            sp.wait_ge(tables, 4)
            sp.dma_start(SRC2.rearrange("(p t) c -> p (t c)", p=P), split[:, :, :].rearrange("p t c -> p (t c)")).then_inc(written, 16)
            sp.wait_ge(written, 48)

        @block.scalar
        def _(act):
            act.dma_start(NV[0:E, :], nvec[:, :]).then_inc(nv_done, 16)
            act.wait_ge(zeroed, 1)
            act.dma_start(NV[E:EP, :].rearrange("t c -> (t c)").rearrange("(p t) -> p t", p=PADP),
                          zeros[0:PADP, 0:2 * (EP - E) // PADP]).then_inc(nv_done, 16)
            act.wait_ge(nv_done, 32)

        @block.gpsimd
        def _(pool):
            o = Chain(pool, pool_order)
            pool.memset(zeros[:, :], 0.0).then_inc(zeroed, 1)
            o.link(pool.memset(ident[:, :], 0.0))
            pool.memset(ones[:, :], 1.0).then_inc(consts, 1)
            pool.affine_select(out=ident[:, :], in_=ident[:, :], compare_op=ALU.not_equal, fill=1.0,
                               base=0, pattern=[[-1, P]], channel_multiplier=1).then_inc(consts, 1)
            pool.iota(part_row[:, :], pattern=[[1, 1]], base=0, channel_multiplier=T,
                      allow_small_or_imprecise_dtypes=True).then_inc(consts, 1)
            pool.iota(col[:, :], pattern=[[1, T]], base=0, channel_multiplier=0,
                      allow_small_or_imprecise_dtypes=True).then_inc(consts, 1)

        @block.tensor
        def _(pe):
            pe.wait_ge(consts, 4)
            pe.wait_ge(diag_ready, 2)
            pe.matmul(rows_ps[:, :], ones[:, :], diag[:, :], start=True, stop=True).then_inc(rows_seen, 1)

        @block.vector
        def _(dve):
            o = Chain(dve, order)
            dve.memset(dst_i[:, :], PAD_DST).then_inc(cleared, 1)
            dve.memset(wide_src[:, :], 0).then_inc(cleared, 1)
            dve.memset(eps_col[:, :], EPS)
            dve.memset(keep[:, 0:1], 0.0)
            dve.memset(goes_on[:, 0:1], 0.0)
            dve.memset(passes[:, 0:1], 0.0)
            dve.memset(ends_here[:, P - 1:P], 1.0)
            dve.wait_ge(loaded, 80)
            dve.tensor_copy(dst_f[:, :], dst_i[:, :]).then_inc(tables, 1)
            dve.wait_ge(tables, 1)
            dve.tensor_copy(firsts[:, :], dst_f[:, :].rearrange("p (b e) -> p b e", e=BLK)[:, :, 0]).then_inc(tables, 1)
            dve.wait_ge(consts, 4)
            dve.tensor_scalar(diag[:, 0:P], ident[:, :], dst_f[:, 0:1], None, ALU.mult).then_inc(diag_ready, 1)
            dve.tensor_scalar(diag[:, P:2 * P], ident[:, :], dst_f[:, T - 1:T], None, ALU.mult).then_inc(diag_ready, 1)
            o.link(dve.tensor_scalar(low[:, :], wide_src[:, mid], P - 1, None, ALU.bitwise_and))
            dve.tensor_copy(split[:, :, 0], low[:, :]).then_inc(tables, 1)
            dve.wait_ge(tables, 3)
            o.link(dve.tensor_scalar(low[:, :], wide_src[:, mid], 7, None, ALU.logical_shift_right))
            dve.tensor_copy(split[:, :, 1], low[:, :]).then_inc(tables, 1)
            dve.tensor_copy(src_sb[:, :], wide_src[:, mid])
            dve.tensor_tensor(keep[:, 1:T], dst_f[:, 1:T], dst_f[:, 0:T - 1], ALU.is_equal)
            dve.tensor_copy(first_dst[:, :], dst_i[:, 0:1])
            o.link(dve.tensor_copy(src_f[:, :], wide_src[:, :]))
            o.link(dve.scalar_tensor_tensor(col[:, :], dst_f[:, :], float(NP), col[:, :], ALU.is_ge, ALU.mult))
            o.link(dve.tensor_tensor(src_f[:, mid], src_f[:, mid], col[:, :], ALU.add))
            o.link(dve.tensor_scalar(col[:, :], dst_f[:, :], dst_f[:, 0:1], None, ALU.is_equal))
            o.link(dve.tensor_reduce(lead[:, :], col[:, :], AX, ALU.add))
            o.link(dve.tensor_scalar(lead[:, :], lead[:, :], part_row[:, 0:1], -1.0, ALU.add, ALU.add))
            dve.tensor_copy(lead_idx[:, :], lead[:, :])
            dve.wait_ge(rows_seen, 1)
            o.link(dve.tensor_copy(first_row[:, :], rows_ps[:, :]))
            fr, lr = first_row[:, 0:P], first_row[:, P:2 * P]
            o.link(dve.tensor_tensor(one_part[:, :], fr, lr, ALU.is_equal))
            o.link(dve.tensor_tensor(goes_on[:, 1:P], fr[:, 1:P], lr[:, 0:P - 1], ALU.is_equal))
            o.link(dve.tensor_tensor(passes[:, 1:P], goes_on[:, 1:P], one_part[:, 0:P - 1], ALU.mult))
            o.link(dve.tensor_scalar(ends_here[:, 0:P - 1], passes[:, 1:P], -1.0, 1.0, ALU.mult, ALU.add))


def find_nodes(nc, B, b_zero, zeros, FIRST, DST, SRC2, SLOT, src_f, first_row, ident, ones, cnt, has, rcnt, end_idx,
               start_idx, beyond):
    with semaphores(nc) as sem_, ExitStack() as ctx:
        sem = lambda name: sem_(f"find_{name}")
        sb = lambda name, shape, dt=F32: ctx.enter_context(nc.sbuf_tensor(f"find_{name}", shape, dt))
        node_id, start, at = sb("node_id", [P, J]), sb("start", [P, J + 1]), sb("at", [P, J])
        slot_id = sb("slot_id", [P, SLOTS])
        idx = [sb(f"idx{i}", [P, J], I32) for i in range(3)]
        less = sb("less", [P, JG, P])
        less2 = sb("less2", [P, JG, P])
        firsts, near = sb("firsts", [P, J, NBLK]), sb("near", [P, J, BLK])
        picked = sb("picked", [P, J, SLOTS, 2], BF16)
        mask = sb("mask", [P, JG, SLOTS], BF16)
        down, wrap = sb("down", [P, P]), sb("wrap", [P, P])
        ident_bf = sb("ident_bf", [P, P], BF16)
        turned_sb = sb("turned_sb", [P, PAIRS, 2, P], BF16)
        same, same_sum = sb("same", [P, T], BF16), sb("same_sum", [P, T], BF16)
        hits, most, t, u, end = sb("hits", [P, NBLK]), sb("most", [P, 1]), sb("t", [P, J]), sb("u", [P, J]), sb("end", [P, J])
        big = sb("big", [P, 1])
        end_ps, any_ps = (ctx.enter_context(nc.psum_tensor(n, [P, J], F32)) for n in ("end_ps", "any_ps"))
        turned_ps = [ctx.enter_context(nc.psum_tensor(f"turned_ps{i}", [P, 2, P], F32)) for i in range(2)]
        consts, order, pool_order, starts, ends, asked, told, masked, turned, taken, slots_out = (
            sem(n) for n in ("consts", "order", "pool_order", "starts", "ends", "asked", "told", "masked",
                             "turned", "taken", "slots_out"))
        found = [sem(f"found{i}") for i in range(3)]
        fetched = [[sem(f"fetched{i}_{g}") for g in range(NG)] for i in range(3)]
        block = ctx.enter_context(nc.Block())

        @block.gpsimd
        def _(pool):
            o = Chain(pool, pool_order)
            pool.iota(node_id[:, :], pattern=[[P, J]], base=0, channel_multiplier=1,
                      allow_small_or_imprecise_dtypes=True).then_inc(consts, 1)
            pool.iota(slot_id[:, :], pattern=[[1, SLOTS]], base=0, channel_multiplier=0,
                      allow_small_or_imprecise_dtypes=True).then_inc(consts, 1)
            o.link(pool.memset(down[:, :], 0.0))
            o.link(pool.memset(wrap[:, :], 0.0))
            pool.affine_select(out=down[:, :], in_=down[:, :], compare_op=ALU.not_equal, fill=1.0,
                               base=-1, pattern=[[-1, P]], channel_multiplier=1).then_inc(consts, 1)
            pool.memset(wrap[0:1, P - 1:P], 1.0).then_inc(consts, 1)
            views = (FIRST, DST.rearrange("(e o) -> e o", o=1), SRC2)
            for i, (table, rows) in enumerate(zip(views, (firsts, near, picked))):
                for g in range(NG):
                    pool.wait_ge(found[i], g + 1)
                    for j in range(g * JG, (g + 1) * JG):
                        into = rows[:, j, :] if i < 2 else rows[:, j, :, :].rearrange("p s c -> p (s c)")
                        pool.indirect_dma_start(into, None, table,
                                                bass.IndirectOffsetOnAxis(ap=idx[i][:, j:j + 1], axis=0))\
                            .then_inc(fetched[i][g], 16)

        @block.tensor
        def _(pe):
            pe.wait_ge(consts, 4)
            pe.wait_ge(starts, 1)
            pe.matmul(end_ps[:, :], down[:, :], start[:, 0:J], start=True, stop=False)
            pe.matmul(end_ps[:, :], wrap[:, :], start[:, 1:J + 1], start=False, stop=True).then_inc(ends, 1)
            pe.wait_ge(asked, 1)
            pe.matmul(any_ps[:, 0:1], ones[:, :], big[:, :], start=True, stop=True).then_inc(told, 1)
            for q in range(PAIRS):
                pe.wait_ge(masked, 2 * q // JG + 1)
                if q >= 2:
                    pe.wait_ge(taken, q - 1)
                for i in range(2):
                    mm = pe.matmul(turned_ps[q % 2][:, i, :], picked[:, 2 * q:2 * q + 2, :, i].rearrange("p j s -> p (j s)"),
                                   ident_bf[:, :], start=True, stop=True)
                mm.then_inc(turned, 1)

        @block.scalar
        def _(act):
            for q in range(PAIRS):
                act.wait_ge(turned, q + 1)
                act.activation(turned_sb[:, q, :, :], turned_ps[q % 2][:, :, :], ACT.Copy).then_inc(taken, 1)

        @block.sync
        def _(sp):
            for z in range(CLEARS - PAIRS):
                sp.dma_start(B[0:EP, :].rearrange("(p t) c -> p (t c)", p=P)[:, z * Z:(z + 1) * Z], zeros[:, :]).then_inc(b_zero, 16)
            sp.wait_ge(taken, PAIRS)
            sp.dma_start(SLOT, turned_sb[:, :, :, :].rearrange("p q i n -> p (q i n)")).then_inc(slots_out, 16)
            sp.wait_ge(slots_out, 16)

        @block.vector
        def _(dve):
            o = Chain(dve, order)
            dve.wait_ge(consts, 4)
            o.link(dve.tensor_copy(ident_bf[:, :], ident[:, :]))
            o.link(dve.memset(start[:, J:J + 1], float(E)))
            for i in range(3):
                for g in range(NG):
                    js = slice(g * JG, (g + 1) * JG)
                    if i:
                        dve.wait_ge(fetched[i - 1][g], 16 * JG)
                    n = (P, NBLK, BLK)[i]
                    keys = (first_row[:, 0:P].unsqueeze(1).broadcast_to([P, JG, P]), firsts[:, js, :], near[:, js, :])[i]
                    buf = (less if g % 2 else less2)[:, :, 0:n]
                    o.link(dve.tensor_tensor(buf, keys, node_id[:, js].unsqueeze(2).broadcast_to([P, JG, n]), ALU.is_lt))
                    o.link(dve.tensor_reduce(t[:, js], buf, AX, ALU.add))
                    if i < 2:
                        o.link(dve.tensor_scalar(t[:, js], t[:, js], -1.0, 0.0, ALU.add, ALU.max))
                    if i == 0:
                        dve.tensor_copy(idx[0][:, js], t[:, js]).then_inc(found[0], 1)
                        o.link(dve.tensor_scalar(at[:, js], t[:, js], float(T), None, ALU.mult))
                    elif i == 1:
                        o.link(dve.scalar_tensor_tensor(at[:, js], t[:, js], float(BLK), at[:, js], ALU.mult, ALU.add))
                        dve.tensor_copy(idx[1][:, js], at[:, js]).then_inc(found[1], 1)
                    else:
                        o.link(dve.tensor_tensor(start[:, js], t[:, js], at[:, js], ALU.add))
                        dve.tensor_copy(idx[2][:, js], start[:, js]).then_inc(found[2], 1)
            dve.sem_inc(starts, 1)
            for d in range(1, NEAR + 1):
                into = same_sum if d == 1 else same
                o.link(dve.tensor_tensor(into[:, :], src_f[:, NEAR:NEAR + T], src_f[:, NEAR - d:NEAR - d + T], ALU.is_equal))
                if d > 1:
                    o.link(dve.tensor_tensor(same_sum[:, :], same_sum[:, :], same[:, :], ALU.add))
            o.link(dve.tensor_reduce(hits[:, :], same_sum[:, :].rearrange("p (b e) -> p b e", e=BLK), AX, ALU.add))
            o.link(dve.tensor_reduce(most[:, :], hits[:, :], AX, ALU.max))
            o.link(dve.tensor_scalar(most[:, :], most[:, :], float(MANY), None, ALU.is_ge))
            dve.wait_ge(ends, 1)
            o.link(dve.tensor_copy(end[:, :], end_ps[:, :]))
            o.link(dve.tensor_tensor(cnt[:, :], end[:, :], start[:, 0:J], ALU.subtract))
            o.link(dve.tensor_reduce(big[:, :], cnt[:, :], AX, ALU.max))
            o.link(dve.tensor_scalar(big[:, :], big[:, :], float(SLOTS), None, ALU.is_gt))
            dve.tensor_tensor(big[:, :], big[:, :], most[:, :], ALU.add).then_inc(asked, 1)
            for g in range(NG):
                js = slice(g * JG, (g + 1) * JG)
                dve.wait_ge(fetched[2][g], 16 * JG)
                o.link(dve.tensor_tensor(mask[:, :, :], slot_id[:, :].unsqueeze(1).broadcast_to([P, JG, SLOTS]),
                                         cnt[:, js].unsqueeze(2).broadcast_to([P, JG, SLOTS]), ALU.is_lt))
                o.link(dve.scalar_tensor_tensor(picked[:, js, :, 0], picked[:, js, :, 0], 1.0, mask[:, :, :], ALU.add, ALU.mult))
                dve.sem_inc(masked, 1)
            dve.wait_ge(told, 1)
            o.link(dve.tensor_copy(beyond[:, :], any_ps[:, 0:1]))
            o.link(dve.tensor_scalar(has[:, :], cnt[:, :], 0.0, None, ALU.is_gt))
            o.link(dve.tensor_scalar(t[:, :], cnt[:, :], 1.0, None, ALU.max))
            o.link(dve.reciprocal(t[:, :], t[:, :]))
            o.link(dve.tensor_tensor(rcnt[:, :], t[:, :], has[:, :], ALU.mult))
            o.link(dve.tensor_scalar(t[:, :], end[:, :], -1.0, 0.0, ALU.add, ALU.max))
            o.link(dve.tensor_copy(end_idx[:, :], t[:, :]))
            o.link(dve.tensor_scalar(u[:, :], node_id[:, :], float(EP), None, ALU.add))
            o.link(dve.tensor_tensor(t[:, :], start[:, 0:J], u[:, :], ALU.subtract))
            o.link(dve.tensor_tensor(t[:, :], t[:, :], has[:, :], ALU.mult))
            o.link(dve.tensor_tensor(t[:, :], t[:, :], u[:, :], ALU.add))
            o.link(dve.tensor_copy(start_idx[:, :], t[:, :]))


def build_matrix(nc, SLOT, A, B, b_zero, zeros):
    with semaphores(nc) as sem_, ExitStack() as ctx:
        sem = lambda name: sem_(f"bld_{name}")
        sb = lambda name, shape, dt=F32: ctx.enter_context(nc.sbuf_tensor(f"bld_{name}", shape, dt))
        slot = sb("slot", [P, 2, 2, P], BF16)
        hot = sb("hot", [P, 2, VALS, P], BF16)
        win = sb("win", [P, 2, 2, J, P], U8)
        count = [[ctx.enter_context(nc.psum_tensor(f"count{s}_{half}", [P, 2, 512], F32)) for half in range(2)]
                 for s in range(2)]
        hot_ready, counted, taken = (sem(n) for n in ("hot_ready", "counted", "taken"))
        issued, storing = sem("issued"), sem("storing")
        brought, stored = ([sem(f"{n}{b}") for b in range(2)] for n in ("brought", "stored"))
        block = ctx.enter_context(nc.Block())

        @block.sync
        def _(sp):
            def store(h):
                sp.wait_ge(taken, (h.c + 1) * 2 * STEPS)
                sp.sem_inc(storing, 1)
                for half in range(2):
                    sp.dma_start(A[bass.ds((2 * h.c + half) * P, P), :],
                                 win[:, h.b, half, :, :].rearrange("p j n -> p (j n)")).then_inc(stored[h.b], 16)

            def step(h):
                if not early(h, 2):
                    sp.wait_ge(hot_ready, h.c - 1)
                    sp.sem_inc(storing, 1)
                sp.dma_start(slot[:, h.b, :, :].rearrange("p i n -> p (i n)"),
                             SLOT[:, bass.ds(h.c * 2 * P, 2 * P)]).then_inc(brought[h.b], 16)
                if not early(h, 2):
                    store(h.before().before())
            chunks(sp, step, PAIRS, 2)
            for c in range(PAIRS - 2, PAIRS):
                store(Chunk(0, c, 2))
            for b in range(2):
                sp.wait_ge(stored[b], 32 * len(range(b, PAIRS, 2)))

        @block.vector
        def _(dve):
            def step(h):
                dve.wait_ge(brought[h.b], 16 * (h.turn + 1))
                if not early(h, 2):
                    dve.wait_ge(counted, (h.c - 1) * 2 * STEPS)
                for v in range(VALS):
                    low = v < P
                    ins = dve.tensor_scalar(hot[:, h.b, v, :], slot[:, h.b, 0 if low else 1, :],
                                            float(v + 1 if low else v - P), None, ALU.is_equal)
                ins.then_inc(hot_ready, 1)
            chunks(dve, step, PAIRS, 2)

        @block.tensor
        def _(pe):
            def step(h):
                pe.wait_ge(hot_ready, h.c + 1)
                for s in range(STEPS):
                    if s >= 2 or not early(h, 1):
                        pe.wait_ge(taken, h.c * 2 * STEPS + 2 * (s - 1))
                    for i in range(GN):
                        n = s * GN + i
                        for half in range(2):
                            r = slice(half * SLOTS, (half + 1) * SLOTS)
                            to = count[s % 2][half][:, i // 4, (i % 4) * J:(i % 4 + 1) * J]
                            mm = pe.matmul(to, hot[r, h.b, 0:P, n], hot[r, h.b, P:VALS, n], start=True, stop=True)
                            if i == GN - 1:
                                mm.then_inc(counted, 1)
            chunks(pe, step, PAIRS, 2)

        @block.scalar
        def _(act):
            Bv = B[0:EP, :].rearrange("(p t) c -> p (t c)", p=P)

            def step(h):
                if not early(h, 2):
                    act.wait_ge(stored[h.b], 32 * h.turn)
                for s in range(STEPS):
                    for half in range(2):
                        act.wait_ge(counted, h.c * 2 * STEPS + 2 * s + half + 1)
                        act.sem_inc(issued, 1)
                        to = win[:, h.b, half, :, s * GN:(s + 1) * GN].bitcast(FP8).rearrange("p j (b n) -> p b n j", b=2)
                        act.activation(to, count[s % 2][half][:, :, 0:4 * J].rearrange("p b (n j) -> p b n j", n=4),
                                       ACT.Copy, saturate=True).then_inc(taken, 1)
                act.dma_start(Bv[:, bass.ds((h.c + CLEARS - PAIRS) * Z, Z)], zeros[:, :]).then_inc(b_zero, 16)
            chunks(act, step, PAIRS, 2)
            act.wait_ge(b_zero, 16 * CLEARS)


def split3(o, dve, whole, parts, rest):
    o.link(dve.tensor_copy(parts[0], whole))
    o.link(dve.tensor_tensor(rest, whole, parts[0], ALU.subtract))
    o.link(dve.tensor_copy(parts[1], rest))
    o.link(dve.tensor_tensor(rest, rest, parts[1], ALU.subtract))
    o.link(dve.tensor_copy(parts[2], rest))


def dense_layers(nc, A, x, X, rcnt):
    with ExitStack() as ctx:
        sb = lambda name, shape, dt=F32: ctx.enter_context(nc.sbuf_tensor(f"d_{name}", shape, dt))
        parts = [sb(f"parts{i}", [P, J, 3 * C], BF16) for i in range(2)]
        with semaphores(nc) as sem_, ExitStack() as ctx2:
            x0 = ctx2.enter_context(nc.sbuf_tensor("d_x0", [P, J, C], F32))
            cleared, loaded, order = sem_("d_cleared"), sem_("d_loaded"), sem_("d_order")
            block = ctx2.enter_context(nc.Block())

            @block.sync
            def _(sp):
                sp.wait_ge(cleared, 1)
                sp.dma_start(x0[:, 0:J - 1, :], x[0:(J - 1) * P, :].rearrange("(j p) c -> p j c", p=P)).then_inc(loaded, 16)
                sp.dma_start(x0[0:N_LAST, J - 1, :], x[(J - 1) * P:N, :]).then_inc(loaded, 16)

            @block.vector
            def _(dve):
                o = Chain(dve, order)
                dve.memset(x0[:, J - 1, :], 0.0).then_inc(cleared, 1)
                dve.wait_ge(loaded, 32)
                split3(o, dve, x0[:, :, :], [parts[0][:, :, i * C:(i + 1) * C] for i in range(3)], x0[:, :, :])

        win = sb("win", [P, 2, J * P], U8)
        xw = sb("xw", [P, 2, C])
        rest = sb("rest", [P, C])
        xp = sb("xp", [P, 2, 3 * C], BF16)
        acc = [ctx.enter_context(nc.psum_tensor(f"d_acc{i}", [P, 512], F32)) for i in range(2)]
        for layer in range(3):
            now, new = parts[layer % 2], parts[1 - layer % 2]
            with semaphores(nc) as sem_, nc.Block() as block:
                sem = lambda name: sem_(f"d{layer}_{name}")
                brought = [sem(f"brought{b}") for b in range(2)]
                issued, summed, order, made, stored = (sem(n) for n in ("issued", "summed", "order", "made", "stored"))
                last = layer == 2

                @block.sync
                def _(sp):
                    def step(h):
                        if not early(h, 2):
                            sp.wait_ge(summed, h.c - 1)
                        sp.dma_start(win[:, h.b, :], A[bass.ds(h.c * P, P), :]).then_inc(brought[h.b], 16)
                    chunks(sp, step, J, 2)

                @block.tensor
                def _(pe):
                    def step(h):
                        pe.wait_ge(brought[h.b], 16 * (h.turn + 1))
                        if not early(h, 2):
                            pe.wait_ge(made, h.c - 1)
                        pe.sem_inc(issued, 1)
                        for j in range(J):
                            mm = pe.matmul(acc[h.b][:, 0:3 * C], win[:, h.b, j * P:(j + 1) * P].bitcast(FP8),
                                           now[:, j, :], start=(j == 0), stop=(j == J - 1))
                        mm.then_inc(summed, 1)
                    chunks(pe, step, J, 2)

                @block.vector
                def _(dve):
                    o = Chain(dve, order)

                    def step(h):
                        o.at(h.c * 7)
                        dve.wait_ge(summed, h.c + 1)
                        if last and not early(h, 2):
                            dve.wait_ge(stored, 16 * (h.c - 1))
                        xh = xw[:, h.b, :]
                        o.link(dve.tensor_reduce(xh, acc[h.b][:, 0:3 * C].rearrange("p (t c) -> p c t", t=3), AX, ALU.add))
                        o.link(dve.tensor_scalar(xh, xh, rcnt[:, bass.ds(h.c, 1)], None, ALU.mult))
                        split3(o, dve, xh, [xp[:, h.b, i * C:(i + 1) * C] for i in range(3)], rest[:, :])
                        dve.tensor_copy(new[:, bass.ds(h.c, 1), :], xp[:, h.b, :].unsqueeze(1)).then_inc(made, 1)
                        dve.wait_ge(made, h.c + 1)
                    chunks(dve, step, J, 2)

                if last:
                    @block.scalar
                    def _(act):
                        def step(h):
                            act.wait_ge(made, h.c + 1)
                            act.dma_start(X[bass.ds(h.c * P, P), :], xw[:, h.b, :]).then_inc(stored, 16)
                            act.wait_ge(stored, 16 * (h.c + 1))
                        chunks(act, step, J, 2)


def gcn_pass(nc, tag, table, src_sb, keep, S, run_end):
    with semaphores(nc) as sem_, ExitStack() as ctx:
        sem = lambda name: sem_(f"{tag}_{name}")
        sb = lambda name, shape, dt=F32: ctx.enter_context(nc.sbuf_tensor(f"{tag}_{name}", shape, dt))
        rows = sb("rows", [P, NB, K, C])
        idx = sb("idx", [P, NB, K], I32)
        kc = sb("kc", [P, 2, K])
        carry = sb("carry", [P, C])
        idx_ready, gathered, stored = ([sem(f"{n}{b}") for b in range(NB)] for n in ("idx_ready", "gathered", "stored"))
        issued = sem("issued")
        order = sem("order")
        summed = sem("summed")
        carry_zero = sem("carry_zero")
        Sv = S.rearrange("(p t) c -> p (t c)", p=P)

        with nc.Block() as block:
            @block.sync
            def _(sp):
                def store(c, b):
                    sp.wait_ge(summed, c + 1)
                    sp.dma_start(Sv[:, bass.ds(c * (K * C), K * C)],
                                 rows[:, b, :, :].rearrange("p k c -> p (k c)")).then_inc(stored[b], 16)

                def step(h):
                    if not (early(h, NB)):
                        sp.wait_ge(summed, h.c - (NB - 1))
                    sp.dma_start(idx[:, h.b, :], src_sb[:, bass.ds(h.c * K, K)]).then_inc(idx_ready[h.b], 16)
                    if not (early(h, 3)):
                        store(h.c - 3, (h.b + 1) % NB)
                chunks(sp, step)
                for c in range(CH - 3, CH):
                    store(c, c % NB)
                for b in range(NB):
                    sp.wait_ge(stored[b], 16 * len(range(b, CH, NB)))

            @block.gpsimd
            def _(pool):
                def step(h):
                    pool.wait_ge(idx_ready[h.b], 16 * (h.turn + 1))
                    if not (early(h, NB)):
                        pool.wait_ge(stored[h.b], 16 * h.turn)
                    pool.sem_inc(issued, 1)
                    for k in range(K):
                        pool.indirect_dma_start(rows[:, h.b, k, :], None, table,
                                                bass.IndirectOffsetOnAxis(ap=idx[:, h.b, k:k + 1], axis=0))\
                            .then_inc(gathered[h.b], 16)
                chunks(pool, step)

            @block.vector
            def _(dve):
                o = Chain(dve, order)
                dve.memset(carry[:, :], 0.0).then_inc(carry_zero, 1)

                def step(h):
                    o.at(h.c * (K + 1))
                    o.link(dve.tensor_copy(kc[:, h.b2, :], keep[:, bass.ds(h.c * K, K)]))
                    dve.wait_ge(gathered[h.b], 16 * K * (h.turn + 1))
                    if early(h, 1):
                        dve.wait_ge(carry_zero, 1)
                    else:
                        dve.wait_ge(summed, h.c)
                    for k in range(K):
                        prev = carry[:, :] if k == 0 else rows[:, h.b, k - 1, :]
                        o.link(dve.scalar_tensor_tensor(rows[:, h.b, k, :], prev, kc[:, h.b2, k:k + 1],
                                                        rows[:, h.b, k, :], ALU.mult, ALU.add))
                    dve.tensor_copy(carry[:, :], rows[:, h.b, K - 1, :]).then_inc(summed, 1)
                chunks(dve, step)
                dve.wait_ge(summed, CH)
                o.at(CH * (K + 1))
                o.link(dve.tensor_copy(run_end[:, 0:C], carry[:, :]))


def mend(nc, sem_, ctx, tag, S, width, run_end, carried, ident, goes_on, passes, ends_here, lead_idx, mended):
    sem = lambda name: sem_(f"{tag}_m_{name}")
    sb = lambda name, shape, dt=F32: ctx.enter_context(nc.sbuf_tensor(f"{tag}_m_{name}", shape, dt))
    parts = [(lo, min(lo + P, width)) for lo in range(0, width, P)]
    n = len(parts)
    turned_ps = [ctx.enter_context(nc.psum_tensor(f"{tag}_m_turned{i}", [P, P], F32)) for i in range(n)]
    back_ps = [ctx.enter_context(nc.psum_tensor(f"{tag}_m_back{i}", [P, P], F32)) for i in range(n)]
    arriving = sb("arriving", [P, n, P])
    coming = sb("coming", [P, n, P])
    turned, swept, turned_back, order, set_ = (sem(s) for s in ("turned", "swept", "turned_back", "order", "set"))

    def pe_part(pe):
        for i, (lo, hi) in enumerate(parts):
            pe.transpose(turned_ps[i][0:hi - lo, :], run_end[:, lo:hi], ident[:, :]).then_inc(turned, 1)
        for i, (lo, hi) in enumerate(parts):
            w = hi - lo
            pe.wait_ge(swept, i + 1)
            pe.transpose(back_ps[i][:, 0:w], coming[0:w, i, :], ident[0:w, 0:w]).then_inc(turned_back, 1)

    def dve_part(dve):
        o = Chain(dve, order)
        for i, (lo, hi) in enumerate(parts):
            w = hi - lo
            dve.wait_ge(turned, i + 1)
            o.link(dve.memset(arriving[0:w, i, 0:1], 0.0))
            o.link(dve.tensor_tensor(arriving[0:w, i, 1:P], turned_ps[i][0:w, 0:P - 1], goes_on[0:w, 1:P], ALU.mult))
            o.link(dve.tensor_tensor_scan(coming[0:w, i, :], passes[0:w, :], arriving[0:w, i, :], 0.0, ALU.mult, ALU.add))
            dve.tensor_tensor(coming[0:w, i, :], coming[0:w, i, :], ends_here[0:w, :], ALU.mult).then_inc(swept, 1)
        for i, (lo, hi) in enumerate(parts):
            dve.wait_ge(turned_back, i + 1)
            dve.tensor_copy(carried[:, lo:hi], back_ps[i][:, 0:hi - lo]).then_inc(set_, 1)

    def pool_part(pool):
        pool.wait_ge(set_, n)
        pool.indirect_dma_start(S, bass.IndirectOffsetOnAxis(ap=lead_idx[:, 0:1], axis=0), carried[:, 0:width], None,
                                compute_op=ALU.add).then_inc(mended, 16)
        pool.wait_ge(mended, 16)

    return pe_part, dve_part, pool_part


def node_sums(nc, tag, S, X, run_end, carried, ident, goes_on, passes, ends_here, lead_idx, end_idx, rcnt):
    with semaphores(nc) as sem_, ExitStack() as ctx:
        sem = lambda name: sem_(f"{tag}_{name}")
        sb = lambda name, shape, dt=F32: ctx.enter_context(nc.sbuf_tensor(f"{tag}_{name}", shape, dt))
        sums = sb("sums", [P, J, C])
        mended, scaled, stored = sem("mended"), sem("scaled"), sem("stored")
        fetched = [sem(f"fetched{g}") for g in range(NG)]
        block = ctx.enter_context(nc.Block())
        pe_part, dve_part, pool_part = mend(nc, sem_, ctx, tag, S, C, run_end, carried, ident, goes_on,
                                            passes, ends_here, lead_idx, mended)

        @block.tensor
        def _(pe):
            pe_part(pe)

        @block.vector
        def _(dve):
            dve_part(dve)
            for g in range(NG):
                js = slice(g * JG, (g + 1) * JG)
                dve.wait_ge(fetched[g], 16 * JG)
                dve.tensor_tensor(sums[:, js, :], sums[:, js, :],
                                  rcnt[:, js].unsqueeze(2).broadcast_to([P, JG, C]), ALU.mult).then_inc(scaled, 1)

        @block.gpsimd
        def _(pool):
            pool_part(pool)
            for j in range(J):
                pool.indirect_dma_start(sums[:, j, :], None, S,
                                        bass.IndirectOffsetOnAxis(ap=end_idx[:, j:j + 1], axis=0))\
                    .then_inc(fetched[j // JG], 16)

        @block.sync
        def _(sp):
            for g in range(NG):
                sp.wait_ge(scaled, g + 1)
                sp.dma_start(X.rearrange("(j p) c -> p j c", p=P)[:, g * JG:(g + 1) * JG, :],
                             sums[:, g * JG:(g + 1) * JG, :]).then_inc(stored, 16)
            sp.wait_ge(stored, 16 * NG)


def layer_norm(o, dve, h, sq, stat, mean, eps_col, root, n):
    G = h.shape[1]
    wide = lambda col: col.unsqueeze(2).broadcast_to([P, G, n])
    o.link(dve.tensor_reduce(mean, h, AX, ALU.add))
    o.link(dve.tensor_scalar(mean, mean, 1.0 / n, None, ALU.mult))
    o.link(dve.tensor_tensor(h, h, wide(mean), ALU.subtract))
    o.link(dve.tensor_tensor(sq, h, h, ALU.mult))
    o.link(dve.tensor_reduce(stat, sq, AX, ALU.add))
    root()
    o.link(dve.reciprocal(stat, stat))
    o.link(dve.tensor_tensor(h, h, wide(stat), ALU.mult))


def both_halves(ap):
    return ap[0:C], ap[C:2 * C]


def node_mlps(nc, x, X, X1, T4, B, start_idx, eps_col, ident, fWh, fbh, fWo, fbo, flw, flb, aWh, alw, alb):
    PAD_J = -(-J // GP) * GP
    NGP = PAD_J // GP
    with semaphores(nc) as sem_, ExitStack() as ctx:
        sem = lambda name: sem_(f"mlp_{name}")
        sb = lambda name, shape, dt=F32: ctx.enter_context(nc.sbuf_tensor(f"mlp_{name}", shape, dt))
        ps = lambda name, shape: ctx.enter_context(nc.psum_tensor(f"mlp_{name}", shape, F32))
        x1 = sb("x1", [P, PAD_J, C])
        x3 = sb("x3", [P, J, C])
        mean, stat = sb("mean", [P, J]), sb("stat", [P, J])
        W = sb("W", [P, 3, P])
        WY = sb("WY", [P, P])
        WO = sb("WO", [P, 2, 2 * C])
        wo = sb("wo", [P, 2 * C])
        wmean = sb("wmean", [P, 1])
        bh = sb("bh", [P, 3])
        bo = sb("bo", [P, 2 * C])
        bo4 = sb("bo4", [1, 4, 2 * C])
        ones = sb("ones", [1, P])
        flw_b, flb_b = sb("flw", [P, 2 * C]), sb("flb", [P, 2 * C])
        alw_b, alb_b = sb("alw", [P, C]), sb("alb", [P, C])
        xT = sb("xT", [P, 4 * P])
        hT = [sb(f"h{i}", [P, 4 * P]) for i in range(3)]
        sq = sb("sq", [P, GP, 2 * C])
        ssq = sb("ssq", [P, GP])
        row = sb("row", [P, 2, GP, ROW])
        tp = ps("tp", [P, 4 * P])
        yp = ps("yp", [P, 4 * P])
        hp = [ps(f"hp{i}", [P, 4 * P]) for i in range(3)]
        op = ps("op", [P, 2 * 4 * P])
        names = "cleared loaded order order2 rooted squares normed w_ready turned x_ready h_ready m_ready y_ready o_ready sq_ready std_ready y_done row_done scattered y_stored x_stored row_stored act_order var2"
        S_ = {k: sem(k) for k in names.split()}
        row_stored = [sem(f"row_stored{b}") for b in range(2)]
        scattered = [sem(f"scattered{b}") for b in range(2)]
        block = ctx.enter_context(nc.Block())
        real = [min(GP, J - g * GP) for g in range(NGP)]

        @block.sync
        def _(sp):
            L = S_["loaded"]
            sp.wait_ge(S_["cleared"], 5)
            sp.dma_start(x1[:, 0:J - 1, :], x[0:(J - 1) * P, :].rearrange("(j p) c -> p j c", p=P)).then_inc(L, 16)
            sp.dma_start(x1[0:N_LAST, J - 1, :], x[(J - 1) * P:N, :]).then_inc(L, 16)
            sp.dma_start(x3[:, :, :], X.rearrange("(j p) c -> p j c", p=P)).then_inc(L, 16)
            for half in range(2):
                r = slice(C * half, C * half + C)
                for i in range(3):
                    sp.dma_start(W[r, i, r], fWh[i, :, :]).then_inc(L, 16)
                    sp.dma_start(bh[r, i:i + 1], fbh[i, :].rearrange("(c o) -> c o", o=1)).then_inc(L, 16)
                sp.dma_start(WY[r, r], aWh[0, :, :]).then_inc(L, 16)
                sp.dma_start(wo[r, :], fWo).then_inc(L, 16)
            for t, a in ((bo, fbo), (flw_b, flw), (flb_b, flb), (alw_b, alw), (alb_b, alb)):
                sp.dma_start(t[:, :], a.partition_broadcast(P)).then_inc(L, 16)
            sp.wait_ge(S_["normed"], 1)
            sp.dma_start(X1.rearrange("(j p) c -> p j c", p=P), x1[:, 0:J, :]).then_inc(S_["x_stored"], 16)
            for g in range(NGP):
                sp.wait_ge(S_["row_done"], g + 1)
                sp.dma_start(T4.rearrange("(j p) c -> p j c", p=P)[:, g * GP:g * GP + real[g], :],
                             row[:, g % 2, 0:real[g], :]).then_inc(row_stored[g % 2], 16)
            sp.wait_ge(S_["x_stored"], 16)
            for b in range(2):
                sp.wait_ge(row_stored[b], 16 * len(range(b, NGP, 2)))

        n_loaded = 16 * (3 + 2 * 8 + 5)

        @block.vector
        def _(dve):
            o = Chain(dve, S_["order"])
            cl = S_["cleared"]
            dve.memset(x1[:, J - 1, :], 0.0).then_inc(cl, 1)
            dve.memset(W[:, :, :], 0.0).then_inc(cl, 1)
            dve.memset(WY[:, :], 0.0).then_inc(cl, 1)
            dve.memset(x1[:, J:PAD_J, :], 0.0).then_inc(cl, 1)
            dve.memset(WO[:, :, :], 0.0).then_inc(cl, 1)
            o.link(dve.memset(ones[:, :], 1.0))
            dve.wait_ge(S_["loaded"], n_loaded)
            for t in (wo, bo):
                o.link(dve.tensor_reduce(wmean[:, :], t[:, :], AX, ALU.add))
                o.link(dve.tensor_scalar(wmean[:, :], wmean[:, :], 1.0 / (2 * C), None, ALU.mult))
                o.link(dve.tensor_scalar(t[:, :], t[:, :], wmean[:, 0:1], None, ALU.subtract))
            for half in range(2):
                r = slice(C * half, C * half + C)
                o.link(dve.tensor_copy(WO[r, half, :], wo[r, :]))
            o.link(dve.tensor_copy(bo4[0:1, :, :], bo[0:1, :].unsqueeze(1).broadcast_to([1, 4, 2 * C])))
            o.link(dve.tensor_scalar(WY[:, :], WY[:, :], 0.5, None, ALU.mult))
            xr = x1[:, 0:J, :]
            o.link(dve.tensor_tensor(xr, xr, x3[:, :, :], ALU.add))

            def root():
                dve.sem_inc(S_["squares"], 1)
                dve.wait_ge(S_["rooted"], 1)
            layer_norm(o, dve, xr, x3[:, :, :], stat[:, :], mean[:, :], eps_col, root, C)
            dve.sem_inc(S_["normed"], 1)
            o2 = Chain(dve, S_["order2"])
            for g in range(NGP):
                rw = row[:, g % 2, :, :]
                xg = x1[:, g * GP:(g + 1) * GP, :]
                n = real[g]
                if g >= 2:
                    dve.wait_ge(row_stored[g % 2], 16 * (g // 2))
                    dve.wait_ge(scattered[g % 2], 16 * sum(real[g % 2:g - 1:2]))
                for i, t in enumerate((alw_b, alb_b)):
                    dve.tensor_tensor(rw[:, :, i * C:(i + 1) * C], xg, t[:, :].unsqueeze(1).broadcast_to([P, GP, C]), ALU.mult)
                dve.wait_ge(S_["y_ready"], g + 1)
                dve.tensor_copy(rw[:, :, 2 * C:3 * C], yp[:, :].rearrange("p (j c) -> p j c", c=C)).then_inc(S_["y_done"], 1)
                dve.wait_ge(S_["sq_ready"], g + 1)
                o2.link(dve.tensor_reduce(ssq[:, :], sq[:, :, :], AX, ALU.add))
                dve.sem_inc(S_["var2"], 1)
                dve.wait_ge(S_["std_ready"], g + 1)
                o2.link(dve.reciprocal(ssq[:, :], ssq[:, :]))
                fx = rw[:, :, 3 * C:5 * C]
                o2.link(dve.tensor_tensor(fx, op[:, :].rearrange("p (j c) -> p j c", c=2 * C),
                                          ssq[:, :].unsqueeze(2).broadcast_to([P, GP, 2 * C]), ALU.mult))
                o2.link(dve.tensor_tensor(fx, fx, flw_b[:, :].unsqueeze(1).broadcast_to([P, GP, 2 * C]), ALU.mult))
                dve.tensor_tensor(fx, fx, flb_b[:, :].unsqueeze(1).broadcast_to([P, GP, 2 * C]), ALU.add)\
                    .then_inc(S_["row_done"], 1)

        @block.scalar
        def _(act):
            act.wait_ge(S_["squares"], 1)
            act.activation(stat[:, :], stat[:, :], ACT.Sqrt, bias=eps_col[:, 0:1], scale=1.0 / C).then_inc(S_["rooted"], 1)
            for g in range(NGP):
                act.wait_ge(S_["turned"], g + 1)
                if g:
                    act.wait_ge(S_["y_ready"], g)
                act.activation(xT[:, :], tp[:, :], ACT.Copy).then_inc(S_["x_ready"], 1)
                for i in range(3):
                    act.wait_ge(S_["m_ready"], 3 * g + i + 1)
                    act.activation(hT[i][:, :], hp[i][:, :], ACT.Relu, bias=bh[:, i:i + 1]).then_inc(S_["h_ready"], 1)
                act.wait_ge(S_["o_ready"], g + 1)
                if g:
                    act.wait_ge(S_["var2"], g)
                act.activation(sq[:, :, :].rearrange("p j c -> p (j c)"), op[:, :], ACT.Square).then_inc(S_["sq_ready"], 1)
                act.wait_ge(S_["var2"], g + 1)
                act.activation(ssq[:, :], ssq[:, :], ACT.Sqrt, bias=eps_col[:, 0:1], scale=1.0 / (2 * C)).then_inc(S_["std_ready"], 1)

        @block.tensor
        def _(pe):
            pe.wait_ge(S_["normed"], 1)
            for g in range(NGP):
                if g:
                    pe.wait_ge(S_["x_ready"], g)
                for q in range(4):
                    j = g * GP + 2 * q
                    mm = pe.transpose(tp[:, q * P:(q + 1) * P], x1[:, j:j + 2, :].rearrange("p j c -> p (j c)"), ident[:, :])
                mm.then_inc(S_["turned"], 1)
                pe.wait_ge(S_["x_ready"], g + 1)
                pe.matmul(hp[0][:, :], W[:, 0, :], xT[:, :], start=True, stop=True).then_inc(S_["m_ready"], 1)
                if g:
                    pe.wait_ge(S_["y_done"], g)
                for q in range(4):
                    mm = pe.matmul(yp[:, q * P:(q + 1) * P], xT[:, q * P:(q + 1) * P], WY[:, :], start=True, stop=True)
                mm.then_inc(S_["y_ready"], 1)
                for i in (1, 2):
                    pe.wait_ge(S_["h_ready"], 3 * g + i)
                    pe.matmul(hp[i][:, :], W[:, i, :], hT[i - 1][:, :], start=True, stop=True).then_inc(S_["m_ready"], 1)
                pe.wait_ge(S_["h_ready"], 3 * g + 3)
                if g:
                    pe.wait_ge(S_["row_done"], g)
                for bank in range(2):
                    pe.matmul(op[:, bank * 512:(bank + 1) * 512], ones[0:1, :], bo4[0:1, :, :].rearrange("p j c -> p (j c)"),
                              start=True, stop=False)
                    for q in range(2):
                        at = bank * 512 + q * 256
                        mm = pe.matmul(op[:, at:at + 256], hT[2][:, (2 * bank + q) * P:(2 * bank + q + 1) * P],
                                       WO[:, :, :].rearrange("p h c -> p (h c)"), start=False, stop=(q == 1))
                mm.then_inc(S_["o_ready"], 1)

        @block.gpsimd
        def _(pool):
            for g in range(NGP):
                pool.wait_ge(S_["y_done"], g + 1)
                for jj in range(real[g]):
                    pool.indirect_dma_start(B, bass.IndirectOffsetOnAxis(ap=start_idx[:, g * GP + jj:g * GP + jj + 1], axis=0),
                                            row[:, g % 2, jj, 2 * C:3 * C], None).then_inc(scattered[g % 2], 16)
            for b in range(2):
                pool.wait_ge(scattered[b], 16 * sum(real[b::2]))


def flux_pass(nc, T4, B, NV, S4, src_sb, keep, first_dst, run_end, ident, eps_col, aWh, abh, aWo, abo):
    Q = K // 2
    H = K * C // 512
    with semaphores(nc) as sem_, ExitStack() as ctx:
        sem = lambda name: sem_(f"flux_{name}")
        sb = lambda name, shape, dt=F32: ctx.enter_context(nc.sbuf_tensor(f"flux_{name}", shape, dt))
        ps = lambda name, shape: ctx.enter_context(nc.psum_tensor(f"flux_{name}", shape, F32))
        rows = sb("rows", [P, NB, K, ROW])
        idx = sb("idx", [P, NB, K], I32)
        nv = sb("nv", [P, NB, K, 2])
        yr = sb("yr", [P, 2, K, C])
        yc = sb("yc", [P, 2, C, K])
        kb = sb("kb", [P, K], BF16)
        kw = sb("kw", [P, 2, W4, K], BF16)
        h0 = sb("h0", [P, 2, K, C])
        kc = sb("kc", [P, 4, K])
        row_first = sb("row_first", [P, ROW])
        y_carry = sb("y_carry", [P, C])
        carry = sb("carry", [P, W4])
        hT = [sb(f"h{i + 1}", [P, Q * P]) for i in range(3)]
        sq = sb("sq", [P, K, C])
        ssq = sb("ssq", [P, K])
        f0 = sb("f0", [P, 2, K, C])
        run = sb("run", [P, 2, W4, K])
        row_out = sb("row_out", [P, 2, K, W4])
        W = sb("W", [P, 2, P])
        WO = sb("WO", [P, P])
        wo = sb("wo", [P, C])
        wmean = sb("wmean", [P, 1])
        bo = sb("bo", [P, C])
        bo8 = sb("bo8", [1, 8, C])
        ones = sb("ones", [1, P])
        bh = sb("bh", [P, 3])
        tp, mp = ps("tp", [P, Q * P]), ps("mp", [P, Q * P])
        mp2, zp = ps("mp2", [P, Q * P]), ps("zp", [P, Q * P])
        names = ("cleared loaded setup first fetched_first summed issued order_a order_b h0_ready turned h_ready "
                 "m_ready z_ready sq_ready ssq_ready std_ready fn_ready v_done z_used y_carried nrow_ready y_turned turned_out")
        S_ = {k: sem(k) for k in names.split()}
        ring = lambda name, n: [sem(f"{name}{b}") for b in range(n)]
        idx_ready, nv_ready, gathered = ring("idx_ready", NB), ring("nv_ready", NB), ring("gathered", NB)
        yr_ready, stored = ring("yr_ready", 2), ring("stored", 2)
        Bv = B[0:EP, :].rearrange("(p t) c -> p (t c)", p=P)
        S4v = S4.rearrange("(p t) c -> p (t c)", p=P)
        NVv = NV.rearrange("(p t) c -> p (t c)", p=P)
    
        n_loaded = 16 * (2 * (2 + 3 + 1) + 1)
        block = ctx.enter_context(nc.Block())

        @block.sync
        def _(sp):
            L = S_["loaded"]
            sp.wait_ge(S_["cleared"], 2)
            for half in range(2):
                r = slice(C * half, C * half + C)
                for i in range(2):
                    sp.dma_start(W[r, i, r], aWh[i + 1, :, :]).then_inc(L, 16)
                for i in range(3):
                    sp.dma_start(bh[r, i:i + 1], abh[i, :].rearrange("(c o) -> c o", o=1)).then_inc(L, 16)
                sp.dma_start(wo[r, :], aWo).then_inc(L, 16)
            sp.dma_start(bo[:, :], abo.partition_broadcast(P)).then_inc(L, 16)

            def store(c, b):
                sp.wait_ge(S_["turned_out"], c + 1)
                sp.dma_start(S4v[:, bass.ds(c * (K * W4), K * W4)],
                             row_out[:, b, :, :].rearrange("p k c -> p (k c)")).then_inc(stored[b], 16)

            def step(h):
                if not early(h, NB):
                    sp.wait_ge(S_["summed"], h.c - (NB - 1))
                sp.dma_start(idx[:, h.b, :], src_sb[:, bass.ds(h.c * K, K)]).then_inc(idx_ready[h.b], 16)
                sp.dma_start(nv[:, h.b, :, :].rearrange("p k c -> p (k c)"),
                             NVv[:, bass.ds(h.c * (2 * K), 2 * K)]).then_inc(nv_ready[h.b], 16)
                if not early(h, 2):
                    sp.wait_ge(S_["y_turned"], h.c - 1)
                sp.dma_start(yr[:, h.b2, :, :].rearrange("p k c -> p (k c)"),
                             Bv[:, bass.ds(h.c * (K * C), K * C)]).then_inc(yr_ready[h.b2], 16)
                if not early(h, 3):
                    store(h.c - 3, (h.b2 + 1) % 2)
            chunks(sp, step)
            for c in range(CH - 3, CH):
                store(c, c % 2)
            for b in range(2):
                sp.wait_ge(stored[b], 16 * len(range(b, CH, 2)))

        @block.gpsimd
        def _(pool):
            pool.indirect_dma_start(row_first[:, :], None, T4, bass.IndirectOffsetOnAxis(ap=first_dst[:, 0:1], axis=0))\
                .then_inc(S_["fetched_first"], 16)

            def step(h):
                pool.wait_ge(idx_ready[h.b], 16 * (h.turn + 1))
                if not early(h, NB):
                    pool.wait_ge(S_["v_done"], h.c - (NB - 1))
                pool.sem_inc(S_["issued"], 1)
                for k in range(K):
                    pool.indirect_dma_start(rows[:, h.b, k, :], None, T4,
                                            bass.IndirectOffsetOnAxis(ap=idx[:, h.b, k:k + 1], axis=0))\
                        .then_inc(gathered[h.b], 16)
            chunks(pool, step)

        @block.tensor
        def _(pe):
            pe.wait_ge(S_["setup"], 1)

            def step(h):
                pe.wait_ge(S_["h0_ready"], h.c + 1)
                if not early(h, 1):
                    pe.wait_ge(S_["h_ready"], h.c * 6 - 4)
                for q in range(Q):
                    mm = pe.transpose(tp[:, q * P:(q + 1) * P], h0[:, h.b2, 2 * q:2 * q + 2, :].rearrange("p k c -> p (k c)"),
                                      ident[:, :])
                    if q % 4 == 3:
                        mm.then_inc(S_["turned"], 1)
                for i, m in ((0, mp), (1, mp2)):
                    for half in range(H):
                        pe.wait_ge(S_["h_ready"], h.c * 6 + i * H + half + 1)
                        cols = slice(512 * half, 512 * half + 512)
                        pe.matmul(m[:, cols], W[:, i, :], hT[i][:, cols], start=True, stop=True).then_inc(S_["m_ready"], 1)
                if not early(h, 1):
                    pe.wait_ge(S_["z_used"], h.c)
                for half in range(H):
                    pe.wait_ge(S_["h_ready"], h.c * 6 + 2 * H + half + 1)
                    pe.matmul(zp[:, 512 * half:512 * half + 512], ones[0:1, :], bo8[0:1, :, :].rearrange("p j c -> p (j c)"),
                              start=True, stop=False)
                    for q in range(4):
                        cols = slice((4 * half + q) * P, (4 * half + q + 1) * P)
                        mm = pe.matmul(zp[:, cols], hT[2][:, cols], WO[:, :], start=False, stop=(q == 3))
                    mm.then_inc(S_["z_ready"], 1)
            chunks(pe, step)

        fx_of = lambda h: rows[:, h.b, :, 3 * C:5 * C].rearrange("p k (c d) -> p k c d", d=2)

        @block.scalar
        def _(act):
            act.wait_ge(S_["setup"], 1)

            def turn_y(h):
                act.wait_ge(yr_ready[h.b2], 16 * (h.turn2 + 1))
                if not early(h, 2):
                    act.wait_ge(S_["h0_ready"], h.c - 1)
                    act.wait_ge(S_["y_carried"], h.c - 1)
                act.activation(yc[:, h.b2, :, :].rearrange("p c k -> p k c"), yr[:, h.b2, :, :], ACT.Copy)\
                    .then_inc(S_["y_turned"], 1)

            def turn_sums(h):
                act.wait_ge(S_["summed"], h.c + 1)
                if not early(h, 2):
                    act.wait_ge(stored[h.b2], 16 * h.turn2)
                act.activation(row_out[:, h.b2, :, :], run[:, h.b2, :, :].rearrange("p c k -> p k c"), ACT.Copy)\
                    .then_inc(S_["turned_out"], 1)

            def layers(h):
                for i, p in enumerate((tp, mp, mp2)):
                    for half in range(H):
                        cols = slice(512 * half, 512 * half + 512)
                        if i == 0:
                            act.wait_ge(S_["turned"], h.c * H + half + 1)
                            if not early(h, 1):
                                act.wait_ge(S_["m_ready"], (h.c - 1) * 2 * H + half + 1)
                        else:
                            act.wait_ge(S_["m_ready"], h.c * 2 * H + (i - 1) * H + half + 1)
                            if i == 2 and not early(h, 1):
                                act.wait_ge(S_["z_ready"], (h.c - 1) * H + half + 1)
                        act.activation(hT[i][:, cols], p[:, cols], ACT.Relu, bias=bh[:, i:i + 1]).then_inc(S_["h_ready"], 1)
                    if i == 0:
                        act.wait_ge(gathered[h.b], 16 * K * (h.turn + 1))
                        act.wait_ge(nv_ready[h.b], 16 * (h.turn + 1))
                        if not early(h, 2):
                            act.wait_ge(S_["v_done"], h.c - 1)
                    if i < 2:
                        for k in range(i * K // 2, (i + 1) * K // 2):
                            a = act.activation(f0[:, h.b2, k, :], fx_of(h)[:, k, :, 0], ACT.Copy, scale=nv[:, h.b, k, 0:1])
                a.then_inc(S_["fn_ready"], 1)
                if not early(h, 1):
                    turn_sums(h.before())
                act.wait_ge(S_["z_ready"], (h.c + 1) * H)
                if not early(h, 1):
                    act.wait_ge(S_["v_done"], h.c)
                act.activation(sq[:, :, :].rearrange("p k c -> p (k c)"), zp[:, :], ACT.Square).then_inc(S_["sq_ready"], 1)
                act.activation(run[:, h.b2, 2 * C:W4, :].rearrange("p c k -> p k c"), nv[:, h.b, :, :], ACT.Copy)\
                    .then_inc(S_["nrow_ready"], 1)
                act.wait_ge(S_["ssq_ready"], h.c + 1)
                act.activation(ssq[:, :], ssq[:, :], ACT.Sqrt, bias=eps_col[:, 0:1], scale=1.0 / C).then_inc(S_["std_ready"], 1)

            def step(h):
                turn_y(h)
                if not early(h, 1):
                    layers(h.before())
            chunks(act, step)
            layers(Chunk(0, CH - 1))
            turn_sums(Chunk(0, CH - 1))

        A_STEPS = 5
        B_STEPS = 7

        @block.vector
        def _(dve):
            o = Chain(dve, S_["order_a"])
            dve.memset(W[:, :, :], 0.0).then_inc(S_["cleared"], 1)
            dve.memset(WO[:, :], 0.0).then_inc(S_["cleared"], 1)
            o.link(dve.memset(ones[:, :], 1.0))
            o.link(dve.memset(carry[:, :], 0.0))
            o.link(dve.memset(kb[:, :], 0.0))
            dve.wait_ge(S_["loaded"], n_loaded)
            for t in (wo, bo):
                o.link(dve.tensor_reduce(wmean[:, :], t[:, :], AX, ALU.add))
                o.link(dve.tensor_scalar(wmean[:, :], wmean[:, :], 1.0 / C, None, ALU.mult))
                o.link(dve.tensor_scalar(t[:, :], t[:, :], wmean[:, 0:1], None, ALU.subtract))
            for half in range(2):
                r = slice(C * half, C * half + C)
                o.link(dve.tensor_copy(WO[r, r], wo[r, :]))
            o.link(dve.tensor_copy(bo8[0:1, :, :], bo[0:1, :].unsqueeze(1).broadcast_to([1, 8, C])))
            dve.sem_inc(S_["setup"], 1)
            base = o.n

            def spread(h):
                o.at(h.c * A_STEPS + base)
                y = yc[:, h.b2, :, :]
                o.link(dve.tensor_copy(kc[:, h.b, :], keep[:, bass.ds(h.c * K, K)]))
                o.link(dve.tensor_copy(kb[:, 1:K], kc[:, h.b, 1:K]))
                o.link(dve.tensor_copy(kw[:, h.b2, :, :], kb[:, :].unsqueeze(1).broadcast_to([P, W4, K])))
                dve.wait_ge(S_["y_turned"], h.c + 1)
                if early(h, 1):
                    dve.wait_ge(S_["fetched_first"], 16)
                    o.link(dve.tensor_copy(y[:, :, 0], row_first[:, 2 * C:3 * C]))
                else:
                    dve.wait_ge(S_["y_carried"], h.c)
                    o.link(dve.scalar_tensor_tensor(y[:, :, 0], y_carry[:, :], kc[:, h.b, 0:1], y[:, :, 0], ALU.mult, ALU.add))
                flat = y.rearrange("p c k -> p (c k)")
                o.link(dve.tensor_tensor_scan(flat, kw[:, h.b2, 0:C, :].rearrange("p c k -> p (c k)"), flat,
                                              0.0, ALU.mult, ALU.add))
                dve.tensor_copy(y_carry[:, :], y[:, :, K - 1]).then_inc(S_["y_carried"], 1)
                dve.wait_ge(gathered[h.b], 16 * K * (h.turn + 1))
                if not early(h, 2):
                    dve.wait_ge(S_["turned"], (h.c - 1) * H)
                dve.tensor_tensor(h0[:, h.b2, :, :], rows[:, h.b, :, 2 * C:3 * C], y.rearrange("p c k -> p k c"), ALU.add)\
                    .then_inc(S_["h0_ready"], 1)

            ob = Chain(dve, S_["order_b"])

            def combine(h):
                ob.at(h.c * B_STEPS)
                by_edge = run[:, h.b2, :, :].rearrange("p c k -> p k c")
                a, v, f = by_edge[:, :, C:2 * C], by_edge[:, :, 0:C], f0[:, h.b2, :, :]
                dve.wait_ge(gathered[h.b], 16 * K * (h.turn + 1))
                dve.wait_ge(nv_ready[h.b], 16 * (h.turn + 1))
                f1 = fx_of(h)[:, :, :, 1]
                ob.link(dve.tensor_tensor(f1, f1,
                                          nv[:, h.b, :, 1:2].broadcast_to([P, K, C]), ALU.mult))
                ob.link(dve.tensor_tensor(f1, f1, rows[:, h.b, :, C:2 * C], ALU.subtract))
                dve.wait_ge(S_["sq_ready"], h.c + 1)
                dve.tensor_reduce(ssq[:, :], sq[:, :, :], AX, ALU.add).then_inc(S_["ssq_ready"], 1)
                dve.wait_ge(S_["fn_ready"], h.c + 1)
                ob.link(dve.tensor_tensor(f, f, f1, ALU.add))
                dve.wait_ge(S_["std_ready"], h.c + 1)
                ob.link(dve.reciprocal(ssq[:, :], ssq[:, :]))
                if not early(h, 2):
                    dve.wait_ge(S_["turned_out"], h.c - 1)
                dve.tensor_tensor(a, zp[:, :].rearrange("p (k c) -> p k c", c=C),
                                  ssq[:, :].unsqueeze(2).broadcast_to([P, K, C]), ALU.mult).then_inc(S_["z_used"], 1)
                dve.wait_ge(S_["z_used"], h.c + 1)
                ob.link(dve.tensor_tensor(sq[:, :, :], a, rows[:, h.b, :, 0:C], ALU.mult))
                dve.tensor_tensor(v, f, sq[:, :, :], ALU.subtract).then_inc(S_["v_done"], 1)
                dve.wait_ge(S_["v_done"], h.c + 1)
                dve.wait_ge(S_["nrow_ready"], h.c + 1)
                if not early(h, 1):
                    dve.wait_ge(S_["summed"], h.c)
                first = run[:, h.b2, :, 0]
                ob.link(dve.scalar_tensor_tensor(first, carry[:, :], kc[:, h.b, 0:1], first, ALU.mult, ALU.add))
                flat = run[:, h.b2, :, :].rearrange("p c k -> p (c k)")
                ob.link(dve.tensor_tensor_scan(flat, kw[:, h.b2, :, :].rearrange("p c k -> p (c k)"), flat,
                                               0.0, ALU.mult, ALU.add))
                dve.tensor_copy(carry[:, :], run[:, h.b2, :, K - 1]).then_inc(S_["summed"], 1)

            def step(h):
                spread(h)
                if not early(h, 1):
                    combine(h.before())
            chunks(dve, step)
            combine(Chunk(0, CH - 1))
            dve.wait_ge(S_["summed"], CH)
            ob.at(CH * B_STEPS)
            ob.link(dve.tensor_copy(run_end[:, :], carry[:, :]))


def final(nc, S4, T4, X1, out, run_end, carried, ident, goes_on, passes, ends_here, lead_idx, end_idx,
          has, cnt, eps_col, alw, alb):
    with semaphores(nc) as sem_, ExitStack() as ctx:
        sem = lambda name: sem_(f"fin_{name}")
        sb = lambda name, shape, dt=F32: ctx.enter_context(nc.sbuf_tensor(f"fin_{name}", shape, dt))
        sums = sb("sums", [P, 2, JG, W4])
        own = sb("own", [P, 2, JG, 2 * C])
        x1 = sb("x1", [P, 2, JG, C])
        sq, am = sb("sq", [P, JG, C]), sb("am", [P, JG, C])
        stat, mean = sb("stat", [P, JG]), sb("mean", [P, JG])
        res = sb("res", [P, J, C])
        alw_b, alb_b = sb("alw", [P, C]), sb("alb", [P, C])
        mended, order, loaded, squares, rooted, used, done, stored = (
            sem(n) for n in ("mended", "order", "loaded", "squares", "rooted", "used", "done", "stored"))
        fetched = [sem(f"fetched{b}") for b in range(2)]
        brought = [sem(f"brought{b}") for b in range(2)]
        block = ctx.enter_context(nc.Block())
        pe_part, dve_part, pool_part = mend(nc, sem_, ctx, "fin", S4, W4, run_end, carried, ident, goes_on,
                                            passes, ends_here, lead_idx, mended)

        @block.tensor
        def _(pe):
            pe_part(pe)

        @block.gpsimd
        def _(pool):
            pool_part(pool)
            for g in range(NG):
                if g >= 2:
                    pool.wait_ge(used, g - 1)
                for jj in range(JG):
                    pool.indirect_dma_start(sums[:, g % 2, jj, :], None, S4,
                                            bass.IndirectOffsetOnAxis(ap=end_idx[:, g * JG + jj:g * JG + jj + 1], axis=0))\
                        .then_inc(fetched[g % 2], 16)

        @block.sync
        def _(sp):
            sp.dma_start(alw_b[:, :], alw.partition_broadcast(P)).then_inc(loaded, 16)
            sp.dma_start(alb_b[:, :], alb.partition_broadcast(P)).then_inc(loaded, 16)
            for g in range(NG):
                if g >= 2:
                    sp.wait_ge(used, g - 1)
                js = slice(g * JG, (g + 1) * JG)
                sp.dma_start(own[:, g % 2, :, :], T4.rearrange("(j p) c -> p j c", p=P)[:, js, 3 * C:5 * C]).then_inc(brought[g % 2], 16)
                sp.dma_start(x1[:, g % 2, :, :], X1.rearrange("(j p) c -> p j c", p=P)[:, js, :]).then_inc(brought[g % 2], 16)
            sp.wait_ge(done, 1)
            sp.dma_start(out[0:(J - 1) * P, :].rearrange("(j p) c -> p j c", p=P), res[:, 0:J - 1, :]).then_inc(stored, 16)
            sp.dma_start(out[(J - 1) * P:N, :], res[0:N_LAST, J - 1, :]).then_inc(stored, 16)
            sp.wait_ge(stored, 32)

        @block.scalar
        def _(act):
            for g in range(NG):
                act.wait_ge(squares, g + 1)
                act.activation(stat[:, :], stat[:, :], ACT.Sqrt, bias=eps_col[:, 0:1], scale=1.0 / C).then_inc(rooted, 1)

        @block.vector
        def _(dve):
            dve_part(dve)
            o = Chain(dve, order)
            dve.wait_ge(loaded, 32)
            for g in range(NG):
                b, js = g % 2, slice(g * JG, (g + 1) * JG)
                dve.wait_ge(fetched[b], 16 * JG * (g // 2 + 1))
                dve.wait_ge(brought[b], 32 * (g // 2 + 1))
                sm, ow, xg, h = sums[:, b, :, :], own[:, b, :, :], x1[:, b, :, :], res[:, js, :]
                wide = lambda col, n: col.unsqueeze(2).broadcast_to([P, JG, n])
                each = lambda rw: rw.unsqueeze(1).broadcast_to([P, JG, C])
                o.link(dve.tensor_tensor(sm, sm, wide(has[:, js], W4), ALU.mult))
                ow4 = ow.rearrange("p j (c d) -> p j c d", d=2)
                o.link(dve.tensor_tensor(ow4, ow4, sm[:, :, 2 * C:W4].unsqueeze(2).broadcast_to([P, JG, C, 2]), ALU.mult))
                o.link(dve.tensor_tensor(h, ow4[:, :, :, 0], ow4[:, :, :, 1], ALU.add))
                o.link(dve.tensor_tensor(h, h, sm[:, :, 0:C], ALU.add))
                o.link(dve.tensor_tensor(am[:, :, :], sm[:, :, C:2 * C], each(alw_b[:, :]), ALU.mult))
                o.link(dve.tensor_tensor(sq[:, :, :], wide(cnt[:, js], C), each(alb_b[:, :]), ALU.mult))
                o.link(dve.tensor_tensor(am[:, :, :], am[:, :, :], sq[:, :, :], ALU.add))
                o.link(dve.scalar_tensor_tensor(am[:, :, :], am[:, :, :], 4.0, xg, ALU.add, ALU.mult))
                o.link(dve.tensor_tensor(h, h, am[:, :, :], ALU.add))
                o.link(dve.tensor_scalar(h, h, 0.5, None, ALU.mult))
                dve.sem_inc(used, 1)

                def root():
                    dve.sem_inc(squares, 1)
                    dve.wait_ge(rooted, g + 1)
                layer_norm(o, dve, h, sq[:, :, :], stat[:, :], mean[:, :], eps_col, root, C)
            dve.sem_inc(done, 1)


_INS = ["x", "src", "dst", "edge_attr_2"] + [f"L1_gnn_{n}" for n in (
    "flux_Wh", "flux_bh", "flux_Wo", "flux_bo", "flux_ln_w", "flux_ln_b",
    "a_Wh", "a_bh", "a_Wo", "a_bo", "a_ln_w", "a_ln_b")]


def kernel(**inputs):
    import numpy as _np
    import concourse.bacc as _bacc
    from concourse import mybir as _mybir
    from concourse.bass_utils import run_bass_kernel_spmd as _run

    nc = _bacc.Bacc("TRN2", target_bir_lowering=False, num_devices=1)
    arrays, args = {}, []
    for name in _INS:
        a = _np.ascontiguousarray(inputs[name])
        arrays[f"in_{name}"] = a
        args.append(nc.dram_tensor(f"in_{name}", a.shape, _mybir.dt.from_np(a.dtype), kind="ExternalInput").ap())
    args.append(nc.dram_tensor("out_0", (N, C), F32, kind="ExternalOutput").ap())
    build_program(nc, *args)
    r = _run(nc, [arrays], core_ids=[0])
    return r.results[0]["out_0"]
```

```python
from contextlib import ExitStack, contextmanager

import concourse.bass as bass
import concourse.mybir as mybir

F32 = mybir.dt.float32
BF16 = mybir.dt.bfloat16
I32 = mybir.dt.int32
U8 = mybir.dt.uint8
FP8 = mybir.dt.float8e4
ALU = mybir.AluOpType
ACT = mybir.ActivationFunctionType
AX = mybir.AxisListType.X

P = 128
N = 12500
E = 412500
C = 64
K = 16
NB = 4
CH = -(-E // (P * K))
T = CH * K
EP = P * T
J = -(-N // P)
NP = P * J
SLOTS = 64
BLK = 32
NBLK = T // BLK
NEAR = 7
MANY = 4
PAIRS = J // 2
GN = 8
STEPS = P // GN
VALS = P + J
AROW = J * P
E_LAST = E - (P - 1) * T
N_LAST = N - (J - 1) * P
W4 = 2 * C + 2
ROW = 5 * C
JG = 14
NG = J // JG
GP = 8
PADP = max(p for p in range(1, P + 1) if 2 * (EP - E) % p == 0)
EPS = 1e-5
PAD_DST = 128 * P - 1
assert J % JG == 0 and CH > NB and P == 128 and J < P and T % BLK == 0 and 2 * SLOTS == P and JG % 2 == 0
CLEARS = 64
Z = T * C // CLEARS


class Chunk:

    def __init__(self, r, place, ring=NB):
        self.r, self.place, self.ring = r, place, ring
        self.c = r * ring + place
        self.b, self.b2 = place % ring, place % 2
        self.turn = r + place // ring
        self.turn2 = r * (ring // 2) + place // 2

    def before(self):
        return Chunk(self.r, self.place - 1, self.ring)


def chunks(eng, body, total=CH, ring=NB):
    peel = ring + (total - ring) % ring
    for c in range(peel):
        body(Chunk(0, c, ring))
    with eng.Fori(0, (total - peel) // ring) as r:
        for j in range(ring):
            body(Chunk(r, peel + j, ring))


def early(h, n):
    return isinstance(h.c, int) and h.c < n


@contextmanager
def semaphores(nc):
    held = []

    def sem(name):
        held.append(nc.alloc_semaphore(name))
        return held[-1]
    yield sem
    nc.clear_and_free_semaphores(held)
    nc.all_engine_barrier()


class Chain:

    def __init__(self, eng, sem):
        self.eng, self.sem, self.base, self.n = eng, sem, 0, 0

    def link(self, ins):
        self.n += 1
        ins.then_inc(self.sem, 1)
        self.eng.wait_ge(self.sem, self.base + self.n)

    def at(self, base):
        self.base, self.n = base, 0


def build_program(nc, x, src, dst, nvec, fWh, fbh, fWo, fbo, flw, flb, aWh, abh, aWo, abo, alw, alb, out):
    scratch = lambda name, shape, dt=F32: nc.dram_tensor(name, shape, dt).ap()
    X = scratch("x_layer", (NP, C))
    XP = scratch("x_parts", (P, J * 3 * C), BF16)
    X1 = scratch("x_mid", (NP, C))
    S = scratch("running", (EP, C))
    S4 = scratch("running_flux", (EP, W4))
    B = scratch("first_rows", (EP + NP, C))
    T4 = scratch("table", (NP, ROW))
    NV = scratch("nvec_padded", (EP, 2))
    A = scratch("adjacency", (J * P, AROW), U8)
    FIRST = scratch("block_firsts", (P, NBLK))
    DST = scratch("dst_padded", (EP,))
    SRC2 = scratch("src_split", (EP, 2), BF16)
    SLOT = scratch("slots", (P, PAIRS * 2 * P), BF16)

    top = ExitStack()
    with top:
        sb = lambda name, shape, dt=F32: top.enter_context(nc.sbuf_tensor(name, shape, dt))
        src_sb = sb("src_sb", [P, T], I32)
        keep = sb("keep", [P, T])
        ident = sb("ident", [P, P])
        eps_col = sb("eps_col", [P, 1])
        end_idx = sb("end_idx", [P, J], I32)
        start_idx = sb("start_idx", [P, J], I32)
        has = sb("has", [P, J])
        cnt = sb("cnt", [P, J])
        rcnt = sb("rcnt", [P, J])
        beyond = sb("beyond", [P, 1], I32)
        first_dst = sb("first_dst", [P, 1], I32)
        lead_idx = sb("lead_idx", [P, 1], I32)
        goes_on = sb("goes_on", [P, P])
        passes = sb("passes", [P, P])
        ends_here = sb("ends_here", [P, P])
        run_end = sb("run_end", [P, W4])
        carried = sb("carried", [P, W4])
        ones = sb("ones", [P, P])

        b_zero = nc.alloc_semaphore("b_zero")
        front = ExitStack()
        zeros = front.enter_context(nc.sbuf_tensor("zeros", [P, Z], F32))
        with ExitStack() as ctx:
            sb = lambda name, shape, dt=F32: ctx.enter_context(nc.sbuf_tensor(name, shape, dt))
            src_f = sb("src_f", [P, NEAR + T])
            first_row = sb("first_row", [P, 2 * P])
            prepare(nc, src, dst, nvec, NV, FIRST, DST, SRC2, src_sb, src_f, keep, ident, eps_col, first_dst,
                    lead_idx, goes_on, passes, ends_here, ones, first_row, zeros)
            find_nodes(nc, x, XP, B, b_zero, zeros, FIRST, DST, SRC2, SLOT, src_f, first_row, ident, ones, cnt, has, rcnt, end_idx,
                       start_idx, beyond)
        build_matrix(nc, SLOT, A, B, b_zero, zeros)
        nc.clear_and_free_semaphores([b_zero])
        nc.all_engine_barrier()
        front.close()

        middle = ExitStack()
        x3 = middle.enter_context(nc.sbuf_tensor("x3", [P, J, C], F32))
        general = nc.values_load(beyond[0:1, 0:1], min_val=0, max_val=2 * P)
        with nc.If(general == 0):
            nc.all_engine_barrier()
            dense_layers(nc, A, XP, x3, rcnt)
            nc.all_engine_barrier()
        with nc.Else():
            nc.all_engine_barrier()
            for layer, table in ((1, x), (2, X), (3, X)):
                gcn_pass(nc, f"l{layer}", table, src_sb, keep, S, run_end)
                node_sums(nc, f"n{layer}", S, X, run_end, carried, ident, goes_on, passes, ends_here,
                          lead_idx, end_idx, rcnt)
            bring(nc, X, x3)
            nc.all_engine_barrier()
        node_mlps(nc, x, x3, X1, T4, B, start_idx, eps_col, ident, fWh, fbh, fWo, fbo, flw, flb,
                  aWh, alw, alb)
        middle.close()
        flux_pass(nc, T4, B, NV, S4, src_sb, keep, first_dst, run_end, ident, eps_col,
                  aWh, abh, aWo, abo)
        final(nc, S4, T4, X1, out, run_end, carried, ident, goes_on, passes, ends_here, lead_idx,
              end_idx, has, cnt, eps_col, alw, alb)


def prepare(nc, src, dst, nvec, NV, FIRST, DST, SRC2, src_sb, src_f, keep, ident, eps_col, first_dst,
            lead_idx, goes_on, passes, ends_here, ones, first_row, zeros):
    with semaphores(nc) as sem_, ExitStack() as ctx:
        sem = lambda name: sem_(f"prep_{name}")
        sb = lambda name, shape, dt=F32: ctx.enter_context(nc.sbuf_tensor(f"prep_{name}", shape, dt))
        wide_src = sb("wide_src", [P, NEAR + T], I32)
        dst_i = sb("dst_i", [P, T], I32)
        dst_f, col = sb("dst_f", [P, T]), sb("col", [P, T])
        low = sb("low", [P, T], I32)
        firsts = sb("firsts", [P, NBLK])
        split = sb("split", [P, T, 2], BF16)
        part_row = sb("part_row", [P, 1])
        lead = sb("lead", [P, 1])
        diag = sb("diag", [P, 2 * P])
        one_part = sb("one_part", [P, P])
        rows_ps = ctx.enter_context(nc.psum_tensor("rows_ps", [P, 2 * P], F32))
        cleared, zeroed, loaded, consts, order, pool_order = (
            sem(n) for n in ("cleared", "zeroed", "loaded", "consts", "order", "pool_order"))
        diag_ready, rows_seen, nv_done, tables, written = (
            sem(n) for n in ("diag_ready", "rows_seen", "nv_done", "tables", "written"))
        mid = slice(NEAR, NEAR + T)
        block = ctx.enter_context(nc.Block())

        @block.sync
        def _(sp):
            sp.wait_ge(cleared, 3)
            for own, e in ((dst_i[:, :], dst), (wide_src[:, mid], src)):
                sp.dma_start(own[0:P - 1, :], e[0:(P - 1) * T].rearrange("(p t) -> p t", p=P - 1)).then_inc(loaded, 16)
                sp.dma_start(own[P - 1:P, 0:E_LAST], e[(P - 1) * T:E].rearrange("(p t) -> p t", p=1)).then_inc(loaded, 16)
            sp.dma_start(wide_src[1:P, 0:NEAR], src[0:(P - 1) * T].rearrange("(p t) -> p t", p=P - 1)[:, T - NEAR:T]).then_inc(loaded, 16)
            sp.wait_ge(tables, 1)
            sp.dma_start(DST.rearrange("(p t) -> p t", p=P), dst_f[:, :]).then_inc(written, 16)
            sp.wait_ge(tables, 2)
            sp.dma_start(FIRST, firsts[:, :]).then_inc(written, 16)
            sp.wait_ge(tables, 4)
            sp.dma_start(SRC2.rearrange("(p t) c -> p (t c)", p=P), split[:, :, :].rearrange("p t c -> p (t c)")).then_inc(written, 16)
            sp.wait_ge(written, 48)

        @block.scalar
        def _(act):
            act.dma_start(NV[0:E, :], nvec[:, :]).then_inc(nv_done, 16)
            act.wait_ge(zeroed, 1)
            act.dma_start(NV[E:EP, :].rearrange("t c -> (t c)").rearrange("(p t) -> p t", p=PADP),
                          zeros[0:PADP, 0:2 * (EP - E) // PADP]).then_inc(nv_done, 16)
            act.wait_ge(nv_done, 32)

        @block.gpsimd
        def _(pool):
            o = Chain(pool, pool_order)
            pool.memset(zeros[:, :], 0.0).then_inc(zeroed, 1)
            o.link(pool.memset(ident[:, :], 0.0))
            pool.memset(ones[:, :], 1.0).then_inc(consts, 1)
            pool.affine_select(out=ident[:, :], in_=ident[:, :], compare_op=ALU.not_equal, fill=1.0,
                               base=0, pattern=[[-1, P]], channel_multiplier=1).then_inc(consts, 1)
            pool.iota(part_row[:, :], pattern=[[1, 1]], base=0, channel_multiplier=T,
                      allow_small_or_imprecise_dtypes=True).then_inc(consts, 1)
            pool.iota(col[:, :], pattern=[[1, T]], base=0, channel_multiplier=0,
                      allow_small_or_imprecise_dtypes=True).then_inc(consts, 1)

        @block.tensor
        def _(pe):
            pe.wait_ge(consts, 4)
            pe.wait_ge(diag_ready, 2)
            pe.matmul(rows_ps[:, :], ones[:, :], diag[:, :], start=True, stop=True).then_inc(rows_seen, 1)

        @block.vector
        def _(dve):
            o = Chain(dve, order)
            dve.memset(dst_i[:, :], PAD_DST).then_inc(cleared, 1)
            dve.memset(wide_src[:, mid], 0).then_inc(cleared, 1)
            dve.memset(wide_src[:, 0:NEAR], -1).then_inc(cleared, 1)
            dve.memset(eps_col[:, :], EPS)
            dve.memset(keep[:, 0:1], 0.0)
            dve.memset(goes_on[:, 0:1], 0.0)
            dve.memset(passes[:, 0:1], 0.0)
            dve.memset(ends_here[:, P - 1:P], 1.0)
            dve.wait_ge(loaded, 80)
            dve.tensor_copy(dst_f[:, :], dst_i[:, :]).then_inc(tables, 1)
            dve.wait_ge(tables, 1)
            dve.tensor_copy(firsts[:, :], dst_f[:, :].rearrange("p (b e) -> p b e", e=BLK)[:, :, 0]).then_inc(tables, 1)
            dve.wait_ge(consts, 4)
            dve.tensor_scalar(diag[:, 0:P], ident[:, :], dst_f[:, 0:1], None, ALU.mult).then_inc(diag_ready, 1)
            dve.tensor_scalar(diag[:, P:2 * P], ident[:, :], dst_f[:, T - 1:T], None, ALU.mult).then_inc(diag_ready, 1)
            o.link(dve.tensor_scalar(low[:, :], wide_src[:, mid], P - 1, None, ALU.bitwise_and))
            dve.tensor_copy(split[:, :, 0], low[:, :]).then_inc(tables, 1)
            dve.wait_ge(tables, 3)
            o.link(dve.tensor_scalar(low[:, :], wide_src[:, mid], 7, None, ALU.logical_shift_right))
            dve.tensor_copy(split[:, :, 1], low[:, :]).then_inc(tables, 1)
            dve.tensor_copy(src_sb[:, :], wide_src[:, mid])
            dve.tensor_tensor(keep[:, 1:T], dst_f[:, 1:T], dst_f[:, 0:T - 1], ALU.is_equal)
            dve.tensor_copy(first_dst[:, :], dst_i[:, 0:1])
            o.link(dve.tensor_copy(src_f[:, :], wide_src[:, :]))
            o.link(dve.scalar_tensor_tensor(col[:, :], dst_f[:, :], float(NP), col[:, :], ALU.is_ge, ALU.mult))
            o.link(dve.tensor_tensor(src_f[:, mid], src_f[:, mid], col[:, :], ALU.add))
            o.link(dve.tensor_scalar(col[:, :], dst_f[:, :], dst_f[:, 0:1], None, ALU.is_equal))
            o.link(dve.tensor_reduce(lead[:, :], col[:, :], AX, ALU.add))
            o.link(dve.tensor_scalar(lead[:, :], lead[:, :], part_row[:, 0:1], -1.0, ALU.add, ALU.add))
            dve.tensor_copy(lead_idx[:, :], lead[:, :])
            dve.wait_ge(rows_seen, 1)
            o.link(dve.tensor_copy(first_row[:, :], rows_ps[:, :]))
            fr, lr = first_row[:, 0:P], first_row[:, P:2 * P]
            o.link(dve.tensor_tensor(one_part[:, :], fr, lr, ALU.is_equal))
            o.link(dve.tensor_tensor(goes_on[:, 1:P], fr[:, 1:P], lr[:, 0:P - 1], ALU.is_equal))
            o.link(dve.tensor_tensor(passes[:, 1:P], goes_on[:, 1:P], one_part[:, 0:P - 1], ALU.mult))
            o.link(dve.tensor_scalar(ends_here[:, 0:P - 1], passes[:, 1:P], -1.0, 1.0, ALU.mult, ALU.add))


def find_nodes(nc, x, XP, B, b_zero, zeros, FIRST, DST, SRC2, SLOT, src_f, first_row, ident, ones, cnt, has, rcnt, end_idx,
               start_idx, beyond):
    with semaphores(nc) as sem_, ExitStack() as ctx:
        sem = lambda name: sem_(f"find_{name}")
        sb = lambda name, shape, dt=F32: ctx.enter_context(nc.sbuf_tensor(f"find_{name}", shape, dt))
        node_id, start, at = sb("node_id", [P, J]), sb("start", [P, J + 1]), sb("at", [P, J])
        slot_id = sb("slot_id", [P, SLOTS])
        idx = [sb(f"idx{i}", [P, J], I32) for i in range(3)]
        less = sb("less", [P, JG, P])
        less2 = sb("less2", [P, JG, P])
        firsts, near = sb("firsts", [P, J, NBLK]), sb("near", [P, J, BLK])
        picked = sb("picked", [P, J, SLOTS, 2], BF16)
        mask = sb("mask", [P, JG, SLOTS], BF16)
        down, wrap = sb("down", [P, P]), sb("wrap", [P, P])
        ident_bf = sb("ident_bf", [P, P], BF16)
        turned_sb = sb("turned_sb", [P, PAIRS, 2, P], BF16)
        hits, most, t, u, end = sb("hits", [P, NBLK]), sb("most", [P, 1]), sb("t", [P, J]), sb("u", [P, J]), sb("end", [P, J])
        big = sb("big", [P, 1])
        real = sb("real", [P, 1])
        x0 = sb("x0", [P, 2, JG, C])
        both = sb("both", [P, 2 * T], BF16)
        xp = both[:, 0:2 * JG * 3 * C].rearrange("p (b j c) -> p b j c", b=2, j=JG)
        same, same_sum = both[:, 0:T], both[:, T:2 * T]
        end_ps, any_ps = (ctx.enter_context(nc.psum_tensor(n, [P, J], F32)) for n in ("end_ps", "any_ps"))
        turned_ps = [ctx.enter_context(nc.psum_tensor(f"turned_ps{i}", [P, 2, P], F32)) for i in range(2)]
        consts, order, pool_order, starts, ends, asked, told, masked, turned, taken, slots_out = (
            sem(n) for n in ("consts", "order", "pool_order", "starts", "ends", "asked", "told", "masked",
                             "turned", "taken", "slots_out"))
        x_in, x_out = ([sem(f"{n}{b}") for b in range(2)] for n in ("x_in", "x_out"))
        x_clear, x_split = sem("x_clear"), sem("x_split")
        found = [sem(f"found{i}") for i in range(3)]
        fetched = [[sem(f"fetched{i}_{g}") for g in range(NG)] for i in range(3)]
        block = ctx.enter_context(nc.Block())

        @block.gpsimd
        def _(pool):
            o = Chain(pool, pool_order)
            pool.iota(node_id[:, :], pattern=[[P, J]], base=0, channel_multiplier=1,
                      allow_small_or_imprecise_dtypes=True).then_inc(consts, 1)
            pool.iota(slot_id[:, :], pattern=[[1, SLOTS]], base=0, channel_multiplier=0,
                      allow_small_or_imprecise_dtypes=True).then_inc(consts, 1)
            o.link(pool.memset(down[:, :], 0.0))
            o.link(pool.memset(wrap[:, :], 0.0))
            pool.affine_select(out=down[:, :], in_=down[:, :], compare_op=ALU.not_equal, fill=1.0,
                               base=-1, pattern=[[-1, P]], channel_multiplier=1).then_inc(consts, 1)
            pool.memset(wrap[0:1, P - 1:P], 1.0).then_inc(consts, 1)
            views = (FIRST, DST.rearrange("(e o) -> e o", o=1), SRC2)
            for i, (table, rows) in enumerate(zip(views, (firsts, near, picked))):
                for g in range(NG):
                    pool.wait_ge(found[i], g + 1)
                    for j in range(g * JG, (g + 1) * JG):
                        into = rows[:, j, :] if i < 2 else rows[:, j, :, :].rearrange("p s c -> p (s c)")
                        pool.indirect_dma_start(into, None, table,
                                                bass.IndirectOffsetOnAxis(ap=idx[i][:, j:j + 1], axis=0))\
                            .then_inc(fetched[i][g], 16)

        @block.tensor
        def _(pe):
            pe.wait_ge(consts, 4)
            pe.wait_ge(starts, 1)
            pe.matmul(end_ps[:, :], down[:, :], start[:, 0:J], start=True, stop=False)
            pe.matmul(end_ps[:, :], wrap[:, :], start[:, 1:J + 1], start=False, stop=True).then_inc(ends, 1)
            pe.wait_ge(asked, 1)
            pe.matmul(any_ps[:, 0:1], ones[:, :], big[:, :], start=True, stop=True).then_inc(told, 1)
            for q in range(PAIRS):
                pe.wait_ge(masked, 2 * q // JG + 1)
                if q >= 2:
                    pe.wait_ge(taken, q - 1)
                for i in range(2):
                    mm = pe.matmul(turned_ps[q % 2][:, i, :], picked[:, 2 * q:2 * q + 2, :, i].rearrange("p j s -> p (j s)"),
                                   ident_bf[:, :], start=True, stop=True)
                mm.then_inc(turned, 1)

        @block.scalar
        def _(act):
            for q in range(PAIRS):
                act.wait_ge(turned, q + 1)
                act.activation(turned_sb[:, q, :, :], turned_ps[q % 2][:, :, :], ACT.Copy).then_inc(taken, 1)

        @block.sync
        def _(sp):
            def load(g):
                if g >= 2:
                    sp.wait_ge(x_split, g - 1)
                elif g == 0:
                    sp.wait_ge(x_clear, 1)
                whole = min(JG, J - 1 - g * JG)
                sp.dma_start(x0[:, g % 2, 0:whole, :],
                             x[g * JG * P:(g * JG + whole) * P, :].rearrange("(j p) c -> p j c", p=P)).then_inc(x_in[g % 2], 16)
                if whole < JG:
                    sp.dma_start(x0[0:N_LAST, g % 2, JG - 1, :], x[(J - 1) * P:N, :]).then_inc(x_in[g % 2], 16)

            for g in range(NG + 1):
                if g < NG:
                    load(g)
                if g:
                    sp.wait_ge(x_split, g)
                    sp.dma_start(XP[:, (g - 1) * JG * 3 * C:g * JG * 3 * C],
                                 xp[:, (g - 1) % 2, :, :].rearrange("p j c -> p (j c)")).then_inc(x_out[(g - 1) % 2], 16)
            for b in range(2):
                sp.wait_ge(x_out[b], 16 * len(range(b, NG, 2)))
            for z in range(CLEARS - PAIRS):
                sp.dma_start(B[0:EP, :].rearrange("(p t) c -> p (t c)", p=P)[:, z * Z:(z + 1) * Z], zeros[:, :]).then_inc(b_zero, 16)
            sp.wait_ge(taken, PAIRS)
            sp.dma_start(SLOT, turned_sb[:, :, :, :].rearrange("p q i n -> p (q i n)")).then_inc(slots_out, 16)
            sp.wait_ge(slots_out, 16)

        @block.vector
        def _(dve):
            o = Chain(dve, order)
            dve.wait_ge(consts, 4)
            o.link(dve.tensor_copy(ident_bf[:, :], ident[:, :]))
            o.link(dve.memset(start[:, J:J + 1], float(E)))
            dve.memset(x0[:, (NG - 1) % 2, :, :], 0.0).then_inc(x_clear, 1)
            o.link(dve.tensor_scalar(real[:, :], node_id[:, J - 1:J], float(N), None, ALU.is_lt))

            def split_x():
                for g in range(NG):
                    b = g % 2
                    n_in = g // 2 + 1 + (g == NG - 1)
                    dve.wait_ge(x_in[b], 16 * n_in)
                    if g >= 2:
                        dve.wait_ge(x_out[b], 16 * (g // 2))
                    if g == NG - 1:
                        o.link(dve.tensor_scalar(x0[:, b, JG - 1, :], x0[:, b, JG - 1, :], real[:, 0:1], None, ALU.mult))
                    split3(o, dve, x0[:, b, :, :], [xp[:, b, :, i * C:(i + 1) * C] for i in range(3)], x0[:, b, :, :])
                    dve.sem_inc(x_split, 1)

            for i in range(3):
                if i == 1:
                    split_x()
                for g in range(NG):
                    js = slice(g * JG, (g + 1) * JG)
                    if i:
                        dve.wait_ge(fetched[i - 1][g], 16 * JG)
                    n = (P, NBLK, BLK)[i]
                    keys = (first_row[:, 0:P].unsqueeze(1).broadcast_to([P, JG, P]), firsts[:, js, :], near[:, js, :])[i]
                    buf = (less if g % 2 else less2)[:, :, 0:n]
                    o.link(dve.tensor_tensor(buf, keys, node_id[:, js].unsqueeze(2).broadcast_to([P, JG, n]), ALU.is_lt))
                    o.link(dve.tensor_reduce(t[:, js], buf, AX, ALU.add))
                    if i < 2:
                        o.link(dve.tensor_scalar(t[:, js], t[:, js], -1.0, 0.0, ALU.add, ALU.max))
                    if i == 0:
                        dve.tensor_copy(idx[0][:, js], t[:, js]).then_inc(found[0], 1)
                        o.link(dve.tensor_scalar(at[:, js], t[:, js], float(T), None, ALU.mult))
                    elif i == 1:
                        o.link(dve.scalar_tensor_tensor(at[:, js], t[:, js], float(BLK), at[:, js], ALU.mult, ALU.add))
                        dve.tensor_copy(idx[1][:, js], at[:, js]).then_inc(found[1], 1)
                    else:
                        o.link(dve.tensor_tensor(start[:, js], t[:, js], at[:, js], ALU.add))
                        dve.tensor_copy(idx[2][:, js], start[:, js]).then_inc(found[2], 1)
            dve.sem_inc(starts, 1)
            for b in range(2):
                dve.wait_ge(x_out[b], 16 * len(range(b, NG, 2)))
            for d in range(1, NEAR + 1):
                into = same_sum if d == 1 else same
                o.link(dve.tensor_tensor(into[:, :], src_f[:, NEAR:NEAR + T], src_f[:, NEAR - d:NEAR - d + T], ALU.is_equal))
                if d > 1:
                    o.link(dve.tensor_tensor(same_sum[:, :], same_sum[:, :], same[:, :], ALU.add))
            o.link(dve.tensor_reduce(hits[:, :], same_sum[:, :].rearrange("p (b e) -> p b e", e=BLK), AX, ALU.add))
            o.link(dve.tensor_reduce(most[:, :], hits[:, :], AX, ALU.max))
            o.link(dve.tensor_scalar(most[:, :], most[:, :], float(MANY), None, ALU.is_ge))
            dve.wait_ge(ends, 1)
            o.link(dve.tensor_copy(end[:, :], end_ps[:, :]))
            o.link(dve.tensor_tensor(cnt[:, :], end[:, :], start[:, 0:J], ALU.subtract))
            o.link(dve.tensor_reduce(big[:, :], cnt[:, :], AX, ALU.max))
            o.link(dve.tensor_scalar(big[:, :], big[:, :], float(SLOTS), None, ALU.is_gt))
            dve.tensor_tensor(big[:, :], big[:, :], most[:, :], ALU.add).then_inc(asked, 1)
            for g in range(NG):
                js = slice(g * JG, (g + 1) * JG)
                dve.wait_ge(fetched[2][g], 16 * JG)
                o.link(dve.tensor_tensor(mask[:, :, :], slot_id[:, :].unsqueeze(1).broadcast_to([P, JG, SLOTS]),
                                         cnt[:, js].unsqueeze(2).broadcast_to([P, JG, SLOTS]), ALU.is_lt))
                o.link(dve.scalar_tensor_tensor(picked[:, js, :, 0], picked[:, js, :, 0], 1.0, mask[:, :, :], ALU.add, ALU.mult))
                dve.sem_inc(masked, 1)
            dve.wait_ge(told, 1)
            o.link(dve.tensor_copy(beyond[:, :], any_ps[:, 0:1]))
            o.link(dve.tensor_scalar(has[:, :], cnt[:, :], 0.0, None, ALU.is_gt))
            o.link(dve.tensor_scalar(t[:, :], cnt[:, :], 1.0, None, ALU.max))
            o.link(dve.reciprocal(t[:, :], t[:, :]))
            o.link(dve.tensor_tensor(rcnt[:, :], t[:, :], has[:, :], ALU.mult))
            o.link(dve.tensor_scalar(t[:, :], end[:, :], -1.0, 0.0, ALU.add, ALU.max))
            o.link(dve.tensor_copy(end_idx[:, :], t[:, :]))
            o.link(dve.tensor_scalar(u[:, :], node_id[:, :], float(EP), None, ALU.add))
            o.link(dve.tensor_tensor(t[:, :], start[:, 0:J], u[:, :], ALU.subtract))
            o.link(dve.tensor_tensor(t[:, :], t[:, :], has[:, :], ALU.mult))
            o.link(dve.tensor_tensor(t[:, :], t[:, :], u[:, :], ALU.add))
            o.link(dve.tensor_copy(start_idx[:, :], t[:, :]))


def build_matrix(nc, SLOT, A, B, b_zero, zeros):
    with semaphores(nc) as sem_, ExitStack() as ctx:
        sem = lambda name: sem_(f"bld_{name}")
        sb = lambda name, shape, dt=F32: ctx.enter_context(nc.sbuf_tensor(f"bld_{name}", shape, dt))
        slot = sb("slot", [P, 2, 2, P], BF16)
        hot = sb("hot", [P, 2, VALS, P], BF16)
        win = sb("win", [P, 2, 2, J, P], U8)
        count = [[ctx.enter_context(nc.psum_tensor(f"count{s}_{half}", [P, 2, 512], F32)) for half in range(2)]
                 for s in range(2)]
        hot_ready, counted, taken = (sem(n) for n in ("hot_ready", "counted", "taken"))
        issued, storing = sem("issued"), sem("storing")
        brought, stored = ([sem(f"{n}{b}") for b in range(2)] for n in ("brought", "stored"))
        block = ctx.enter_context(nc.Block())

        @block.sync
        def _(sp):
            def store(h):
                sp.wait_ge(taken, (h.c + 1) * 2 * STEPS)
                sp.sem_inc(storing, 1)
                for half in range(2):
                    sp.dma_start(A[bass.ds((2 * h.c + half) * P, P), :],
                                 win[:, h.b, half, :, :].rearrange("p j n -> p (j n)")).then_inc(stored[h.b], 16)

            def step(h):
                if not early(h, 2):
                    sp.wait_ge(hot_ready, h.c - 1)
                    sp.sem_inc(storing, 1)
                sp.dma_start(slot[:, h.b, :, :].rearrange("p i n -> p (i n)"),
                             SLOT[:, bass.ds(h.c * 2 * P, 2 * P)]).then_inc(brought[h.b], 16)
                if not early(h, 2):
                    store(h.before().before())
            chunks(sp, step, PAIRS, 2)
            for c in range(PAIRS - 2, PAIRS):
                store(Chunk(0, c, 2))
            for b in range(2):
                sp.wait_ge(stored[b], 32 * len(range(b, PAIRS, 2)))

        @block.vector
        def _(dve):
            def step(h):
                dve.wait_ge(brought[h.b], 16 * (h.turn + 1))
                if not early(h, 2):
                    dve.wait_ge(counted, (h.c - 1) * 2 * STEPS)
                for v in range(VALS):
                    low = v < P
                    ins = dve.tensor_scalar(hot[:, h.b, v, :], slot[:, h.b, 0 if low else 1, :],
                                            float(v + 1 if low else v - P), None, ALU.is_equal)
                ins.then_inc(hot_ready, 1)
            chunks(dve, step, PAIRS, 2)

        @block.tensor
        def _(pe):
            def step(h):
                pe.wait_ge(hot_ready, h.c + 1)
                for s in range(STEPS):
                    if s >= 2 or not early(h, 1):
                        pe.wait_ge(taken, h.c * 2 * STEPS + 2 * (s - 1))
                    for i in range(GN):
                        n = s * GN + i
                        for half in range(2):
                            r = slice(half * SLOTS, (half + 1) * SLOTS)
                            to = count[s % 2][half][:, i // 4, (i % 4) * J:(i % 4 + 1) * J]
                            mm = pe.matmul(to, hot[r, h.b, 0:P, n], hot[r, h.b, P:VALS, n], start=True, stop=True)
                            if i == GN - 1:
                                mm.then_inc(counted, 1)
            chunks(pe, step, PAIRS, 2)

        @block.scalar
        def _(act):
            Bv = B[0:EP, :].rearrange("(p t) c -> p (t c)", p=P)

            def step(h):
                if not early(h, 2):
                    act.wait_ge(stored[h.b], 32 * h.turn)
                for s in range(STEPS):
                    for half in range(2):
                        act.wait_ge(counted, h.c * 2 * STEPS + 2 * s + half + 1)
                        act.sem_inc(issued, 1)
                        to = win[:, h.b, half, :, s * GN:(s + 1) * GN].bitcast(FP8).rearrange("p j (b n) -> p b n j", b=2)
                        act.activation(to, count[s % 2][half][:, :, 0:4 * J].rearrange("p b (n j) -> p b n j", n=4),
                                       ACT.Copy, saturate=True).then_inc(taken, 1)
                act.dma_start(Bv[:, bass.ds((h.c + CLEARS - PAIRS) * Z, Z)], zeros[:, :]).then_inc(b_zero, 16)
            chunks(act, step, PAIRS, 2)
            act.wait_ge(b_zero, 16 * CLEARS)


def split3(o, dve, whole, parts, rest):
    o.link(dve.tensor_copy(parts[0], whole))
    o.link(dve.tensor_tensor(rest, whole, parts[0], ALU.subtract))
    o.link(dve.tensor_copy(parts[1], rest))
    o.link(dve.tensor_tensor(rest, rest, parts[1], ALU.subtract))
    o.link(dve.tensor_copy(parts[2], rest))


def dense_layers(nc, A, XP, x3, rcnt):
    with semaphores(nc) as sem_, ExitStack() as ctx:
        sem = lambda name: sem_(f"d_{name}")
        sb = lambda name, shape, dt=F32: ctx.enter_context(nc.sbuf_tensor(f"d_{name}", shape, dt))
        parts = [sb(f"parts{i}", [P, J, 3 * C], BF16) for i in range(2)]
        win = sb("win", [P, 2, J * P], U8)
        xw = sb("xw", [P, 2, C])
        rest = sb("rest", [P, C])
        xp = sb("xp", [P, 2, 3 * C], BF16)
        acc = [ctx.enter_context(nc.psum_tensor(f"d_acc{i}", [P, 512], F32)) for i in range(2)]
        x_in = [sem(f"x_in{g}") for g in range(NG)]
        brought = [sem(f"brought{b}") for b in range(2)]
        issued, summed, order, made = (sem(n) for n in ("issued", "summed", "order", "made"))
        block = ctx.enter_context(nc.Block())

        @block.sync
        def _(sp):
            for layer in range(3):
                def step(h):
                    if layer or not early(h, 2):
                        sp.wait_ge(summed, layer * J + h.c - 1)
                    sp.dma_start(win[:, h.b, :], A[bass.ds(h.c * P, P), :]).then_inc(brought[h.b], 16)
                chunks(sp, step, J, 2)

        @block.tensor
        def _(pe):
            for layer in range(3):
                now = parts[layer % 2]

                def step(h):
                    pe.wait_ge(brought[h.b], 16 * (layer * (J // 2) + h.turn + 1))
                    if not early(h, 2):
                        pe.wait_ge(made, layer * J + h.c - 1)
                    elif layer:
                        pe.wait_ge(made, layer * J)
                    pe.sem_inc(issued, 1)
                    for j in range(J):
                        if layer == 0 and early(h, 1) and j % JG == 0:
                            pe.wait_ge(x_in[j // JG], 16)
                        mm = pe.matmul(acc[h.b][:, 0:3 * C], win[:, h.b, j * P:(j + 1) * P].bitcast(FP8),
                                       now[:, j, :], start=(j == 0), stop=(j == J - 1))
                    mm.then_inc(summed, 1)
                chunks(pe, step, J, 2)

        @block.vector
        def _(dve):
            o = Chain(dve, order)
            for layer in range(3):
                new = parts[1 - layer % 2]

                def step(h):
                    o.at(layer * J * 7 + h.c * (1 if layer == 2 else 7))
                    dve.wait_ge(summed, layer * J + h.c + 1)
                    xh = xw[:, h.b, :]
                    o.link(dve.tensor_reduce(xh, acc[h.b][:, 0:3 * C].rearrange("p (t c) -> p c t", t=3), AX, ALU.add))
                    if layer == 2:
                        dve.tensor_scalar(x3[:, bass.ds(h.c, 1), :], xh.unsqueeze(1), rcnt[:, bass.ds(h.c, 1)], None, ALU.mult)\
                            .then_inc(made, 1)
                        return
                    o.link(dve.tensor_scalar(xh, xh, rcnt[:, bass.ds(h.c, 1)], None, ALU.mult))
                    split3(o, dve, xh, [xp[:, h.b, i * C:(i + 1) * C] for i in range(3)], rest[:, :])
                    dve.tensor_copy(new[:, bass.ds(h.c, 1), :], xp[:, h.b, :].unsqueeze(1)).then_inc(made, 1)
                    dve.wait_ge(made, layer * J + h.c + 1)
                chunks(dve, step, J, 2)

        @block.scalar
        def _(act):
            for g in range(NG):
                cols = slice(g * JG * 3 * C, (g + 1) * JG * 3 * C)
                act.dma_start(parts[0][:, g * JG:(g + 1) * JG, :].rearrange("p j c -> p (j c)"), XP[:, cols]).then_inc(x_in[g], 16)


def bring(nc, X, x3):
    with semaphores(nc) as sem, nc.Block() as block:
        loaded = sem("x3_loaded")

        @block.sync
        def _(sp):
            sp.dma_start(x3[:, :, :], X.rearrange("(j p) c -> p j c", p=P)).then_inc(loaded, 16)
            sp.wait_ge(loaded, 16)


def gcn_pass(nc, tag, table, src_sb, keep, S, run_end):
    with semaphores(nc) as sem_, ExitStack() as ctx:
        sem = lambda name: sem_(f"{tag}_{name}")
        sb = lambda name, shape, dt=F32: ctx.enter_context(nc.sbuf_tensor(f"{tag}_{name}", shape, dt))
        rows = sb("rows", [P, NB, K, C])
        idx = sb("idx", [P, NB, K], I32)
        kc = sb("kc", [P, 2, K])
        carry = sb("carry", [P, C])
        idx_ready, gathered, stored = ([sem(f"{n}{b}") for b in range(NB)] for n in ("idx_ready", "gathered", "stored"))
        issued = sem("issued")
        order = sem("order")
        summed = sem("summed")
        carry_zero = sem("carry_zero")
        Sv = S.rearrange("(p t) c -> p (t c)", p=P)

        with nc.Block() as block:
            @block.sync
            def _(sp):
                def store(c, b):
                    sp.wait_ge(summed, c + 1)
                    sp.dma_start(Sv[:, bass.ds(c * (K * C), K * C)],
                                 rows[:, b, :, :].rearrange("p k c -> p (k c)")).then_inc(stored[b], 16)

                def step(h):
                    if not (early(h, NB)):
                        sp.wait_ge(summed, h.c - (NB - 1))
                    sp.dma_start(idx[:, h.b, :], src_sb[:, bass.ds(h.c * K, K)]).then_inc(idx_ready[h.b], 16)
                    if not (early(h, 3)):
                        store(h.c - 3, (h.b + 1) % NB)
                chunks(sp, step)
                for c in range(CH - 3, CH):
                    store(c, c % NB)
                for b in range(NB):
                    sp.wait_ge(stored[b], 16 * len(range(b, CH, NB)))

            @block.gpsimd
            def _(pool):
                def step(h):
                    pool.wait_ge(idx_ready[h.b], 16 * (h.turn + 1))
                    if not (early(h, NB)):
                        pool.wait_ge(stored[h.b], 16 * h.turn)
                    pool.sem_inc(issued, 1)
                    for k in range(K):
                        pool.indirect_dma_start(rows[:, h.b, k, :], None, table,
                                                bass.IndirectOffsetOnAxis(ap=idx[:, h.b, k:k + 1], axis=0))\
                            .then_inc(gathered[h.b], 16)
                chunks(pool, step)

            @block.vector
            def _(dve):
                o = Chain(dve, order)
                dve.memset(carry[:, :], 0.0).then_inc(carry_zero, 1)

                def step(h):
                    o.at(h.c * (K + 1))
                    o.link(dve.tensor_copy(kc[:, h.b2, :], keep[:, bass.ds(h.c * K, K)]))
                    dve.wait_ge(gathered[h.b], 16 * K * (h.turn + 1))
                    if early(h, 1):
                        dve.wait_ge(carry_zero, 1)
                    else:
                        dve.wait_ge(summed, h.c)
                    for k in range(K):
                        prev = carry[:, :] if k == 0 else rows[:, h.b, k - 1, :]
                        o.link(dve.scalar_tensor_tensor(rows[:, h.b, k, :], prev, kc[:, h.b2, k:k + 1],
                                                        rows[:, h.b, k, :], ALU.mult, ALU.add))
                    dve.tensor_copy(carry[:, :], rows[:, h.b, K - 1, :]).then_inc(summed, 1)
                chunks(dve, step)
                dve.wait_ge(summed, CH)
                o.at(CH * (K + 1))
                o.link(dve.tensor_copy(run_end[:, 0:C], carry[:, :]))


def mend(nc, sem_, ctx, tag, S, width, run_end, carried, ident, goes_on, passes, ends_here, lead_idx, mended):
    sem = lambda name: sem_(f"{tag}_m_{name}")
    sb = lambda name, shape, dt=F32: ctx.enter_context(nc.sbuf_tensor(f"{tag}_m_{name}", shape, dt))
    parts = [(lo, min(lo + P, width)) for lo in range(0, width, P)]
    n = len(parts)
    turned_ps = [ctx.enter_context(nc.psum_tensor(f"{tag}_m_turned{i}", [P, P], F32)) for i in range(n)]
    back_ps = [ctx.enter_context(nc.psum_tensor(f"{tag}_m_back{i}", [P, P], F32)) for i in range(n)]
    arriving = sb("arriving", [P, n, P])
    coming = sb("coming", [P, n, P])
    turned, swept, turned_back, order, set_ = (sem(s) for s in ("turned", "swept", "turned_back", "order", "set"))

    def pe_part(pe):
        for i, (lo, hi) in enumerate(parts):
            pe.transpose(turned_ps[i][0:hi - lo, :], run_end[:, lo:hi], ident[:, :]).then_inc(turned, 1)
        for i, (lo, hi) in enumerate(parts):
            w = hi - lo
            pe.wait_ge(swept, i + 1)
            pe.transpose(back_ps[i][:, 0:w], coming[0:w, i, :], ident[0:w, 0:w]).then_inc(turned_back, 1)

    def dve_part(dve):
        o = Chain(dve, order)
        for i, (lo, hi) in enumerate(parts):
            w = hi - lo
            dve.wait_ge(turned, i + 1)
            o.link(dve.memset(arriving[0:w, i, 0:1], 0.0))
            o.link(dve.tensor_tensor(arriving[0:w, i, 1:P], turned_ps[i][0:w, 0:P - 1], goes_on[0:w, 1:P], ALU.mult))
            o.link(dve.tensor_tensor_scan(coming[0:w, i, :], passes[0:w, :], arriving[0:w, i, :], 0.0, ALU.mult, ALU.add))
            dve.tensor_tensor(coming[0:w, i, :], coming[0:w, i, :], ends_here[0:w, :], ALU.mult).then_inc(swept, 1)
        for i, (lo, hi) in enumerate(parts):
            dve.wait_ge(turned_back, i + 1)
            dve.tensor_copy(carried[:, lo:hi], back_ps[i][:, 0:hi - lo]).then_inc(set_, 1)

    def pool_part(pool):
        pool.wait_ge(set_, n)
        pool.indirect_dma_start(S, bass.IndirectOffsetOnAxis(ap=lead_idx[:, 0:1], axis=0), carried[:, 0:width], None,
                                compute_op=ALU.add).then_inc(mended, 16)
        pool.wait_ge(mended, 16)

    return pe_part, dve_part, pool_part


def node_sums(nc, tag, S, X, run_end, carried, ident, goes_on, passes, ends_here, lead_idx, end_idx, rcnt):
    with semaphores(nc) as sem_, ExitStack() as ctx:
        sem = lambda name: sem_(f"{tag}_{name}")
        sb = lambda name, shape, dt=F32: ctx.enter_context(nc.sbuf_tensor(f"{tag}_{name}", shape, dt))
        sums = sb("sums", [P, J, C])
        mended, scaled, stored = sem("mended"), sem("scaled"), sem("stored")
        fetched = [sem(f"fetched{g}") for g in range(NG)]
        block = ctx.enter_context(nc.Block())
        pe_part, dve_part, pool_part = mend(nc, sem_, ctx, tag, S, C, run_end, carried, ident, goes_on,
                                            passes, ends_here, lead_idx, mended)

        @block.tensor
        def _(pe):
            pe_part(pe)

        @block.vector
        def _(dve):
            dve_part(dve)
            for g in range(NG):
                js = slice(g * JG, (g + 1) * JG)
                dve.wait_ge(fetched[g], 16 * JG)
                dve.tensor_tensor(sums[:, js, :], sums[:, js, :],
                                  rcnt[:, js].unsqueeze(2).broadcast_to([P, JG, C]), ALU.mult).then_inc(scaled, 1)

        @block.gpsimd
        def _(pool):
            pool_part(pool)
            for j in range(J):
                pool.indirect_dma_start(sums[:, j, :], None, S,
                                        bass.IndirectOffsetOnAxis(ap=end_idx[:, j:j + 1], axis=0))\
                    .then_inc(fetched[j // JG], 16)

        @block.sync
        def _(sp):
            for g in range(NG):
                sp.wait_ge(scaled, g + 1)
                sp.dma_start(X.rearrange("(j p) c -> p j c", p=P)[:, g * JG:(g + 1) * JG, :],
                             sums[:, g * JG:(g + 1) * JG, :]).then_inc(stored, 16)
            sp.wait_ge(stored, 16 * NG)


def layer_norm(o, dve, h, sq, stat, mean, eps_col, root, n):
    G = h.shape[1]
    wide = lambda col: col.unsqueeze(2).broadcast_to([P, G, n])
    o.link(dve.tensor_reduce(mean, h, AX, ALU.add))
    o.link(dve.tensor_scalar(mean, mean, 1.0 / n, None, ALU.mult))
    o.link(dve.tensor_tensor(h, h, wide(mean), ALU.subtract))
    o.link(dve.tensor_tensor(sq, h, h, ALU.mult))
    o.link(dve.tensor_reduce(stat, sq, AX, ALU.add))
    root()
    o.link(dve.reciprocal(stat, stat))
    o.link(dve.tensor_tensor(h, h, wide(stat), ALU.mult))


def node_mlps(nc, x, x3, X1, T4, B, start_idx, eps_col, ident, fWh, fbh, fWo, fbo, flw, flb, aWh, alw, alb):
    PAD_J = -(-J // GP) * GP
    NGP = PAD_J // GP
    with semaphores(nc) as sem_, ExitStack() as ctx:
        sem = lambda name: sem_(f"mlp_{name}")
        sb = lambda name, shape, dt=F32: ctx.enter_context(nc.sbuf_tensor(f"mlp_{name}", shape, dt))
        ps = lambda name, shape: ctx.enter_context(nc.psum_tensor(f"mlp_{name}", shape, F32))
        x1 = sb("x1", [P, PAD_J, C])
        scratch = sb("scratch", [P, GP, C])
        mean, stat = sb("mean", [P, GP]), sb("stat", [P, GP])
        W = sb("W", [P, 3, P])
        WY = sb("WY", [P, P])
        WO = sb("WO", [P, 2, 2 * C])
        wo = sb("wo", [P, 2 * C])
        wmean = sb("wmean", [P, 1])
        bh = sb("bh", [P, 3])
        bo = sb("bo", [P, 2 * C])
        bo4 = sb("bo4", [1, 4, 2 * C])
        ones = sb("ones", [1, P])
        flw_b, flb_b = sb("flw", [P, 2 * C]), sb("flb", [P, 2 * C])
        alw_b, alb_b = sb("alw", [P, C]), sb("alb", [P, C])
        xT = sb("xT", [P, 4 * P])
        hT = [sb(f"h{i}", [P, 4 * P]) for i in range(3)]
        sq = sb("sq", [P, GP, 2 * C])
        ssq = sb("ssq", [P, GP])
        row = sb("row", [P, 2, GP, ROW])
        tp = ps("tp", [P, 4 * P])
        yp = ps("yp", [P, 4 * P])
        hp = [ps(f"hp{i}", [P, 4 * P]) for i in range(3)]
        op = ps("op", [P, 2 * 4 * P])
        names = "cleared loaded order order2 rooted squares normed x_first x_rest turned x_ready h_ready m_ready y_ready o_ready sq_ready std_ready y_done o_used row_done x_stored var2"
        sems = {k: sem(k) for k in names.split()}
        row_stored = [sem(f"row_stored{b}") for b in range(2)]
        scattered = [sem(f"scattered{b}") for b in range(2)]
        block = ctx.enter_context(nc.Block())
        real = [min(GP, J - g * GP) for g in range(NGP)]

        @block.sync
        def _(sp):
            L = sems["loaded"]
            sp.wait_ge(sems["cleared"], 5)
            sp.dma_start(x1[:, 0:GP, :], x[0:GP * P, :].rearrange("(j p) c -> p j c", p=P)).then_inc(sems["x_first"], 16)
            for half in range(2):
                r = slice(C * half, C * half + C)
                for i in range(3):
                    sp.dma_start(W[r, i, r], fWh[i, :, :]).then_inc(L, 16)
                    sp.dma_start(bh[r, i:i + 1], fbh[i, :].rearrange("(c o) -> c o", o=1)).then_inc(L, 16)
                sp.dma_start(WY[r, r], aWh[0, :, :]).then_inc(L, 16)
                sp.dma_start(wo[r, :], fWo).then_inc(L, 16)
            for t, a in ((bo, fbo), (flw_b, flw), (flb_b, flb), (alw_b, alw), (alb_b, alb)):
                sp.dma_start(t[:, :], a.partition_broadcast(P)).then_inc(L, 16)
            sp.dma_start(x1[:, GP:J - 1, :], x[GP * P:(J - 1) * P, :].rearrange("(j p) c -> p j c", p=P)).then_inc(sems["x_rest"], 16)
            sp.dma_start(x1[0:N_LAST, J - 1, :], x[(J - 1) * P:N, :]).then_inc(sems["x_rest"], 16)
            for g in range(NGP):
                sp.wait_ge(sems["row_done"], g + 1)
                sp.dma_start(T4.rearrange("(j p) c -> p j c", p=P)[:, g * GP:g * GP + real[g], :],
                             row[:, g % 2, 0:real[g], :]).then_inc(row_stored[g % 2], 16)
            sp.wait_ge(sems["normed"], NGP)
            sp.dma_start(X1.rearrange("(j p) c -> p j c", p=P), x1[:, 0:J, :]).then_inc(sems["x_stored"], 16)
            sp.wait_ge(sems["x_stored"], 16)
            for b in range(2):
                sp.wait_ge(row_stored[b], 16 * len(range(b, NGP, 2)))

        n_loaded = 16 * (2 * 8 + 5)

        @block.vector
        def _(dve):
            o = Chain(dve, sems["order"])
            cl = sems["cleared"]
            dve.memset(x1[:, J - 1, :], 0.0).then_inc(cl, 1)
            dve.memset(W[:, :, :], 0.0).then_inc(cl, 1)
            dve.memset(WY[:, :], 0.0).then_inc(cl, 1)
            dve.memset(x1[:, J:PAD_J, :], 0.0).then_inc(cl, 1)
            dve.memset(WO[:, :, :], 0.0).then_inc(cl, 1)
            o.link(dve.memset(ones[:, :], 1.0))
            dve.wait_ge(sems["loaded"], n_loaded)
            for t in (wo, bo):
                o.link(dve.tensor_reduce(wmean[:, :], t[:, :], AX, ALU.add))
                o.link(dve.tensor_scalar(wmean[:, :], wmean[:, :], 1.0 / (2 * C), None, ALU.mult))
                o.link(dve.tensor_scalar(t[:, :], t[:, :], wmean[:, 0:1], None, ALU.subtract))
            for half in range(2):
                r = slice(C * half, C * half + C)
                o.link(dve.tensor_copy(WO[r, half, :], wo[r, :]))
            o.link(dve.tensor_copy(bo4[0:1, :, :], bo[0:1, :].unsqueeze(1).broadcast_to([1, 4, 2 * C])))
            o.link(dve.tensor_scalar(WY[:, :], WY[:, :], 0.5, None, ALU.mult))

            def norm(g):
                n = real[g]
                xr = x1[:, g * GP:g * GP + n, :]
                if g == 0:
                    dve.wait_ge(sems["x_first"], 16)
                elif g == 1:
                    dve.wait_ge(sems["x_rest"], 32)
                o.link(dve.tensor_tensor(xr, xr, x3[:, g * GP:g * GP + n, :], ALU.add))

                def root():
                    dve.sem_inc(sems["squares"], 1)
                    dve.wait_ge(sems["rooted"], g + 1)
                layer_norm(o, dve, xr, scratch[:, 0:n, :], stat[:, 0:n], mean[:, 0:n], eps_col, root, C)
                dve.sem_inc(sems["normed"], 1)

            norm(0)
            o2 = Chain(dve, sems["order2"])
            for g in range(NGP):
                rw = row[:, g % 2, :, :]
                xg = x1[:, g * GP:(g + 1) * GP, :]
                n = real[g]
                if g >= 2:
                    dve.wait_ge(row_stored[g % 2], 16 * (g // 2))
                    dve.wait_ge(scattered[g % 2], 16 * sum(real[g % 2:g - 1:2]))
                for i, t in enumerate((alw_b, alb_b)):
                    dve.tensor_tensor(rw[:, :, i * C:(i + 1) * C], xg, t[:, :].unsqueeze(1).broadcast_to([P, GP, C]), ALU.mult)
                dve.wait_ge(sems["y_ready"], g + 1)
                dve.tensor_copy(rw[:, :, 2 * C:3 * C], yp[:, :].rearrange("p (j c) -> p j c", c=C)).then_inc(sems["y_done"], 1)
                if g + 1 < NGP:
                    norm(g + 1)
                dve.wait_ge(sems["sq_ready"], g + 1)
                o2.link(dve.tensor_reduce(ssq[:, :], sq[:, :, :], AX, ALU.add))
                dve.sem_inc(sems["var2"], 1)
                dve.wait_ge(sems["std_ready"], g + 1)
                o2.link(dve.reciprocal(ssq[:, :], ssq[:, :]))
                fx = rw[:, :, 3 * C:5 * C]
                o2.link(dve.tensor_tensor(fx, op[:, :].rearrange("p (j c) -> p j c", c=2 * C),
                                          ssq[:, :].unsqueeze(2).broadcast_to([P, GP, 2 * C]), ALU.mult))
                dve.sem_inc(sems["o_used"], 1)
                o2.link(dve.tensor_tensor(fx, fx, flw_b[:, :].unsqueeze(1).broadcast_to([P, GP, 2 * C]), ALU.mult))
                dve.tensor_tensor(fx, fx, flb_b[:, :].unsqueeze(1).broadcast_to([P, GP, 2 * C]), ALU.add)\
                    .then_inc(sems["row_done"], 1)

        @block.scalar
        def _(act):
            def root(g):
                act.wait_ge(sems["squares"], g + 1)
                act.activation(stat[:, 0:real[g]], stat[:, 0:real[g]], ACT.Sqrt, bias=eps_col[:, 0:1], scale=1.0 / C)\
                    .then_inc(sems["rooted"], 1)

            root(0)
            for g in range(NGP):
                act.wait_ge(sems["turned"], g + 1)
                if g:
                    act.wait_ge(sems["y_ready"], g)
                act.activation(xT[:, :], tp[:, :], ACT.Copy).then_inc(sems["x_ready"], 1)
                for i in range(3):
                    act.wait_ge(sems["m_ready"], 3 * g + i + 1)
                    act.activation(hT[i][:, :], hp[i][:, :], ACT.Relu, bias=bh[:, i:i + 1]).then_inc(sems["h_ready"], 1)
                if g + 1 < NGP:
                    root(g + 1)
                act.wait_ge(sems["o_ready"], g + 1)
                if g:
                    act.wait_ge(sems["var2"], g)
                act.activation(sq[:, :, :].rearrange("p j c -> p (j c)"), op[:, :], ACT.Square).then_inc(sems["sq_ready"], 1)
                act.wait_ge(sems["var2"], g + 1)
                act.activation(ssq[:, :], ssq[:, :], ACT.Sqrt, bias=eps_col[:, 0:1], scale=1.0 / (2 * C)).then_inc(sems["std_ready"], 1)

        @block.tensor
        def _(pe):
            for g in range(NGP):
                pe.wait_ge(sems["normed"], g + 1)
                if g:
                    pe.wait_ge(sems["x_ready"], g)
                for q in range(4):
                    j = g * GP + 2 * q
                    mm = pe.transpose(tp[:, q * P:(q + 1) * P], x1[:, j:j + 2, :].rearrange("p j c -> p (j c)"), ident[:, :])
                mm.then_inc(sems["turned"], 1)
                pe.wait_ge(sems["x_ready"], g + 1)
                pe.matmul(hp[0][:, :], W[:, 0, :], xT[:, :], start=True, stop=True).then_inc(sems["m_ready"], 1)
                if g:
                    pe.wait_ge(sems["y_done"], g)
                for q in range(4):
                    mm = pe.matmul(yp[:, q * P:(q + 1) * P], xT[:, q * P:(q + 1) * P], WY[:, :], start=True, stop=True)
                mm.then_inc(sems["y_ready"], 1)
                for i in (1, 2):
                    pe.wait_ge(sems["h_ready"], 3 * g + i)
                    pe.matmul(hp[i][:, :], W[:, i, :], hT[i - 1][:, :], start=True, stop=True).then_inc(sems["m_ready"], 1)
                pe.wait_ge(sems["h_ready"], 3 * g + 3)
                if g:
                    pe.wait_ge(sems["o_used"], g)
                for bank in range(2):
                    pe.matmul(op[:, bank * 512:(bank + 1) * 512], ones[0:1, :], bo4[0:1, :, :].rearrange("p j c -> p (j c)"),
                              start=True, stop=False)
                    for q in range(2):
                        at = bank * 512 + q * 256
                        mm = pe.matmul(op[:, at:at + 256], hT[2][:, (2 * bank + q) * P:(2 * bank + q + 1) * P],
                                       WO[:, :, :].rearrange("p h c -> p (h c)"), start=False, stop=(q == 1))
                mm.then_inc(sems["o_ready"], 1)

        @block.gpsimd
        def _(pool):
            for g in range(NGP):
                pool.wait_ge(sems["y_done"], g + 1)
                for jj in range(real[g]):
                    pool.indirect_dma_start(B, bass.IndirectOffsetOnAxis(ap=start_idx[:, g * GP + jj:g * GP + jj + 1], axis=0),
                                            row[:, g % 2, jj, 2 * C:3 * C], None).then_inc(scattered[g % 2], 16)
            for b in range(2):
                pool.wait_ge(scattered[b], 16 * sum(real[b::2]))


def flux_pass(nc, T4, B, NV, S4, src_sb, keep, first_dst, run_end, ident, eps_col, aWh, abh, aWo, abo):
    Q = K // 2
    H = K * C // 512
    with semaphores(nc) as sem_, ExitStack() as ctx:
        sem = lambda name: sem_(f"flux_{name}")
        sb = lambda name, shape, dt=F32: ctx.enter_context(nc.sbuf_tensor(f"flux_{name}", shape, dt))
        ps = lambda name, shape: ctx.enter_context(nc.psum_tensor(f"flux_{name}", shape, F32))
        rows = sb("rows", [P, NB, K, ROW])
        idx = sb("idx", [P, NB, K], I32)
        nv = sb("nv", [P, NB, K, 2])
        yr = sb("yr", [P, 2, K, C])
        yc = sb("yc", [P, 2, C, K])
        kb = sb("kb", [P, K], BF16)
        kw = sb("kw", [P, 2, W4, K], BF16)
        h0 = sb("h0", [P, 2, K, C])
        kc = sb("kc", [P, 4, K])
        row_first = sb("row_first", [P, ROW])
        y_carry = sb("y_carry", [P, C])
        carry = sb("carry", [P, W4])
        hT = [sb(f"h{i + 1}", [P, Q * P]) for i in range(3)]
        sq = sb("sq", [P, K, C])
        ssq = sb("ssq", [P, K])
        f0 = sb("f0", [P, 2, K, C])
        run = sb("run", [P, 2, W4, K])
        row_out = sb("row_out", [P, 2, K, W4])
        W = sb("W", [P, 2, P])
        WO = sb("WO", [P, P])
        wo = sb("wo", [P, C])
        wmean = sb("wmean", [P, 1])
        bo = sb("bo", [P, C])
        bo8 = sb("bo8", [1, 8, C])
        ones = sb("ones", [1, P])
        bh = sb("bh", [P, 3])
        tp, mp = ps("tp", [P, Q * P]), ps("mp", [P, Q * P])
        mp2, zp = ps("mp2", [P, Q * P]), ps("zp", [P, Q * P])
        names = ("cleared loaded setup fetched_first summed issued order_a order_b h0_ready turned h_ready "
                 "m_ready z_ready sq_ready ssq_ready std_ready fn_ready v_done z_used y_carried nrow_ready y_turned turned_out")
        sems = {k: sem(k) for k in names.split()}
        ring = lambda name, n: [sem(f"{name}{b}") for b in range(n)]
        idx_ready, nv_ready, gathered = ring("idx_ready", NB), ring("nv_ready", NB), ring("gathered", NB)
        yr_ready, stored = ring("yr_ready", 2), ring("stored", 2)
        Bv = B[0:EP, :].rearrange("(p t) c -> p (t c)", p=P)
        S4v = S4.rearrange("(p t) c -> p (t c)", p=P)
        NVv = NV.rearrange("(p t) c -> p (t c)", p=P)
    
        n_loaded = 16 * (2 * (2 + 3 + 1) + 1)
        block = ctx.enter_context(nc.Block())

        @block.sync
        def _(sp):
            L = sems["loaded"]
            sp.wait_ge(sems["cleared"], 2)
            for half in range(2):
                r = slice(C * half, C * half + C)
                for i in range(2):
                    sp.dma_start(W[r, i, r], aWh[i + 1, :, :]).then_inc(L, 16)
                for i in range(3):
                    sp.dma_start(bh[r, i:i + 1], abh[i, :].rearrange("(c o) -> c o", o=1)).then_inc(L, 16)
                sp.dma_start(wo[r, :], aWo).then_inc(L, 16)
            sp.dma_start(bo[:, :], abo.partition_broadcast(P)).then_inc(L, 16)

            def store(c, b):
                sp.wait_ge(sems["turned_out"], c + 1)
                sp.dma_start(S4v[:, bass.ds(c * (K * W4), K * W4)],
                             row_out[:, b, :, :].rearrange("p k c -> p (k c)")).then_inc(stored[b], 16)

            def step(h):
                if not early(h, NB):
                    sp.wait_ge(sems["summed"], h.c - (NB - 1))
                sp.dma_start(idx[:, h.b, :], src_sb[:, bass.ds(h.c * K, K)]).then_inc(idx_ready[h.b], 16)
                sp.dma_start(nv[:, h.b, :, :].rearrange("p k c -> p (k c)"),
                             NVv[:, bass.ds(h.c * (2 * K), 2 * K)]).then_inc(nv_ready[h.b], 16)
                if not early(h, 2):
                    sp.wait_ge(sems["y_turned"], h.c - 1)
                sp.dma_start(yr[:, h.b2, :, :].rearrange("p k c -> p (k c)"),
                             Bv[:, bass.ds(h.c * (K * C), K * C)]).then_inc(yr_ready[h.b2], 16)
                if not early(h, 3):
                    store(h.c - 3, (h.b2 + 1) % 2)
            chunks(sp, step)
            for c in range(CH - 3, CH):
                store(c, c % 2)
            for b in range(2):
                sp.wait_ge(stored[b], 16 * len(range(b, CH, 2)))

        @block.gpsimd
        def _(pool):
            pool.indirect_dma_start(row_first[:, :], None, T4, bass.IndirectOffsetOnAxis(ap=first_dst[:, 0:1], axis=0))\
                .then_inc(sems["fetched_first"], 16)

            def step(h):
                pool.wait_ge(idx_ready[h.b], 16 * (h.turn + 1))
                if not early(h, NB):
                    pool.wait_ge(sems["v_done"], h.c - (NB - 1))
                pool.sem_inc(sems["issued"], 1)
                for k in range(K):
                    pool.indirect_dma_start(rows[:, h.b, k, :], None, T4,
                                            bass.IndirectOffsetOnAxis(ap=idx[:, h.b, k:k + 1], axis=0))\
                        .then_inc(gathered[h.b], 16)
            chunks(pool, step)

        @block.tensor
        def _(pe):
            pe.wait_ge(sems["setup"], 1)

            def step(h):
                pe.wait_ge(sems["h0_ready"], h.c + 1)
                if not early(h, 1):
                    pe.wait_ge(sems["h_ready"], h.c * 6 - 4)
                for q in range(Q):
                    mm = pe.transpose(tp[:, q * P:(q + 1) * P], h0[:, h.b2, 2 * q:2 * q + 2, :].rearrange("p k c -> p (k c)"),
                                      ident[:, :])
                    if q % 4 == 3:
                        mm.then_inc(sems["turned"], 1)
                for i, m in ((0, mp), (1, mp2)):
                    for half in range(H):
                        pe.wait_ge(sems["h_ready"], h.c * 6 + i * H + half + 1)
                        cols = slice(512 * half, 512 * half + 512)
                        pe.matmul(m[:, cols], W[:, i, :], hT[i][:, cols], start=True, stop=True).then_inc(sems["m_ready"], 1)
                if not early(h, 1):
                    pe.wait_ge(sems["z_used"], h.c)
                for half in range(H):
                    pe.wait_ge(sems["h_ready"], h.c * 6 + 2 * H + half + 1)
                    pe.matmul(zp[:, 512 * half:512 * half + 512], ones[0:1, :], bo8[0:1, :, :].rearrange("p j c -> p (j c)"),
                              start=True, stop=False)
                    for q in range(4):
                        cols = slice((4 * half + q) * P, (4 * half + q + 1) * P)
                        mm = pe.matmul(zp[:, cols], hT[2][:, cols], WO[:, :], start=False, stop=(q == 3))
                    mm.then_inc(sems["z_ready"], 1)
            chunks(pe, step)

        fx_of = lambda h: rows[:, h.b, :, 3 * C:5 * C].rearrange("p k (c d) -> p k c d", d=2)

        @block.scalar
        def _(act):
            act.wait_ge(sems["setup"], 1)

            def turn_y(h):
                act.wait_ge(yr_ready[h.b2], 16 * (h.turn2 + 1))
                if not early(h, 2):
                    act.wait_ge(sems["h0_ready"], h.c - 1)
                    act.wait_ge(sems["y_carried"], h.c - 1)
                act.activation(yc[:, h.b2, :, :].rearrange("p c k -> p k c"), yr[:, h.b2, :, :], ACT.Copy)\
                    .then_inc(sems["y_turned"], 1)

            def turn_sums(h):
                act.wait_ge(sems["summed"], h.c + 1)
                if not early(h, 2):
                    act.wait_ge(stored[h.b2], 16 * h.turn2)
                act.activation(row_out[:, h.b2, :, :], run[:, h.b2, :, :].rearrange("p c k -> p k c"), ACT.Copy)\
                    .then_inc(sems["turned_out"], 1)

            def layers(h):
                for i, p in enumerate((tp, mp, mp2)):
                    for half in range(H):
                        cols = slice(512 * half, 512 * half + 512)
                        if i == 0:
                            act.wait_ge(sems["turned"], h.c * H + half + 1)
                            if not early(h, 1):
                                act.wait_ge(sems["m_ready"], (h.c - 1) * 2 * H + half + 1)
                        else:
                            act.wait_ge(sems["m_ready"], h.c * 2 * H + (i - 1) * H + half + 1)
                            if i == 2 and not early(h, 1):
                                act.wait_ge(sems["z_ready"], (h.c - 1) * H + half + 1)
                        act.activation(hT[i][:, cols], p[:, cols], ACT.Relu, bias=bh[:, i:i + 1]).then_inc(sems["h_ready"], 1)
                    if i == 0:
                        act.wait_ge(gathered[h.b], 16 * K * (h.turn + 1))
                        act.wait_ge(nv_ready[h.b], 16 * (h.turn + 1))
                        if not early(h, 2):
                            act.wait_ge(sems["v_done"], h.c - 1)
                    if i < 2:
                        for k in range(i * K // 2, (i + 1) * K // 2):
                            a = act.activation(f0[:, h.b2, k, :], fx_of(h)[:, k, :, 0], ACT.Copy, scale=nv[:, h.b, k, 0:1])
                a.then_inc(sems["fn_ready"], 1)
                if not early(h, 1):
                    turn_sums(h.before())
                act.wait_ge(sems["z_ready"], (h.c + 1) * H)
                if not early(h, 1):
                    act.wait_ge(sems["v_done"], h.c)
                act.activation(sq[:, :, :].rearrange("p k c -> p (k c)"), zp[:, :], ACT.Square).then_inc(sems["sq_ready"], 1)
                act.activation(run[:, h.b2, 2 * C:W4, :].rearrange("p c k -> p k c"), nv[:, h.b, :, :], ACT.Copy)\
                    .then_inc(sems["nrow_ready"], 1)
                act.wait_ge(sems["ssq_ready"], h.c + 1)
                act.activation(ssq[:, :], ssq[:, :], ACT.Sqrt, bias=eps_col[:, 0:1], scale=1.0 / C).then_inc(sems["std_ready"], 1)

            def step(h):
                turn_y(h)
                if not early(h, 1):
                    layers(h.before())
            chunks(act, step)
            layers(Chunk(0, CH - 1))
            turn_sums(Chunk(0, CH - 1))

        A_STEPS = 5
        B_STEPS = 7

        @block.vector
        def _(dve):
            o = Chain(dve, sems["order_a"])
            dve.memset(W[:, :, :], 0.0).then_inc(sems["cleared"], 1)
            dve.memset(WO[:, :], 0.0).then_inc(sems["cleared"], 1)
            o.link(dve.memset(ones[:, :], 1.0))
            o.link(dve.memset(carry[:, :], 0.0))
            o.link(dve.memset(kb[:, :], 0.0))
            dve.wait_ge(sems["loaded"], n_loaded)
            for t in (wo, bo):
                o.link(dve.tensor_reduce(wmean[:, :], t[:, :], AX, ALU.add))
                o.link(dve.tensor_scalar(wmean[:, :], wmean[:, :], 1.0 / C, None, ALU.mult))
                o.link(dve.tensor_scalar(t[:, :], t[:, :], wmean[:, 0:1], None, ALU.subtract))
            for half in range(2):
                r = slice(C * half, C * half + C)
                o.link(dve.tensor_copy(WO[r, r], wo[r, :]))
            o.link(dve.tensor_copy(bo8[0:1, :, :], bo[0:1, :].unsqueeze(1).broadcast_to([1, 8, C])))
            dve.sem_inc(sems["setup"], 1)
            base = o.n

            def spread(h):
                o.at(h.c * A_STEPS + base)
                y = yc[:, h.b2, :, :]
                o.link(dve.tensor_copy(kc[:, h.b, :], keep[:, bass.ds(h.c * K, K)]))
                o.link(dve.tensor_copy(kb[:, 1:K], kc[:, h.b, 1:K]))
                o.link(dve.tensor_copy(kw[:, h.b2, :, :], kb[:, :].unsqueeze(1).broadcast_to([P, W4, K])))
                dve.wait_ge(sems["y_turned"], h.c + 1)
                if early(h, 1):
                    dve.wait_ge(sems["fetched_first"], 16)
                    o.link(dve.tensor_copy(y[:, :, 0], row_first[:, 2 * C:3 * C]))
                else:
                    dve.wait_ge(sems["y_carried"], h.c)
                    o.link(dve.scalar_tensor_tensor(y[:, :, 0], y_carry[:, :], kc[:, h.b, 0:1], y[:, :, 0], ALU.mult, ALU.add))
                flat = y.rearrange("p c k -> p (c k)")
                o.link(dve.tensor_tensor_scan(flat, kw[:, h.b2, 0:C, :].rearrange("p c k -> p (c k)"), flat,
                                              0.0, ALU.mult, ALU.add))
                dve.tensor_copy(y_carry[:, :], y[:, :, K - 1]).then_inc(sems["y_carried"], 1)
                dve.wait_ge(gathered[h.b], 16 * K * (h.turn + 1))
                if not early(h, 2):
                    dve.wait_ge(sems["turned"], (h.c - 1) * H)
                dve.tensor_tensor(h0[:, h.b2, :, :], rows[:, h.b, :, 2 * C:3 * C], y.rearrange("p c k -> p k c"), ALU.add)\
                    .then_inc(sems["h0_ready"], 1)

            ob = Chain(dve, sems["order_b"])

            def combine(h):
                ob.at(h.c * B_STEPS)
                by_edge = run[:, h.b2, :, :].rearrange("p c k -> p k c")
                a, v, f = by_edge[:, :, C:2 * C], by_edge[:, :, 0:C], f0[:, h.b2, :, :]
                dve.wait_ge(gathered[h.b], 16 * K * (h.turn + 1))
                dve.wait_ge(nv_ready[h.b], 16 * (h.turn + 1))
                f1 = fx_of(h)[:, :, :, 1]
                ob.link(dve.tensor_tensor(f1, f1,
                                          nv[:, h.b, :, 1:2].broadcast_to([P, K, C]), ALU.mult))
                ob.link(dve.tensor_tensor(f1, f1, rows[:, h.b, :, C:2 * C], ALU.subtract))
                dve.wait_ge(sems["sq_ready"], h.c + 1)
                dve.tensor_reduce(ssq[:, :], sq[:, :, :], AX, ALU.add).then_inc(sems["ssq_ready"], 1)
                dve.wait_ge(sems["fn_ready"], h.c + 1)
                ob.link(dve.tensor_tensor(f, f, f1, ALU.add))
                dve.wait_ge(sems["std_ready"], h.c + 1)
                ob.link(dve.reciprocal(ssq[:, :], ssq[:, :]))
                if not early(h, 2):
                    dve.wait_ge(sems["turned_out"], h.c - 1)
                dve.tensor_tensor(a, zp[:, :].rearrange("p (k c) -> p k c", c=C),
                                  ssq[:, :].unsqueeze(2).broadcast_to([P, K, C]), ALU.mult).then_inc(sems["z_used"], 1)
                dve.wait_ge(sems["z_used"], h.c + 1)
                ob.link(dve.tensor_tensor(sq[:, :, :], a, rows[:, h.b, :, 0:C], ALU.mult))
                dve.tensor_tensor(v, f, sq[:, :, :], ALU.subtract).then_inc(sems["v_done"], 1)
                dve.wait_ge(sems["v_done"], h.c + 1)
                dve.wait_ge(sems["nrow_ready"], h.c + 1)
                if not early(h, 1):
                    dve.wait_ge(sems["summed"], h.c)
                first = run[:, h.b2, :, 0]
                ob.link(dve.scalar_tensor_tensor(first, carry[:, :], kc[:, h.b, 0:1], first, ALU.mult, ALU.add))
                flat = run[:, h.b2, :, :].rearrange("p c k -> p (c k)")
                ob.link(dve.tensor_tensor_scan(flat, kw[:, h.b2, :, :].rearrange("p c k -> p (c k)"), flat,
                                               0.0, ALU.mult, ALU.add))
                dve.tensor_copy(carry[:, :], run[:, h.b2, :, K - 1]).then_inc(sems["summed"], 1)

            def step(h):
                spread(h)
                if not early(h, 1):
                    combine(h.before())
            chunks(dve, step)
            combine(Chunk(0, CH - 1))
            dve.wait_ge(sems["summed"], CH)
            ob.at(CH * B_STEPS)
            ob.link(dve.tensor_copy(run_end[:, :], carry[:, :]))


def final(nc, S4, T4, X1, out, run_end, carried, ident, goes_on, passes, ends_here, lead_idx, end_idx,
          has, cnt, eps_col, alw, alb):
    with semaphores(nc) as sem_, ExitStack() as ctx:
        sem = lambda name: sem_(f"fin_{name}")
        sb = lambda name, shape, dt=F32: ctx.enter_context(nc.sbuf_tensor(f"fin_{name}", shape, dt))
        sums = sb("sums", [P, 2, JG, W4])
        own = sb("own", [P, 2, JG, 2 * C])
        x1 = sb("x1", [P, 2, JG, C])
        sq, am = sb("sq", [P, JG, C]), sb("am", [P, JG, C])
        stat, mean = sb("stat", [P, JG]), sb("mean", [P, JG])
        res = sb("res", [P, J, C])
        eps4_col = sb("eps4_col", [P, 1])
        alw_b, alb_b = sb("alw", [P, C]), sb("alb", [P, C])
        mended, order, loaded, squares, rooted, used, done, stored = (
            sem(n) for n in ("mended", "order", "loaded", "squares", "rooted", "used", "done", "stored"))
        fetched = [sem(f"fetched{b}") for b in range(2)]
        brought = [sem(f"brought{b}") for b in range(2)]
        block = ctx.enter_context(nc.Block())
        pe_part, dve_part, pool_part = mend(nc, sem_, ctx, "fin", S4, W4, run_end, carried, ident, goes_on,
                                            passes, ends_here, lead_idx, mended)

        @block.tensor
        def _(pe):
            pe_part(pe)

        @block.gpsimd
        def _(pool):
            pool_part(pool)
            for g in range(NG):
                if g >= 2:
                    pool.wait_ge(used, g - 1)
                for jj in range(JG):
                    pool.indirect_dma_start(sums[:, g % 2, jj, :], None, S4,
                                            bass.IndirectOffsetOnAxis(ap=end_idx[:, g * JG + jj:g * JG + jj + 1], axis=0))\
                        .then_inc(fetched[g % 2], 16)

        @block.sync
        def _(sp):
            sp.dma_start(alw_b[:, :], alw.partition_broadcast(P)).then_inc(loaded, 16)
            sp.dma_start(alb_b[:, :], alb.partition_broadcast(P)).then_inc(loaded, 16)
            for g in range(NG):
                if g >= 2:
                    sp.wait_ge(used, g - 1)
                js = slice(g * JG, (g + 1) * JG)
                sp.dma_start(own[:, g % 2, :, :], T4.rearrange("(j p) c -> p j c", p=P)[:, js, 3 * C:5 * C]).then_inc(brought[g % 2], 16)
                sp.dma_start(x1[:, g % 2, :, :], X1.rearrange("(j p) c -> p j c", p=P)[:, js, :]).then_inc(brought[g % 2], 16)
            sp.wait_ge(done, 1)
            sp.dma_start(out[0:(J - 1) * P, :].rearrange("(j p) c -> p j c", p=P), res[:, 0:J - 1, :]).then_inc(stored, 16)
            sp.dma_start(out[(J - 1) * P:N, :], res[0:N_LAST, J - 1, :]).then_inc(stored, 16)
            sp.wait_ge(stored, 32)

        @block.scalar
        def _(act):
            for g in range(NG):
                act.wait_ge(squares, g + 1)
                act.activation(stat[:, :], stat[:, :], ACT.Sqrt, bias=eps4_col[:, 0:1], scale=1.0 / C).then_inc(rooted, 1)

        @block.vector
        def _(dve):
            dve_part(dve)
            o = Chain(dve, order)
            o.link(dve.memset(eps4_col[:, :], 4 * EPS))
            dve.wait_ge(loaded, 32)
            for g in range(NG):
                b, js = g % 2, slice(g * JG, (g + 1) * JG)
                dve.wait_ge(fetched[b], 16 * JG * (g // 2 + 1))
                dve.wait_ge(brought[b], 32 * (g // 2 + 1))
                sm, ow, xg, h = sums[:, b, :, :], own[:, b, :, :], x1[:, b, :, :], res[:, js, :]
                wide = lambda col, n: col.unsqueeze(2).broadcast_to([P, JG, n])
                each = lambda rw: rw.unsqueeze(1).broadcast_to([P, JG, C])
                o.link(dve.tensor_tensor(sm, sm, wide(has[:, js], W4), ALU.mult))
                ow4 = ow.rearrange("p j (c d) -> p j c d", d=2)
                o.link(dve.tensor_tensor(ow4, ow4, sm[:, :, 2 * C:W4].unsqueeze(2).broadcast_to([P, JG, C, 2]), ALU.mult))
                o.link(dve.tensor_tensor(h, ow4[:, :, :, 0], ow4[:, :, :, 1], ALU.add))
                o.link(dve.tensor_tensor(h, h, sm[:, :, 0:C], ALU.add))
                o.link(dve.tensor_tensor(am[:, :, :], sm[:, :, C:2 * C], each(alw_b[:, :]), ALU.mult))
                o.link(dve.tensor_tensor(sq[:, :, :], wide(cnt[:, js], C), each(alb_b[:, :]), ALU.mult))
                o.link(dve.tensor_tensor(am[:, :, :], am[:, :, :], sq[:, :, :], ALU.add))
                o.link(dve.scalar_tensor_tensor(am[:, :, :], am[:, :, :], 4.0, xg, ALU.add, ALU.mult))
                o.link(dve.tensor_tensor(h, h, am[:, :, :], ALU.add))
                dve.sem_inc(used, 1)

                def root():
                    dve.sem_inc(squares, 1)
                    dve.wait_ge(rooted, g + 1)
                layer_norm(o, dve, h, sq[:, :, :], stat[:, :], mean[:, :], eps_col, root, C)
            dve.sem_inc(done, 1)


_INS = ["x", "src", "dst", "edge_attr_2"] + [f"L1_gnn_{n}" for n in (
    "flux_Wh", "flux_bh", "flux_Wo", "flux_bo", "flux_ln_w", "flux_ln_b",
    "a_Wh", "a_bh", "a_Wo", "a_bo", "a_ln_w", "a_ln_b")]


def kernel(**inputs):
    import numpy as _np
    import concourse.bacc as _bacc
    from concourse import mybir as _mybir
    from concourse.bass_utils import run_bass_kernel_spmd as _run

    nc = _bacc.Bacc("TRN2", target_bir_lowering=False, num_devices=1)
    arrays, args = {}, []
    for name in _INS:
        a = _np.ascontiguousarray(inputs[name])
        arrays[f"in_{name}"] = a
        args.append(nc.dram_tensor(f"in_{name}", a.shape, _mybir.dt.from_np(a.dtype), kind="ExternalInput").ap())
    args.append(nc.dram_tensor("out_0", (N, C), F32, kind="ExternalOutput").ap())
    build_program(nc, *args)
    r = _run(nc, [arrays], core_ids=[0])
    return r.results[0]["out_0"]
```
